# Optimizing a Trainium2 kernel written in Bass

```python
import numpy as np
import jax
import jax.numpy as jnp

def _softmax(x, axis=-1):
    return jax.nn.softmax(x, axis=axis)

def _gelu(x):
    return jax.nn.gelu(x, approximate=True)

def _silu(x):
    return jax.nn.silu(x)

def _sigmoid(x):
    return jax.nn.sigmoid(x)

def _layernorm(x, axis=-1, eps=1e-05):
    m = jnp.mean(x, axis=axis, keepdims=True)
    v = jnp.var(x, axis=axis, keepdims=True)
    return (x - m) / jnp.sqrt(v + eps)

def _scatter_add(tgt, idx, src, axis=0):
    return tgt.at[idx].add(src)

def _segment_sum(src, seg, n):
    return jax.ops.segment_sum(src, seg, n)
kernel_name = 'mk_conv_seq_d4_conv_nhwc512_r4_eb197e'

def setup_inputs(seed: int=0):
    np.random.seed(seed)
    _w = jnp.asarray

    def _rec_inputs():
        import jax
        import jax.numpy as jnp
        _gk = jax.random.key(seed)
        x = -0.0003929 + 0.9999 * jax.random.normal(jax.random.fold_in(_gk, 1), (8, 16, 16, 128), jnp.float32)
        return x
    x = _rec_inputs()

    def _L0_conv_setup():
        import jax, jax.numpy as jnp
        import numpy as np
        B, H, W, C = (8, 16, 16, 128)

        def maxpool2x2(x):
            b, h, w, c = x.shape
            return x.reshape(b, h // 2, 2, w // 2, 2, c).max(axis=(2, 4))
        key = jax.random.key(seed)
        ks = jax.random.split(key, 9)
        c8, c2 = (C // 8, C // 2)
        s_in = 1.0 / np.sqrt(C)
        s_g = 1.0 / np.sqrt(c2)
        return {'x': jax.random.normal(ks[0], (B, H, W, C), jnp.float32), 'w_theta': jax.random.normal(ks[1], (C, c8), jnp.float32) * s_in, 'b_theta': jnp.zeros((c8,), jnp.float32), 'w_phi': jax.random.normal(ks[2], (C, c8), jnp.float32) * s_in, 'b_phi': jnp.zeros((c8,), jnp.float32), 'w_g': jax.random.normal(ks[3], (C, c2), jnp.float32) * s_in, 'b_g': jnp.zeros((c2,), jnp.float32), 'w_o': jax.random.normal(ks[4], (c2, C), jnp.float32) * s_g, 'b_o': jnp.zeros((C,), jnp.float32), 'sigma': jnp.array(0.7, jnp.float32)}
    _L0_conv_all = _L0_conv_setup()
    _L0_conv_in = {k: v for k, v in _L0_conv_all.items() if k in ('w_theta', 'b_theta', 'w_phi', 'b_phi', 'w_g', 'b_g', 'w_o', 'b_o', 'sigma')}
    del _L0_conv_all

    def _L1_conv_setup():
        import jax, jax.numpy as jnp
        import numpy as np
        GROUPS = 32
        EPS = 1e-06
        key = jax.random.key(seed)
        ks = jax.random.split(key, 6)
        B, H, W, C = (4, 16, 16, 128)
        s = 1.0 / np.sqrt(C)
        return {'inputs': jax.random.normal(ks[0], (B, H, W, C), dtype=jnp.float32), 'gn_gamma': jnp.ones((C,), dtype=jnp.float32), 'gn_beta': jnp.zeros((C,), dtype=jnp.float32), 'wq': jax.random.normal(ks[1], (C, C), dtype=jnp.float32) * s, 'bq': jnp.zeros((C,), dtype=jnp.float32), 'wk': jax.random.normal(ks[2], (C, C), dtype=jnp.float32) * s, 'bk': jnp.zeros((C,), dtype=jnp.float32), 'wv': jax.random.normal(ks[3], (C, C), dtype=jnp.float32) * s, 'bv': jnp.zeros((C,), dtype=jnp.float32), 'wo': jax.random.normal(ks[4], (C, C), dtype=jnp.float32) * s, 'bo': jnp.zeros((C,), dtype=jnp.float32)}
    _L1_conv_all = _L1_conv_setup()
    _L1_conv_in = {k: v for k, v in _L1_conv_all.items() if k in ('gn_gamma', 'gn_beta', 'wq', 'bq', 'wk', 'bk', 'wv', 'bv', 'wo', 'bo')}
    del _L1_conv_all

    def _L2_conv_setup():
        import jax, jax.numpy as jnp
        import numpy as np
        NUM_HEADS = 8
        NUM_GROUPS = 16
        EPS = 1e-05

        def _group_norm(x, scale, bias):
            B, H, W, C = x.shape
            g = NUM_GROUPS
            xg = x.reshape(B, H, W, g, C // g)
            mean = jnp.mean(xg, axis=(1, 2, 4), keepdims=True)
            var = jnp.var(xg, axis=(1, 2, 4), keepdims=True)
            xn = (xg - mean) * jax.lax.rsqrt(var + EPS)
            xn = xn.reshape(B, H, W, C)
            return xn * scale + bias
        key = jax.random.key(seed)
        k1, k2, k3 = jax.random.split(key, 3)
        B, H, W, C = (8, 32, 32, 128)
        x = jax.random.normal(k1, (B, H, W, C), dtype=jnp.float32)
        gn_scale = jnp.ones((C,), dtype=jnp.float32)
        gn_bias = jnp.zeros((C,), dtype=jnp.float32)
        w_qkv = jax.random.normal(k2, (C, 3 * C), dtype=jnp.float32) * C ** (-0.5)
        w_out = jax.random.normal(k3, (C, C), dtype=jnp.float32) * C ** (-0.5)
        b_out = jnp.zeros((C,), dtype=jnp.float32)
        return {'x': x, 'gn_scale': gn_scale, 'gn_bias': gn_bias, 'w_qkv': w_qkv, 'w_out': w_out, 'b_out': b_out}
    _L2_conv_all = _L2_conv_setup()
    _L2_conv_in = {k: v for k, v in _L2_conv_all.items() if k in ('gn_scale', 'gn_bias', 'w_qkv', 'w_out', 'b_out')}
    del _L2_conv_all

    def _L3_conv_setup():
        import jax, jax.numpy as jnp
        import numpy as np
        SPARSITY = 0.01

        def _cas(n):
            t = jnp.arange(n, dtype=jnp.float32)
            a = 2.0 * jnp.pi * jnp.outer(t, t) / n
            return jnp.cos(a) + jnp.sin(a)

        def _dht2d(x):
            B, H, W, C = x.shape
            y = jnp.einsum('bhwc,cd->bhwd', x, _cas(C))
            return jnp.einsum('vw,bhwd->bhvd', _cas(W), y)
        key = jax.random.key(seed)
        k0, k1, k2, k3, k4 = jax.random.split(key, 5)
        B, H, W, C = (1, 45, 90, 128)
        nb, bs, f = (8, 16, 1)
        scale = 0.02
        x = jax.random.normal(k0, (B, H, W, C), jnp.float32)
        w1 = scale * jax.random.normal(k1, (2, nb, bs, bs * f), jnp.float32)
        b1 = scale * jax.random.normal(k2, (2, nb, bs * f), jnp.float32)
        w2 = scale * jax.random.normal(k3, (2, nb, bs * f, bs), jnp.float32)
        b2 = scale * jax.random.normal(k4, (2, nb, bs), jnp.float32)
        return {'x': x, 'w1': w1, 'b1': b1, 'w2': w2, 'b2': b2}
    _L3_conv_all = _L3_conv_setup()
    _L3_conv_in = {k: v for k, v in _L3_conv_all.items() if k in ('w1', 'b1', 'w2', 'b2')}
    del _L3_conv_all
    return {'x': x, 'L0_conv_w_theta': _L0_conv_in['w_theta'], 'L0_conv_b_theta': _L0_conv_in['b_theta'], 'L0_conv_w_phi': _L0_conv_in['w_phi'], 'L0_conv_b_phi': _L0_conv_in['b_phi'], 'L0_conv_w_g': _L0_conv_in['w_g'], 'L0_conv_b_g': _L0_conv_in['b_g'], 'L0_conv_w_o': _L0_conv_in['w_o'], 'L0_conv_b_o': _L0_conv_in['b_o'], 'L0_conv_sigma': _L0_conv_in['sigma'], 'L1_conv_gn_gamma': _L1_conv_in['gn_gamma'], 'L1_conv_gn_beta': _L1_conv_in['gn_beta'], 'L1_conv_wq': _L1_conv_in['wq'], 'L1_conv_bq': _L1_conv_in['bq'], 'L1_conv_wk': _L1_conv_in['wk'], 'L1_conv_bk': _L1_conv_in['bk'], 'L1_conv_wv': _L1_conv_in['wv'], 'L1_conv_bv': _L1_conv_in['bv'], 'L1_conv_wo': _L1_conv_in['wo'], 'L1_conv_bo': _L1_conv_in['bo'], 'L2_conv_gn_scale': _L2_conv_in['gn_scale'], 'L2_conv_gn_bias': _L2_conv_in['gn_bias'], 'L2_conv_w_qkv': _L2_conv_in['w_qkv'], 'L2_conv_w_out': _L2_conv_in['w_out'], 'L2_conv_b_out': _L2_conv_in['b_out'], 'L3_conv_w1': _L3_conv_in['w1'], 'L3_conv_b1': _L3_conv_in['b1'], 'L3_conv_w2': _L3_conv_in['w2'], 'L3_conv_b2': _L3_conv_in['b2']}

def reference(x, L0_conv_w_theta, L0_conv_b_theta, L0_conv_w_phi, L0_conv_b_phi, L0_conv_w_g, L0_conv_b_g, L0_conv_w_o, L0_conv_b_o, L0_conv_sigma, L1_conv_gn_gamma, L1_conv_gn_beta, L1_conv_wq, L1_conv_bq, L1_conv_wk, L1_conv_bk, L1_conv_wv, L1_conv_bv, L1_conv_wo, L1_conv_bo, L2_conv_gn_scale, L2_conv_gn_bias, L2_conv_w_qkv, L2_conv_w_out, L2_conv_b_out, L3_conv_w1, L3_conv_b1, L3_conv_w2, L3_conv_b2):
    import jax
    import jax.numpy as jnp

    def _L0_conv_ref(x, w_theta, b_theta, w_phi, b_phi, w_g, b_g, w_o, b_o, sigma):
        import jax, jax.numpy as jnp
        import numpy as np
        B, H, W, C = (8, 16, 16, 128)

        def maxpool2x2(x):
            b, h, w, c = x.shape
            return x.reshape(b, h // 2, 2, w // 2, 2, c).max(axis=(2, 4))
        b, h, w, c = x.shape
        loc = h * w
        down = loc // 4
        c8, c2 = (c // 8, c // 2)
        theta = (jnp.einsum('bhwc,cd->bhwd', x, w_theta) + b_theta).reshape(b, loc, c8)
        phi = maxpool2x2(jnp.einsum('bhwc,cd->bhwd', x, w_phi) + b_phi).reshape(b, down, c8)
        g = maxpool2x2(jnp.einsum('bhwc,cd->bhwd', x, w_g) + b_g).reshape(b, down, c2)
        attn = jax.nn.softmax(jnp.einsum('bnd,bmd->bnm', theta, phi), axis=-1)
        attn_g = jnp.einsum('bnm,bmd->bnd', attn, g).reshape(b, h, w, c2)
        out = jnp.einsum('bhwd,dc->bhwc', attn_g, w_o) + b_o
        return x + out * sigma

    def _L1_conv_ref(inputs, gn_gamma, gn_beta, wq, bq, wk, bk, wv, bv, wo, bo):
        import jax, jax.numpy as jnp
        import numpy as np
        GROUPS = 32
        EPS = 1e-06
        B, H, W, C = inputs.shape
        xg = inputs.astype(jnp.float32).reshape(B, H, W, GROUPS, C // GROUPS)
        mean = jnp.mean(xg, axis=(1, 2, 4), keepdims=True)
        var = jnp.var(xg, axis=(1, 2, 4), keepdims=True)
        xg = (xg - mean) * jax.lax.rsqrt(var + EPS)
        x = xg.reshape(B, H, W, C) * gn_gamma + gn_beta
        q = jnp.einsum('bhwc,cd->bhwd', x, wq) + bq
        k = jnp.einsum('bhwc,cd->bhwd', x, wk) + bk
        v = jnp.einsum('bhwc,cd->bhwd', x, wv) + bv
        N = H * W
        q = q.reshape(B, N, C) * (1.0 / jnp.sqrt(jnp.float32(C)))
        k = k.reshape(B, N, C)
        v = v.reshape(B, N, C)
        scores = jnp.einsum('bnc,bmc->bnm', q, k)
        attn = jax.nn.softmax(scores.astype(jnp.float32), axis=-1).astype(q.dtype)
        out = jnp.einsum('bmc,bnm->bnc', v, attn)
        out = out.reshape(B, H, W, C)
        out = jnp.einsum('bhwc,cd->bhwd', out, wo) + bo
        return out + inputs

    def _L2_conv_ref(x, gn_scale, gn_bias, w_qkv, w_out, b_out):
        import jax, jax.numpy as jnp
        import numpy as np
        NUM_HEADS = 8
        NUM_GROUPS = 16
        EPS = 1e-05

        def _group_norm(x, scale, bias):
            B, H, W, C = x.shape
            g = NUM_GROUPS
            xg = x.reshape(B, H, W, g, C // g)
            mean = jnp.mean(xg, axis=(1, 2, 4), keepdims=True)
            var = jnp.var(xg, axis=(1, 2, 4), keepdims=True)
            xn = (xg - mean) * jax.lax.rsqrt(var + EPS)
            xn = xn.reshape(B, H, W, C)
            return xn * scale + bias
        B, H, W, C = x.shape
        n = NUM_HEADS
        hd = C // n
        skip = x
        xn = _group_norm(x, gn_scale, gn_bias)
        qkv = jnp.einsum('bhwc,cd->bhwd', xn, w_qkv)
        qkv = qkv.reshape(B, H * W, n, 3 * hd)
        qkv = qkv.transpose(0, 2, 3, 1).reshape(B * n, 3 * hd, H * W)
        q, k, v = jnp.split(qkv, 3, axis=1)
        scores = jnp.einsum('bcq,bck->bqk', q, k) * hd ** (-0.5)
        scores = jax.nn.softmax(scores, axis=-1)
        o = jnp.einsum('bqk,bck->bqc', scores, v)
        o = o.reshape(B, n, H * W, hd).transpose(0, 2, 1, 3).reshape(B, H, W, C)
        out = jnp.einsum('bhwc,cd->bhwd', o, w_out) + b_out
        return out + skip

    def _L3_conv_ref(x, w1, b1, w2, b2):
        import jax, jax.numpy as jnp
        import numpy as np
        SPARSITY = 0.01

        def _cas(n):
            t = jnp.arange(n, dtype=jnp.float32)
            a = 2.0 * jnp.pi * jnp.outer(t, t) / n
            return jnp.cos(a) + jnp.sin(a)

        def _dht2d(x):
            B, H, W, C = x.shape
            y = jnp.einsum('bhwc,cd->bhwd', x, _cas(C))
            return jnp.einsum('vw,bhwd->bhvd', _cas(W), y)
        bias = x
        B, H, W, C = x.shape
        nb, bs = (w1.shape[1], w1.shape[2])
        xh = _dht2d(x).reshape(B, H, W, nb, bs)
        xn = jnp.roll(jnp.flip(xh, axis=(1, 2)), shift=(1, 1), axis=(1, 2))
        w1a, w1b = (w1[0] + w1[1], w1[0] - w1[1])
        o1k = jax.nn.relu(0.5 * (jnp.einsum('bhwki,kio->bhwko', xh, w1a) + jnp.einsum('bhwki,kio->bhwko', xn, w1b)) + b1[0])
        o1n = jax.nn.relu(0.5 * (jnp.einsum('bhwki,kio->bhwko', xn, w1a) + jnp.einsum('bhwki,kio->bhwko', xh, w1b)) + b1[1])
        w2a, w2b = (w2[0] + w2[1], w2[0] - w2[1])
        o2k = 0.5 * (jnp.einsum('bhwki,kio->bhwko', o1k, w2a) + jnp.einsum('bhwki,kio->bhwko', o1n, w2b)) + b2[0]
        o2n = 0.5 * (jnp.einsum('bhwki,kio->bhwko', o1n, w2a) + jnp.einsum('bhwki,kio->bhwko', o2k, w2b)) + b2[1]
        y = (o2k + o2n).reshape(B, H, W, C)
        y = jnp.sign(y) * jax.nn.relu(jnp.abs(y) - SPARSITY)
        y = _dht2d(y) / (W * C)
        return y + bias

    def _gn(v, G=32, eps=1e-05):
        B_, H_, W_, C_ = v.shape
        g = v.reshape(B_, H_, W_, G, C_ // G)
        m = jnp.mean(g, axis=(1, 2, 4), keepdims=True)
        s = jnp.var(g, axis=(1, 2, 4), keepdims=True)
        return ((g - m) / jnp.sqrt(s + eps)).reshape(v.shape)

    def _ln_c(v, eps=1e-06):
        m = jnp.mean(v, axis=-1, keepdims=True)
        s = jnp.var(v, axis=-1, keepdims=True)
        return (v - m) / jnp.sqrt(s + eps)

    def _ln_t(v, eps=1e-05):
        m = jnp.mean(v, axis=-1, keepdims=True)
        s = jnp.var(v, axis=-1, keepdims=True)
        return (v - m) / jnp.sqrt(s + eps)

    def _to_tokens(v):
        B_, H_, W_, C_ = v.shape
        return v.reshape(B_, H_ * W_, C_)

    def _from_tokens(t, like):
        return t.reshape(like.shape)
    x = _L0_conv_ref(x, L0_conv_w_theta, L0_conv_b_theta, L0_conv_w_phi, L0_conv_b_phi, L0_conv_w_g, L0_conv_b_g, L0_conv_w_o, L0_conv_b_o, L0_conv_sigma)
    x = _L1_conv_ref(x, L1_conv_gn_gamma, L1_conv_gn_beta, L1_conv_wq, L1_conv_bq, L1_conv_wk, L1_conv_bk, L1_conv_wv, L1_conv_bv, L1_conv_wo, L1_conv_bo)
    x = _L2_conv_ref(x, L2_conv_gn_scale, L2_conv_gn_bias, L2_conv_w_qkv, L2_conv_w_out, L2_conv_b_out)
    x = _L3_conv_ref(x, L3_conv_w1, L3_conv_b1, L3_conv_w2, L3_conv_b2)
    return x

_drawn_inputs = setup_inputs


def setup_inputs(seed=0):
    import zlib

    import numpy as np

    out = dict(_drawn_inputs(seed))
    spreads = {'L0_conv_b_theta': (0.0, 0.1),
     'L0_conv_b_phi': (0.0, 2.0),
     'L0_conv_b_g': (0.0, 0.1),
     'L0_conv_b_o': (0.0, 0.1),
     'L1_conv_gn_gamma': (1.0, 0.2),
     'L1_conv_gn_beta': (0.0, 0.1),
     'L1_conv_bq': (0.0, 0.8),
     'L1_conv_bk': (0.0, 2.0),
     'L1_conv_bv': (0.0, 0.1),
     'L1_conv_bo': (0.0, 0.1),
     'L2_conv_gn_scale': (1.0, 0.2),
     'L2_conv_gn_bias': (0.0, 0.1),
     'L2_conv_b_out': (0.0, 0.1)}
    factors = {'L3_conv_w1': 8.0, 'L3_conv_b1': 200.0, 'L3_conv_w2': 8.0, 'L3_conv_b2': 64.0}
    for name, (base, spread) in spreads.items():
        noise = np.random.default_rng([zlib.crc32(name.encode()), seed]).standard_normal(out[name].shape)
        drawn = base * np.exp(spread * noise) if base else spread * noise
        out[name] = jnp.asarray(drawn.astype(out[name].dtype))
    for name, factor in factors.items():
        out[name] = (out[name] * factor).astype(out[name].dtype)
    return out
```

```python
from contextlib import ExitStack

import numpy as np

import concourse.bass as bass
from concourse import mybir

F32 = mybir.dt.float32
BF16 = mybir.dt.bfloat16
ALU = mybir.AluOpType
ACT = mybir.ActivationFunctionType
AX = mybir.AxisListType

IMAGES, H, W, C = 8, 16, 16, 128
P = 128
TOK = H * W
TILES = TOK // P
POOLED = TOK // 4
C8, C2 = C // 8, C // 2
HEADS, HD = 8, 16
HE, WE = H + 1, W + 1
EXT = HE * WE
PARTS = 3
PAIRS = ((0, 0), (1, 1), (0, 1), (1, 0), (0, 2), (2, 0))
ROWS = len(PAIRS) * HD
AUG = ROWS + PARTS
SPARSITY = 0.01
EPS1, EPS2 = 1e-6, 1e-5
GROUP1, GROUP2 = C // 32, C // 16

CAS_C, CAS_W, CAS_WE, IDENT, MEAN1, MEAN2, BLOCKS = 0, 128, 256, 392, 520, 648, 776
CONST_W = 904

VECTORS = ("b_phi_g", "b_theta", "L0_conv_b_o", "L1_conv_gn_gamma", "L1_conv_gn_beta",
           "L1_conv_bq", "L1_conv_bk", "L1_conv_bv", "L1_conv_bo",
           "L2_conv_gn_scale", "L2_conv_gn_bias", "b1_0", "b1_1", "b2_0", "b2_1")
NV = len(VECTORS)
VEC = {name: n for n, name in enumerate(VECTORS)}


def constants():
    def cas(n):
        a = 2.0 * np.pi * (np.outer(np.arange(n), np.arange(n)) % n) / n
        return np.cos(a) + np.sin(a)

    table = np.zeros((P, CONST_W), np.float32)
    rows = P // W
    table[:, CAS_C:CAS_C + C] = cas(C)
    table[:, CAS_W:CAS_W + P] = np.kron(np.eye(rows), cas(W))
    wrapped = np.concatenate([cas(W), cas(W)[:, :1]], axis=1)
    table[:, CAS_WE:CAS_WE + rows * WE] = np.kron(np.eye(rows), wrapped)
    table[:, IDENT:IDENT + P] = np.eye(P)
    table[:, MEAN1:MEAN1 + P] = np.kron(np.eye(C // GROUP1), np.full((GROUP1, GROUP1), 1.0 / GROUP1))
    table[:, MEAN2:MEAN2 + P] = np.kron(np.eye(C // GROUP2), np.full((GROUP2, GROUP2), 1.0 / GROUP2))
    table[:, BLOCKS:BLOCKS + P] = np.kron(np.eye(8), np.ones((16, 16)))
    return table


def build(nc, t, out):
    x_tok = t["x"].rearrange("b (u h) w c -> (b u) (h w) c", u=TILES)
    out_tok = out.rearrange("b (u h) w c -> (b u) (h w) c", u=TILES)

    with ExitStack() as ctx:
        def sb(name, shape, dt=F32):
            return ctx.enter_context(nc.sbuf_tensor(name, shape, dt))

        def sem(name):
            return ctx.enter_context(nc.semaphore(name))

        const = sb("const", [P, CONST_W])
        w0 = sb("w0", [P, 192])
        w0o = sb("w0o", [P, C])
        w1q, w1k, w1v, w1o = (sb(n, [P, C]) for n in ("w1q", "w1k", "w1v", "w1o"))
        wqkv = sb("wqkv", [P, 3 * C])
        w2q, w2k, w2v = (sb(n, [P, C]) for n in ("w2q", "w2k", "w2v"))
        w2o = sb("w2o", [P, C])
        b2o = sb("b2o", [P, C])
        mlp1, mlp2 = sb("mlp1", [P, 2, 16]), sb("mlp2", [P, 2, 16])
        mlps = sb("mlps", [P, 4, 16])
        blk = sb("blk", [P, 4, P])
        blkT = sb("blkT", [P, 2, P])
        w1vT = sb("w1vT", [P, P])
        wvo = sb("wvo", [P, C])
        fold1 = sb("fold1", [P, 2, P])
        fold2 = sb("fold2", [P, 2, P])
        fold2t = sb("fold2t", [P, 2, P])
        cas_out = sb("cas_out", [P, P])
        rows = sb("rows", [NV, P])
        cols = sb("cols", [P, NV])
        derived = sb("derived", [P, 8])
        BQ, BO0, BO1, CP, CM, CT = range(6)
        half = sb("half", [P, 1])
        eps = sb("eps", [P, 2])
        sigma = sb("sigma", [P, 1])

        xin = sb("xin", [P, 2, TILES, C])
        x0T = sb("x0T", [P, TOK])
        pooled = sb("pooled", [P, POOLED])
        pg = sb("pg", [P, POOLED])
        thetaT = sb("thetaT", [P, TOK])
        nmax0, sum0, inv0 = (sb(n, [P, TILES]) for n in ("nmax0", "sum0", "inv0"))
        p0 = sb("p0", [P, TILES, POOLED])
        p0n = sb("p0n", [P, TILES, POOLED])
        p0T = sb("p0T", [P, TOK])
        gw = sb("gw", [P, C])
        x1T = sb("x1T", [P, TOK])
        bn = sb("bn", [P, 2, 6])
        mv = sb("mv", [P, 2, 2])
        gst = sb("gst", [P, 2, 2])
        nvar = sb("nvar", [P, 2])
        var = sb("var", [P, 2])
        vare = sb("vare", [P, 2])
        rstd = sb("rstd", [P, 2])
        gsc = sb("gsc", [P, 2])
        gms = sb("gms", [P, 2])
        gsh = sb("gsh", [P, 2])
        xn1 = sb("xn1", [P, TOK])
        q1T, k1T = sb("q1T", [P, TOK]), sb("k1T", [P, TOK])
        v1 = sb("v1", [P, TILES, C])
        nmax1, sum1, inv1 = (sb(n, [P, TILES]) for n in ("nmax1", "sum1", "inv1"))
        p1 = sb("p1", [P, TILES, TOK])
        p1n = sb("p1n", [P, TILES, TOK])
        p1T = sb("p1T", [P, TILES, TOK])
        x2T = sb("x2T", [P, TOK])
        xn2 = sb("xn2", [P, TOK])

        x2tok = sb("x2tok", [P, 2, TOK])
        parts = sb("parts", [P, PARTS, 2, TOK], BF16)
        rest = sb("rest", [P, 2, TOK])
        rest2 = sb("rest2", [P, 2, TOK])
        stack = [sb(f"stack{p}", [P, HEADS, 2, TOK], BF16) for p in range(2)]
        vaug = [sb(f"vaug{p}", [P, TILES, HEADS, 32]) for p in range(2)]
        nmax = sb("nmax", [P, HEADS, TILES])
        npart = sb("npart", [P, TILES, PARTS, HEADS])
        nbf = sb("nbf", [P, 2, HEADS, TILES], BF16)
        nrest = sb("nrest", [P, 2, HEADS, TILES])
        nmaxT = sb("nmaxT", [P, TOK], BF16)

        pT = sb("pT", [P, HEADS, TILES, TOK])
        oT = sb("oT", [P, 2, TOK])
        oinv = sb("oinv", [P, TILES, HEADS])
        on = sb("on", [P, TILES, HEADS, HD])
        onT = sb("onT", [P, TOK])
        x3 = sb("x3", [P, TOK])
        zE = sb("zE", [P, HE, WE])
        o1k = sb("o1k", [P, TOK])
        o1nE = sb("o1nE", [P, HE, WE])
        ylow = sb("ylow", [P, TOK])
        y = sb("y", [P, TOK])
        s1 = sb("s1", [P, TILES, C])
        xout = sb("xout", [P, TOK])

        A0, A1, B0, B1, C0, C1, C2_, C3 = (
            ctx.enter_context(nc.psum_tensor(f"bank{n}", [P, 512], F32)) for n in range(8))

        names = """const_in w0_zero w_in x_in0 x_in1 pe_setup dve_setup pool_setup act_setup
            x0T_pe x0T_rd proj_pe theta_rd pool_rd pg_rd s0_pe gw_rd nmax0_rd exp0_rd inv0_rd p0n_rd
            p0T_pe p0T_rd o0_pe x1_rd bn_rd mv_rd st_rd gn_pe gst_rd nvar_rd var_rd vare_rd rstd_rd
            gsc_rd gms_rd gsh_rd xn1_rd xn2_rd qk1_pe q1_rd v1_rd s1_pe nmax1_rd exp1_rd inv1_rd p1n_rd
            p1T_pe p1T_rd o1_pe x2_rd
            xv2_pe x2tok_rd vaug_rd qk2_pe part0_rd rest_rd part1_rd rest2_rd part2_rd
            stack_in smax_pe nmax_rd nb0_rd nr0_rd nb1_rd npart_rd nmT_pe nmT_rd neg_in
            sT_pe exp_rd pv_pe oT_rd oTT_pe oinv_rd on_rd onT_pe onT_rd o2_pe x3_rd
            z_pe z_rd zE_rd a_pe o1k_rd o1n_rd y_pe ylow_rd y_rd v3_pe v3_rd out_pe out_rd out_st""".split()
        s = {n: sem(n) for n in names}
        block = ctx.enter_context(nc.Block())

        ident = const[:, IDENT:IDENT + P]

        def after(engine, name, value):
            if not (isinstance(value, int) and value <= 0):
                engine.wait_ge(s[name], value)

        def wait_apart(engine, name, value):
            if not (isinstance(value, int) and value <= 0):
                value if isinstance(value, int) else engine.lower_val(value)
                engine.wait_ge(s["const_in"], 16)
                engine.wait_ge(s[name], value)

        def steps(engine, step):
            first, turns = 3, (IMAGES - 3) // 2
            step(0, 0, "A")
            step(1, 1, "AB")
            step(2, 0, "ABC")
            with engine.Fori(0, turns) as turn:
                for k in range(2):
                    step(turn * 2 + (first + k), (first + k) % 2, "ABC")
            for n in range(first + 2 * turns, IMAGES):
                step(n, n % 2, "ABC")
            step(IMAGES, 0, "BC")
            step(IMAGES + 1, 1, "C")

        weights = (
            (rows[0:1, 0:C8], t["L0_conv_b_phi"].rearrange("(a n) -> a n", a=1)),
            (rows[0:1, 64:64 + C2], t["L0_conv_b_g"].rearrange("(a n) -> a n", a=1)),
            (rows[1:2, 0:C8], t["L0_conv_b_theta"].rearrange("(a n) -> a n", a=1)),
            *((rows[r:r + 1, :], t[name].rearrange("(a n) -> a n", a=1))
              for r, name in enumerate(VECTORS) if name[0] == "L"),
            (rows[VEC["b1_0"]:VEC["b1_1"] + 1, :], t["L3_conv_b1"].rearrange("a k o -> a (k o)")),
            (rows[VEC["b2_0"]:VEC["b2_1"] + 1, :], t["L3_conv_b2"].rearrange("a k o -> a (k o)")),
            (sigma[:, :], t["L0_conv_sigma"].rearrange("(a n) -> a n", a=1).to_broadcast((P, 1))),
            (w0[:, 0:C8], t["L0_conv_w_phi"]),
            (w0[:, 64:128], t["L0_conv_w_g"]),
            (w0[:, 128:128 + C8], t["L0_conv_w_theta"]),
            (w0o[64:128, :], t["L0_conv_w_o"]),
            (w1q[:, :], t["L1_conv_wq"]), (w1k[:, :], t["L1_conv_wk"]),
            (w1v[:, :], t["L1_conv_wv"]), (w1o[:, :], t["L1_conv_wo"]),
            (wqkv[:, :], t["L2_conv_w_qkv"]), (w2o[:, :], t["L2_conv_w_out"]),
            (b2o[:, :], t["L2_conv_b_out"].rearrange("(a n) -> a n", a=1).to_broadcast((P, C))),
            (mlp1[:, :, :], t["L3_conv_w1"].rearrange("a k i o -> (k i) a o")),
            (mlp2[:, :, :], t["L3_conv_w2"].rearrange("a k i o -> (k i) a o")),
        )
        WEIGHTS = 16 * len(weights)
        STACKS = sum(1 if a == b else 2 for a, b in PAIRS)

        @block.sync
        def _(sp):
            sp.dma_start(const[:, :], t["constants"]).then_inc(s["const_in"], 16)
            sp.wait_ge(s["w0_zero"], 2)
            for dst, src in weights:
                sp.dma_start(dst, src).then_inc(s["w_in"], 16)

            def load_x(i, p):
                wait_apart(sp, "x0T_pe", i - 1)
                sp.dma_start(xin[:, p, :, :],
                             x_tok[bass.ds(i * TILES, TILES)].rearrange("u p c -> p u c")
                             ).then_inc(s[f"x_in{p}"], 16)

            def spread(i, p):
                wait_apart(sp, "sT_pe", (i - 1) * HEADS)
                for g, (a, b) in enumerate(PAIRS):
                    sp.wait_ge(s[("part0_rd", "part1_rd", "part2_rd")[max(a, b)]], i + 1)
                    if a == b:
                        sp.dma_start(stack[p][g * HD:(g + 1) * HD, :, :, :], parts[:, a, :, :]
                                     ).then_inc(s["stack_in"], 16)
                    else:
                        for which, part in enumerate((a, b)):
                            sp.dma_start(stack[p][g * HD:(g + 1) * HD, :, which, :], parts[:, part, which, :]
                                         ).then_inc(s["stack_in"], 16)

            def spread_maxima(i, p):
                sp.wait_ge(s["nmT_rd"], i + 1)
                sp.dma_start(stack[p][ROWS:AUG, :, 0, :], nmaxT[0:PARTS * HEADS, :]).then_inc(s["neg_in"], 16)

            def store(i):
                wait_apart(sp, "out_rd", i + 1)
                sp.dma_start(out_tok[bass.ds(i * TILES, TILES)].rearrange("u p c -> p u c"),
                             xout[:, :].rearrange("p (u c) -> p u c", u=TILES)).then_inc(s["out_st"], 16)

            def step(n, parity, threads):
                if "B" in threads:
                    spread(n - 1, 1 - parity)
                if "A" in threads and not (isinstance(n, int) and n + 1 >= IMAGES):
                    load_x(n + 1, 1 - parity)
                if "B" in threads:
                    spread_maxima(n - 1, 1 - parity)
                if "C" in threads:
                    store(n - 2)

            load_x(0, 0)
            steps(sp, step)
            sp.wait_ge(s["out_st"], 16 * IMAGES)

        @block.gpsimd
        def _(pool):
            nc.gpsimd.memset(w0[:, :], 0.0).then_inc(s["w0_zero"], 1)
            pool.wait_ge(s["w0_zero"], 1)
            nc.gpsimd.memset(rows[:, :], 0.0).then_inc(s["w0_zero"], 1)
            pool.wait_ge(s["w0_zero"], 2)
            for n, (tile, value) in enumerate((
                (half[:, :], -0.5), (eps[:, 0:1], EPS1), (eps[:, 1:2], EPS2),
                (vaug[0][:, :, :, HD:32], 0.0), (vaug[1][:, :, :, HD:32], 0.0),
                (vaug[0][:, :, :, HD:HD + 1], 1.0), (vaug[1][:, :, :, HD:HD + 1], 1.0),
                (stack[0][ROWS:AUG, :, 1, :], 1.0), (stack[1][ROWS:AUG, :, 1, :], 1.0),
            )):
                nc.gpsimd.memset(tile, value).then_inc(s["pool_setup"], 1)
                pool.wait_ge(s["pool_setup"], n + 1)
            pool.wait_ge(s["dve_setup"], 2)

            def group_norm(i, layer, gamma, beta):
                c = slice(layer, layer + 1)
                k = 2 * i + layer + 1
                pool.wait_ge(s["var_rd"], k)
                nc.gpsimd.tensor_tensor(vare[:, c], var[:, c], eps[:, c], ALU.add).then_inc(s["vare_rd"], 1)
                pool.wait_ge(s["vare_rd"], k)
                nc.gpsimd.tensor_tensor(rstd[:, c], vare[:, c], half[:, :], ALU.pow).then_inc(s["rstd_rd"], 1)
                pool.wait_ge(s["rstd_rd"], k)
                nc.gpsimd.tensor_tensor(gsc[:, c], rstd[:, c], cols[:, gamma:gamma + 1], ALU.mult).then_inc(s["gsc_rd"], 1)
                pool.wait_ge(s["gsc_rd"], k)
                nc.gpsimd.tensor_tensor(gms[:, c], gst[:, layer, 0:1], gsc[:, c], ALU.mult).then_inc(s["gms_rd"], 1)
                pool.wait_ge(s["gms_rd"], k)
                nc.gpsimd.tensor_tensor(gsh[:, c], cols[:, beta:beta + 1], gms[:, c], ALU.subtract).then_inc(s["gsh_rd"], 1)

            def split(i):
                pool.wait_ge(s["part1_rd"], i + 1)
                nc.gpsimd.tensor_tensor(parts[:, 2, :, :], rest[:, :, :], parts[:, 1, :, :], ALU.subtract
                                        ).then_inc(s["part2_rd"], 1)

            def step(n, parity, threads):
                if "B" in threads:
                    split(n - 1)
                if "A" in threads:
                    group_norm(n, 0, VEC["L1_conv_gn_gamma"], VEC["L1_conv_gn_beta"])
                    group_norm(n, 1, VEC["L2_conv_gn_scale"], VEC["L2_conv_gn_bias"])

            steps(pool, step)

        @block.tensor
        def _(pe):
            mm, tr = nc.tensor.matmul, nc.tensor.transpose
            pe.wait_ge(s["const_in"], 16)
            pe.wait_ge(s["w_in"], WEIGHTS)
            tr(A0[:, 0:NV], rows[:, :], ident[0:NV, 0:NV]).then_inc(s["pe_setup"], 1)
            tr(A1[:, 0:P], w1v[:, :], ident).then_inc(s["pe_setup"], 1)
            pe.wait_ge(s["dve_setup"], 1)
            tr(B0[:, 0:P], blk[:, 2, :], ident)
            tr(B0[:, P:2 * P], blk[:, 3, :], ident).then_inc(s["pe_setup"], 1)
            for m in range(2):
                mm(B1[:, m * P:(m + 1) * P], const[:, CAS_C:CAS_C + C], blk[:, m, :], start=True, stop=True
                   ).then_inc(s["pe_setup"], 1)
            pe.wait_ge(s["dve_setup"], 3)
            mm(A1[:, 0:C], w1vT[:, :], w1o[:, :], start=True, stop=True)
            mm(A1[:, C:C + 1], w1o[:, :], cols[:, VEC["L1_conv_bv"]:VEC["L1_conv_bv"] + 1],
               start=True, stop=True).then_inc(s["pe_setup"], 1)
            for m in range(2):
                mm(B0[:, m * P:(m + 1) * P], blkT[:, m, :], blk[:, 3, :], start=True, stop=True)
            mm(B0[:, 2 * P:2 * P + 1], blk[:, 3, :], cols[:, VEC["b2_0"]:VEC["b2_0"] + 1], start=True, stop=True
               ).then_inc(s["pe_setup"], 1)
            pe.wait_ge(s["dve_setup"], 4)
            pe.wait_ge(s["pool_setup"], 9)

            def x_transposed(i, p):
                pe.wait_ge(s[f"x_in{p}"], 8 * (i - p) + 16)
                after(pe, "x2_rd", i)
                tr(A0[:, 0:P], xin[:, p, 0, :], ident)
                tr(A0[:, P:2 * P], xin[:, p, 1, :], ident).then_inc(s["x0T_pe"], 1)

            def project0(i):
                pe.wait_ge(s["x0T_rd"], i + 1)
                after(pe, "gst_rd", 2 * i)
                mm(A1[:, 0:TOK], w0[:, 0:P], x0T[:, :], start=True, stop=True)
                mm(A0[0:64, 0:TOK], w0[:, P:192], x0T[:, :], start=True, stop=True).then_inc(s["proj_pe"], 1)

            def scores0(i):
                pe.wait_ge(s["theta_rd"], i + 1)
                pe.wait_ge(s["pg_rd"], i + 1)
                for u in range(TILES):
                    mm(A0[:, u * POOLED:(u + 1) * POOLED], thetaT[0:64, u * P:(u + 1) * P], pg[0:64, :],
                       start=True, stop=True)
                mm(A1[0:POOLED, 0:C], pg[64:128, :], w0o[64:128, :], start=True, stop=True).then_inc(s["s0_pe"], 1)

            def p0_transposed(i):
                wait_apart(pe, "gw_rd", i + 1)
                pe.wait_ge(s["p0n_rd"], i + 1)
                for u in range(TILES):
                    last = tr(A1[0:POOLED, u * P:(u + 1) * P], p0n[:, u, :], ident)
                last.then_inc(s["p0T_pe"], 1)

            def attend0(i):
                pe.wait_ge(s["p0T_rd"], i + 1)
                mm(A0[:, 0:TOK], gw[0:POOLED, :], p0T[0:POOLED, :], start=True, stop=True).then_inc(s["o0_pe"], 1)

            def group_means(i, layer, table):
                pe.wait_ge(s["st_rd"], 2 * i + layer + 1)
                mm(A1[:, 0:2], const[:, table:table + P], mv[:, layer, :], start=True, stop=True).then_inc(s["gn_pe"], 1)

            def project1(i):
                pe.wait_ge(s["xn1_rd"], i + 1)
                mm(A0[:, 0:TOK], w1q[:, :], xn1[:, :], start=True, stop=True)
                mm(A0[:, TOK:2 * TOK], w1k[:, :], xn1[:, :], start=True, stop=True).then_inc(s["qk1_pe"], 1)
                for u in range(TILES):
                    last = mm(A1[:, u * C:(u + 1) * C], xn1[:, u * P:(u + 1) * P], wvo[:, :], start=True, stop=True)
                last.then_inc(s["qk1_pe"], 1)

            def scores1(i):
                pe.wait_ge(s["q1_rd"], 2 * i + 2)
                for u in range(TILES):
                    last = mm(A0[:, u * TOK:(u + 1) * TOK], q1T[:, u * P:(u + 1) * P], k1T[:, :], start=True, stop=True)
                last.then_inc(s["s1_pe"], 1)

            def p1_transposed(i):
                pe.wait_ge(s["v1_rd"], i + 1)
                for u in range(TILES):
                    pe.wait_ge(s["p1n_rd"], 2 * i + u + 1)
                    for m in range(TILES):
                        last = tr(A1[:, m * TOK + u * P:m * TOK + (u + 1) * P], p1n[:, u, m * P:(m + 1) * P], ident)
                last.then_inc(s["p1T_pe"], 1)

            def attend1(i):
                pe.wait_ge(s["p1T_rd"], i + 1)
                for m in range(TILES):
                    last = mm(A0[:, 0:TOK], v1[:, m, :], p1T[:, m, :], start=(m == 0), stop=(m == TILES - 1))
                last.then_inc(s["o1_pe"], 1)

            def project2(i):
                pe.wait_ge(s["xn2_rd"], i + 1)
                after(pe, "nmT_rd", i)
                for u in range(TILES):
                    tr(B0[:, u * P:(u + 1) * P], x2T[:, u * P:(u + 1) * P], ident)
                for u in range(TILES):
                    last = mm(B0[:, TOK + u * C:TOK + (u + 1) * C], xn2[:, u * P:(u + 1) * P], w2v[:, :],
                              start=True, stop=True)
                last.then_inc(s["xv2_pe"], 1)
                after(pe, "nmax_rd", HEADS * i)
                mm(B1[:, 0:TOK], w2q[:, :], xn2[:, :], start=True, stop=True)
                mm(B1[:, TOK:2 * TOK], w2k[:, :], xn2[:, :], start=True, stop=True).then_inc(s["qk2_pe"], 1)

            def scores_by_query(i, p, h):
                bank = (B0, B1)[h % 2]
                if h == 0:
                    pe.wait_ge(s["stack_in"], 16 * STACKS * i + 16 * STACKS)
                    pe.wait_ge(s["vaug_rd"], i + 1)
                    pe.wait_ge(s["rest_rd"], i + 1)
                if h >= 2:
                    pe.wait_ge(s["nmax_rd"], HEADS * i + h - 1)
                for u in range(TILES):
                    last = mm(bank[:, u * TOK:(u + 1) * TOK], stack[p][0:ROWS, h, 0, u * P:(u + 1) * P],
                              stack[p][0:ROWS, h, 1, :], start=True, stop=True)
                last.then_inc(s["smax_pe"], 1)

            def maxima_transposed(i):
                pe.wait_ge(s["npart_rd"], 3 * i + 3)
                for u in range(TILES):
                    last = tr(B0[0:PARTS * HEADS, u * P:(u + 1) * P],
                              npart[:, u, :, :].rearrange("p a h -> p (a h)"), ident)
                last.then_inc(s["nmT_pe"], 1)

            def scores_by_key(i, p, h):
                if h == 0:
                    pe.wait_ge(s["neg_in"], 16 * i + 16)
                    after(pe, "y_rd", i)
                if h == 1:
                    after(pe, "v3_rd", i)
                if h >= 2:
                    pe.wait_ge(s["exp_rd"], HEADS * i + h - 1)
                for m in range(TILES):
                    last = mm((C0, C1)[h % 2][:, m * TOK:(m + 1) * TOK], stack[p][0:AUG, h, 1, m * P:(m + 1) * P],
                              stack[p][0:AUG, h, 0, :], start=True, stop=True)
                last.then_inc(s["sT_pe"], 1)

            def attend2(i, p, g):
                pe.wait_ge(s["exp_rd"], HEADS * i + 4 * g + 4)
                if g == 0:
                    pe.wait_ge(s["vaug_rd"], i + 1)
                    after(pe, "out_rd", i)
                for m in range(TILES):
                    for j in range(4):
                        last = mm(C2_[32 * j:32 * j + 32, g * TOK:(g + 1) * TOK], vaug[p][:, m, 4 * g + j, :],
                                  pT[:, 4 * g + j, m, :], start=(m == 0), stop=(m == TILES - 1))
                last.then_inc(s["pv_pe"], 1)

            def o_back(i):
                pe.wait_ge(s["oT_rd"], i + 1)
                after(pe, "o1n_rd", i)
                for u in range(TILES):
                    for g in range(2):
                        last = tr(C3[:, (2 * u + g) * P:(2 * u + g + 1) * P], oT[:, g, u * P:(u + 1) * P], ident)
                last.then_inc(s["oTT_pe"], 1)

            def on_transposed(i):
                pe.wait_ge(s["on_rd"], i + 1)
                for u in range(TILES):
                    last = tr(C0[:, u * P:(u + 1) * P], on[:, u, :, :].rearrange("p h d -> p (h d)"), ident)
                last.then_inc(s["onT_pe"], 1)

            def project_out(i):
                pe.wait_ge(s["onT_rd"], i + 1)
                for u in range(TILES):
                    last = mm(C1[:, u * C:(u + 1) * C], onT[:, u * P:(u + 1) * P], w2o[:, :], start=True, stop=True)
                last.then_inc(s["o2_pe"], 1)

            def transform_w(i):
                pe.wait_ge(s["x3_rd"], i + 1)
                n = P // W * WE
                for u in range(TILES):
                    last = mm(C2_[:, u * n:(u + 1) * n], x3[:, u * C:(u + 1) * C], const[:, CAS_WE:CAS_WE + n],
                              start=True, stop=True)
                last.then_inc(s["z_pe"], 1)

            def hidden(i):
                pe.wait_ge(s["zE_rd"], i + 1)
                mm(C3[:, 0:EXT].rearrange("p (h w) -> p h w", h=HE), fold1[:, 0, :], zE[:, :, :], start=True, stop=False)
                mm(C3[:, 0:EXT].rearrange("p (h w) -> p h w", h=HE), fold1[:, 1, :], zE[:, ::-1, ::-1],
                   start=False, stop=True).then_inc(s["a_pe"], 1)

            def mlp_out(i):
                pe.wait_ge(s["o1k_rd"], i + 1)
                pe.wait_ge(s["o1n_rd"], i + 1)
                mm(C0[:, 0:TOK].rearrange("p (h w) -> p h w", h=H), fold2[:, 0, :],
                   o1k[:, :].rearrange("p (h w) -> p h w", h=H), start=True, stop=False)
                mm(C0[:, 0:TOK].rearrange("p (h w) -> p h w", h=H), fold2[:, 1, :],
                   o1nE[:, H:0:-1, W:0:-1], start=False, stop=True).then_inc(s["y_pe"], 1)

            def transform_c_back(i):
                pe.wait_ge(s["y_rd"], i + 1)
                for u in range(TILES):
                    last = mm(C1[:, u * C:(u + 1) * C], y[:, u * P:(u + 1) * P], cas_out[:, :], start=True, stop=True)
                last.then_inc(s["v3_pe"], 1)

            def transform_w_back(i):
                pe.wait_ge(s["v3_rd"], i + 1)
                mm(C2_[:, 0:TOK], const[:, CAS_W:CAS_W + P], s1[:, :, :].rearrange("p u c -> p (u c)"),
                   start=True, stop=True).then_inc(s["out_pe"], 1)

            def step(n, p, threads):
                a, b, c = ("A" in threads), ("B" in threads), ("C" in threads)
                q = 1 - p
                if b: project2(n - 1)
                if a: x_transposed(n, p)
                if c: scores_by_key(n - 2, p, 0)
                if c: scores_by_key(n - 2, p, 1)
                if a: project0(n)
                if c: scores_by_key(n - 2, p, 2)
                if c: scores_by_key(n - 2, p, 3)
                if a: scores0(n)
                if c: scores_by_key(n - 2, p, 4)
                if c: scores_by_key(n - 2, p, 5)
                if a: p0_transposed(n)
                if c: attend2(n - 2, p, 0)
                if c: scores_by_key(n - 2, p, 6)
                if a: attend0(n)
                if c: scores_by_key(n - 2, p, 7)
                if a: group_means(n, 0, MEAN1)
                if b: scores_by_query(n - 1, q, 0)
                if b: scores_by_query(n - 1, q, 1)
                if c: attend2(n - 2, p, 1)
                if a: project1(n)
                if b: scores_by_query(n - 1, q, 2)
                if c: o_back(n - 2)
                if b: scores_by_query(n - 1, q, 3)
                if a: scores1(n)
                if c: on_transposed(n - 2)
                if b: scores_by_query(n - 1, q, 4)
                if c: project_out(n - 2)
                if b: scores_by_query(n - 1, q, 5)
                if c: transform_w(n - 2)
                if a: p1_transposed(n)
                if b: scores_by_query(n - 1, q, 6)
                if c: hidden(n - 2)
                if a: attend1(n)
                if b: scores_by_query(n - 1, q, 7)
                if c: mlp_out(n - 2)
                if a: group_means(n, 1, MEAN2)
                if b: maxima_transposed(n - 1)
                if c: transform_c_back(n - 2)
                if c: transform_w_back(n - 2)

            steps(pe, step)

        @block.scalar
        def _(act):
            act.wait_ge(s["dve_setup"], 4)
            go, copy = nc.scalar.activation, nc.scalar.copy

            def col(n):
                return cols[:, n:n + 1]

            def x0T_out(i):
                act.wait_ge(s["x0T_pe"], i + 1)
                after(act, "x1_rd", i)
                copy(x0T[:, :], A0[:, 0:TOK]).then_inc(s["x0T_rd"], 1)

            def theta_out(i):
                act.wait_ge(s["proj_pe"], i + 1)
                b = VEC["b_theta"]
                go(thetaT[0:64, :], A0[0:64, 0:TOK], ACT.Identity, bias=cols[0:64, b:b + 1]).then_inc(s["theta_rd"], 1)

            def exp0(i):
                act.wait_ge(s["s0_pe"], i + 1)
                copy(gw[0:POOLED, :], A1[0:POOLED, 0:C]).then_inc(s["gw_rd"], 1)
                act.wait_ge(s["nmax0_rd"], i + 1)
                for u in range(TILES):
                    go(p0[:, u, :], A0[:, u * POOLED:(u + 1) * POOLED], ACT.Exp, bias=nmax0[:, u:u + 1],
                       accum_out=sum0[:, u:u + 1]).then_inc(s["exp0_rd"], 1)

            def p0T_out(i):
                act.wait_ge(s["p0T_pe"], i + 1)
                copy(p0T[0:POOLED, :], A1[0:POOLED, 0:TOK]).then_inc(s["p0T_rd"], 1)

            def q1_out(i):
                act.wait_ge(s["qk1_pe"], 2 * i + 1)
                go(q1T[:, :], A0[:, 0:TOK], ACT.Identity, bias=derived[:, BQ:BQ + 1], scale=float(C) ** -0.5
                   ).then_inc(s["q1_rd"], 1)
                go(k1T[:, :], A0[:, TOK:2 * TOK], ACT.Identity, bias=col(VEC["L1_conv_bk"])).then_inc(s["q1_rd"], 1)

            def exp1(i):
                act.wait_ge(s["nmax1_rd"], i + 1)
                after(act, "p1n_rd", 2 * i)
                for u in range(TILES):
                    go(p1[:, u, :], A0[:, u * TOK:(u + 1) * TOK], ACT.Exp, bias=nmax1[:, u:u + 1],
                       accum_out=sum1[:, u:u + 1]).then_inc(s["exp1_rd"], 1)

            def p1T_out(i):
                act.wait_ge(s["p1T_pe"], i + 1)
                copy(p1T[:, :, :].rearrange("p m t -> p (m t)"), A1[:, :]).then_inc(s["p1T_rd"], 1)

            def part0(i):
                act.wait_ge(s["qk2_pe"], i + 1)
                after(act, "stack_in", 16 * STACKS * i)
                copy(parts[:, 0, :, :].rearrange("p w t -> p (w t)"), B1[:, :]).then_inc(s["part0_rd"], 1)

            def x2_and_v(i, p):
                act.wait_ge(s["xv2_pe"], i + 1)
                after(act, "x3_rd", i - 1)
                copy(x2tok[:, p, :], B0[:, 0:TOK]).then_inc(s["x2tok_rd"], 1)
                after(act, "pv_pe", 2 * (i - 1))
                copy(vaug[p][:, :, :, 0:HD], B0[:, TOK:2 * TOK].rearrange("p (u h d) -> p u h d", u=TILES, h=HEADS)
                     ).then_inc(s["vaug_rd"], 1)

            def maxima_out(i):
                act.wait_ge(s["nmT_pe"], i + 1)
                after(act, "neg_in", 16 * i)
                copy(nmaxT[0:PARTS * HEADS, :], B0[0:PARTS * HEADS, 0:TOK]).then_inc(s["nmT_rd"], 1)

            def exp2(i, h):
                act.wait_ge(s["sT_pe"], HEADS * i + h + 1)
                if h == 0:
                    after(act, "pv_pe", 2 * i)
                go(pT[:, h, :, :].rearrange("p m t -> p (m t)"), (C0, C1)[h % 2][:, :], ACT.Exp
                   ).then_inc(s["exp_rd"], 1)

            def oT_out(i):
                act.wait_ge(s["pv_pe"], 2 * i + 2)
                copy(oT[:, :, :].rearrange("p g t -> p (g t)"), C2_[:, :]).then_inc(s["oT_rd"], 1)

            def onT_out(i):
                act.wait_ge(s["onT_pe"], i + 1)
                copy(onT[:, :], C0[:, 0:TOK]).then_inc(s["onT_rd"], 1)

            def z_out(i):
                act.wait_ge(s["z_pe"], i + 1)
                copy(zE[:, 0:H, :].rearrange("p h w -> p (h w)"), C2_[:, 0:H * WE]).then_inc(s["z_rd"], 1)

            def o1k_out(i):
                act.wait_ge(s["a_pe"], i + 1)
                go(o1k[:, :].rearrange("p (h w) -> p h w", h=H),
                   C3[:, 0:EXT].rearrange("p (h w) -> p h w", h=HE)[:, 0:H, 0:W], ACT.Relu, bias=col(VEC["b1_0"])
                   ).then_inc(s["o1k_rd"], 1)

            def v3_out(i):
                act.wait_ge(s["v3_pe"], i + 1)
                copy(s1[:, :, :].rearrange("p u c -> p (u c)"), C1[:, 0:TOK]).then_inc(s["v3_rd"], 1)

            def step(n, p, threads):
                a, b, c = ("A" in threads), ("B" in threads), ("C" in threads)
                q = 1 - p
                if b: part0(n - 1)
                if a: x0T_out(n)
                if b: x2_and_v(n - 1, q)
                if c: exp2(n - 2, 0)
                if c: exp2(n - 2, 1)
                if a: theta_out(n)
                if c: exp2(n - 2, 2)
                if c: exp2(n - 2, 3)
                if a: exp0(n)
                if c: exp2(n - 2, 4)
                if c: exp2(n - 2, 5)
                if a: p0T_out(n)
                if c: exp2(n - 2, 6)
                if c: exp2(n - 2, 7)
                if a: q1_out(n)
                if c: oT_out(n - 2)
                if a: exp1(n)
                if c: onT_out(n - 2)
                if c: z_out(n - 2)
                if a: p1T_out(n)
                if c: o1k_out(n - 2)
                if b: maxima_out(n - 1)
                if c: v3_out(n - 2)

            steps(act, step)

        @block.vector
        def _(dve):
            v = nc.vector
            dve.wait_ge(s["const_in"], 16)
            dve.wait_ge(s["w_in"], WEIGHTS)
            own = [0]

            def then(ins, name="act_setup"):
                own[0] += 1
                ins.then_inc(s["act_setup"], 1)
                dve.wait_ge(s["act_setup"], own[0])

            for n, m in enumerate((mlp1, mlp2)):
                v.tensor_tensor(mlps[:, 2 * n, :], m[:, 0, :], m[:, 1, :], ALU.add)
                then(v.tensor_tensor(mlps[:, 2 * n + 1, :], m[:, 0, :], m[:, 1, :], ALU.subtract))
            mask = const[:, BLOCKS:BLOCKS + P].rearrange("p (k o) -> p k o", k=8)
            for m in range(4):
                last = v.scalar_tensor_tensor(out=blk[:, m, :].rearrange("p (k o) -> p k o", k=8), in0=mask, scalar=0.5,
                                              in1=mlps[:, m, :].unsqueeze(1).to_broadcast((P, 8, 16)),
                                              op0=ALU.mult, op1=ALU.mult)
            last.then_inc(s["dve_setup"], 1)
            dve.wait_ge(s["pe_setup"], 1)
            then(v.tensor_copy(cols[:, :], A0[:, 0:NV]))
            v.tensor_scalar(w0o[64:128, :], w0o[64:128, :], sigma[64:128, :], None, ALU.mult)
            v.tensor_tensor(derived[:, BO0:BO0 + 1], cols[:, VEC["L0_conv_b_o"]:VEC["L0_conv_b_o"] + 1],
                            sigma[:, :], ALU.mult)
            v.tensor_scalar(derived[:, BQ:BQ + 1], cols[:, VEC["L1_conv_bq"]:VEC["L1_conv_bq"] + 1],
                            float(C) ** -0.5, None, ALU.mult).then_inc(s["dve_setup"], 1)
            dve.wait_ge(s["pe_setup"], 2)
            v.tensor_copy(w1vT[:, :], A1[:, 0:P])
            dve.wait_ge(s["pe_setup"], 3)
            v.tensor_copy(blkT[:, :, :].rearrange("p m n -> p (m n)"), B0[:, 0:2 * P])
            dve.wait_ge(s["pe_setup"], 5)
            v.tensor_copy(fold1[:, :, :].rearrange("p m n -> p (m n)"), B1[:, 0:2 * P]).then_inc(s["dve_setup"], 1)
            heads = wqkv[:, :].rearrange("c (h w d) -> c w d h", h=HEADS, w=3)
            v.tensor_scalar(w2q[:, :].rearrange("c (d h) -> c d h", d=HD), heads[:, 0], float(HD) ** -0.5, None, ALU.mult)
            v.tensor_copy(w2k[:, :].rearrange("c (d h) -> c d h", d=HD), heads[:, 1])
            v.tensor_copy(w2v[:, :].rearrange("c (h d) -> c h d", h=HEADS),
                          wqkv[:, :].rearrange("c (h w d) -> c w h d", h=HEADS, w=3)[:, 2])
            v.tensor_scalar(cas_out[:, :], const[:, CAS_C:CAS_C + C], 1.0 / (W * C), None, ALU.mult)
            dve.wait_ge(s["pe_setup"], 6)
            v.tensor_copy(wvo[:, :], A1[:, 0:C])
            v.tensor_tensor(derived[:, BO1:BO1 + 1], A1[:, C:C + 1], cols[:, VEC["L1_conv_bo"]:VEC["L1_conv_bo"] + 1],
                            ALU.add)
            dve.wait_ge(s["pe_setup"], 7)
            v.tensor_tensor(fold2[:, 0, :], B0[:, 0:P], blk[:, 2, :], ALU.add)
            v.tensor_tensor(fold2t[:, 0, :], B0[:, P:2 * P], blk[:, 2, :], ALU.add)
            then(v.tensor_tensor(derived[:, CT:CT + 1], B0[:, 2 * P:2 * P + 1], cols[:, VEC["b2_0"]:VEC["b2_0"] + 1],
                                 ALU.add))
            v.tensor_tensor(fold2[:, 1, :], fold2t[:, 0, :], blk[:, 3, :], ALU.add)
            v.scalar_tensor_tensor(out=derived[:, CP:CP + 1], in0=derived[:, CT:CT + 1], scalar=SPARSITY,
                                   in1=cols[:, VEC["b2_1"]:VEC["b2_1"] + 1], op0=ALU.add, op1=ALU.add)
            then(v.scalar_tensor_tensor(out=derived[:, CM:CM + 1], in0=derived[:, CT:CT + 1], scalar=-SPARSITY,
                                        in1=cols[:, VEC["b2_1"]:VEC["b2_1"] + 1], op0=ALU.add, op1=ALU.add))
            v.tensor_copy(derived[:, 6:7], derived[:, CT:CT + 1]).then_inc(s["dve_setup"], 1)

            def pool_out(i):
                dve.wait_ge(s["proj_pe"], i + 1)
                v.tensor_reduce(pooled[:, :], A1[:, 0:TOK].rearrange("p (h a w b) -> p h w a b", h=H // 2, a=2, b=2),
                                AX.XY, ALU.max).then_inc(s["pool_rd"], 1)
                dve.wait_ge(s["pool_rd"], i + 1)
                b = VEC["b_phi_g"]
                v.tensor_scalar(pg[:, :], pooled[:, :], cols[:, b:b + 1], None, ALU.add).then_inc(s["pg_rd"], 1)

            def nmax0_out(i):
                dve.wait_ge(s["s0_pe"], i + 1)
                v.tensor_reduce(nmax0[:, :], A0[:, 0:TILES * POOLED].rearrange("p (u m) -> p u m", u=TILES),
                                AX.X, ALU.max, negate=True).then_inc(s["nmax0_rd"], 1)

            def norm_p0(i):
                dve.wait_ge(s["exp0_rd"], 2 * i + 2)
                v.reciprocal(inv0[:, :], sum0[:, :]).then_inc(s["inv0_rd"], 1)
                dve.wait_ge(s["inv0_rd"], i + 1)
                v.tensor_tensor(p0n[:, :, :], p0[:, :, :], inv0[:, :].unsqueeze(2).to_broadcast((P, TILES, POOLED)),
                                ALU.mult).then_inc(s["p0n_rd"], 1)

            def statistics(i, layer, x, ready):
                k = 2 * i + layer + 1
                dve.wait_ge(s[ready], i + 1)
                v.bn_stats(bn[:, layer, :], x[:, :]).then_inc(s["bn_rd"], 1)
                wait_apart(dve, "bn_rd", k)
                v.bn_aggr(mv[:, layer, :], bn[:, layer, :]).then_inc(s["mv_rd"], 1)
                dve.wait_ge(s["mv_rd"], k)
                v.scalar_tensor_tensor(out=mv[:, layer, 1:2], in0=mv[:, layer, 0:1], scalar=mv[:, layer, 0:1],
                                       in1=mv[:, layer, 1:2], op0=ALU.mult, op1=ALU.add).then_inc(s["st_rd"], 1)

            def group_variance(i, layer):
                k = 2 * i + layer + 1
                dve.wait_ge(s["gn_pe"], k)
                after(dve, "gms_rd", k - 2)
                v.tensor_copy(gst[:, layer, :], A1[:, 0:2]).then_inc(s["gst_rd"], 1)
                dve.wait_ge(s["gst_rd"], k)
                v.scalar_tensor_tensor(out=nvar[:, layer:layer + 1], in0=gst[:, layer, 0:1], scalar=gst[:, layer, 0:1],
                                       in1=gst[:, layer, 1:2], op0=ALU.mult, op1=ALU.subtract).then_inc(s["nvar_rd"], 1)
                dve.wait_ge(s["nvar_rd"], k)
                v.tensor_scalar(var[:, layer:layer + 1], nvar[:, layer:layer + 1], -1.0, 0.0, ALU.mult, ALU.max
                                ).then_inc(s["var_rd"], 1)

            def x1_out(i):
                dve.wait_ge(s["o0_pe"], i + 1)
                after(dve, "x2_rd", i)
                v.scalar_tensor_tensor(out=x1T[:, :], in0=A0[:, 0:TOK], scalar=derived[:, BO0:BO0 + 1], in1=x0T[:, :],
                                       op0=ALU.add, op1=ALU.add).then_inc(s["x1_rd"], 1)
                statistics(i, 0, x1T, "x1_rd")

            def xn_out(i, layer, x, xn, done):
                dve.wait_ge(s["gsh_rd"], 2 * i + layer + 1)
                if layer == 0:
                    after(dve, "qk1_pe", 2 * i)
                else:
                    after(dve, "qk2_pe", i)
                c = slice(layer, layer + 1)
                v.tensor_scalar(xn[:, :], x[:, :], gsc[:, c], gsh[:, c], ALU.mult, ALU.add).then_inc(s[done], 1)

            def v1_out(i):
                dve.wait_ge(s["qk1_pe"], 2 * i + 2)
                v.tensor_copy(v1[:, :, :].rearrange("p u c -> p (u c)"), A1[:, 0:TOK]).then_inc(s["v1_rd"], 1)

            def nmax1_out(i):
                dve.wait_ge(s["s1_pe"], i + 1)
                v.tensor_reduce(nmax1[:, :], A0[:, :].rearrange("p (u m) -> p u m", u=TILES), AX.X, ALU.max,
                                negate=True).then_inc(s["nmax1_rd"], 1)

            def norm_p1(i):
                dve.wait_ge(s["exp1_rd"], 2 * i + 2)
                v.reciprocal(inv1[:, :], sum1[:, :]).then_inc(s["inv1_rd"], 1)
                dve.wait_ge(s["inv1_rd"], i + 1)
                for u in range(TILES):
                    v.tensor_scalar(p1n[:, u, :], p1[:, u, :], inv1[:, u:u + 1], None, ALU.mult).then_inc(s["p1n_rd"], 1)

            def x2_out(i):
                dve.wait_ge(s["o1_pe"], i + 1)
                after(dve, "xv2_pe", i)
                after(dve, "xn2_rd", i)
                v.scalar_tensor_tensor(out=x2T[:, :], in0=A0[:, 0:TOK], scalar=derived[:, BO1:BO1 + 1], in1=x1T[:, :],
                                       op0=ALU.add, op1=ALU.add).then_inc(s["x2_rd"], 1)
                statistics(i, 1, x2T, "x2_rd")

            def rest_out(i):
                dve.wait_ge(s["part0_rd"], i + 1)
                after(dve, "part2_rd", i)
                v.tensor_tensor(rest[:, :, :].rearrange("p w t -> p (w t)"), B1[:, :],
                                parts[:, 0, :, :].rearrange("p w t -> p (w t)"), ALU.subtract).then_inc(s["rest_rd"], 1)
                dve.wait_ge(s["rest_rd"], i + 1)
                after(dve, "stack_in", 16 * STACKS * i)
                v.tensor_copy(parts[:, 1, :, :], rest[:, :, :]).then_inc(s["part1_rd"], 1)

            def nmax_out(i, h):
                dve.wait_ge(s["smax_pe"], HEADS * i + h + 1)
                v.tensor_reduce(nmax[:, h, :], (B0, B1)[h % 2][:, :].rearrange("p (u m) -> p u m", u=TILES),
                                AX.X, ALU.max, negate=True).then_inc(s["nmax_rd"], 1)

            def split_maxima(i):
                dve.wait_ge(s["nmax_rd"], HEADS * i + HEADS)
                after(dve, "nmT_pe", i)
                v.tensor_copy(nbf[:, 0], nmax[:, :, :]).then_inc(s["nb0_rd"], 1)
                dve.wait_ge(s["nb0_rd"], i + 1)
                v.tensor_tensor(nrest[:, 0], nmax[:, :, :], nbf[:, 0], ALU.subtract).then_inc(s["nr0_rd"], 1)
                v.tensor_copy(npart[:, :, 0, :].rearrange("p u h -> p h u"), nbf[:, 0]).then_inc(s["npart_rd"], 1)
                dve.wait_ge(s["nr0_rd"], i + 1)
                v.tensor_copy(nbf[:, 1], nrest[:, 0]).then_inc(s["nb1_rd"], 1)
                dve.wait_ge(s["nb1_rd"], i + 1)
                v.tensor_tensor(npart[:, :, 2, :].rearrange("p u h -> p h u"), nrest[:, 0], nbf[:, 1], ALU.subtract
                                ).then_inc(s["npart_rd"], 1)
                v.tensor_copy(npart[:, :, 1, :].rearrange("p u h -> p h u"), nbf[:, 1]).then_inc(s["npart_rd"], 1)

            def normalise_o(i):
                dve.wait_ge(s["oTT_pe"], i + 1)
                o = C3[:, :].rearrange("p (u h d) -> p u h d", u=TILES, h=HEADS)
                v.reciprocal(oinv[:, :, :], o[:, :, :, HD]).then_inc(s["oinv_rd"], 1)
                dve.wait_ge(s["oinv_rd"], i + 1)
                v.tensor_tensor(on[:, :, :, :], o[:, :, :, 0:HD],
                                oinv[:, :, :].unsqueeze(3).to_broadcast((P, TILES, HEADS, HD)), ALU.mult
                                ).then_inc(s["on_rd"], 1)

            def x3_out(i, p):
                dve.wait_ge(s["o2_pe"], i + 1)
                dve.wait_ge(s["x2tok_rd"], i + 1)
                after(dve, "out_rd", i)
                v.tensor_tensor(x3[:, :], C1[:, 0:TOK], x2tok[:, p, :], ALU.add).then_inc(s["ylow_rd"], 1)
                dve.wait_ge(s["ylow_rd"], 2 * i + 1)
                v.tensor_tensor(x3[:, :].rearrange("p (u c) -> p u c", u=TILES),
                                x3[:, :].rearrange("p (u c) -> p u c", u=TILES),
                                b2o[:, :].unsqueeze(1).to_broadcast((P, TILES, C)), ALU.add).then_inc(s["x3_rd"], 1)

            def wrap_z(i):
                dve.wait_ge(s["z_rd"], i + 1)
                after(dve, "a_pe", i)
                v.tensor_copy(zE[:, H, :], zE[:, 0, :]).then_inc(s["zE_rd"], 1)

            def o1n_out(i):
                dve.wait_ge(s["o1k_rd"], i + 1)
                b = VEC["b1_1"]
                v.tensor_scalar(o1nE[:, :, :].rearrange("p h w -> p (h w)"), C3[:, 0:EXT], cols[:, b:b + 1], 0.0,
                                ALU.add, ALU.max).then_inc(s["o1n_rd"], 1)

            def y_out(i):
                dve.wait_ge(s["y_pe"], i + 1)
                v.tensor_scalar(ylow[:, :], C0[:, 0:TOK], derived[:, CP:CP + 1], 0.0, ALU.add, ALU.min
                                ).then_inc(s["ylow_rd"], 1)
                dve.wait_ge(s["ylow_rd"], 2 * i + 2)
                v.scalar_tensor_tensor(out=y[:, :], in0=C0[:, 0:TOK], scalar=derived[:, CM:CM + 1], in1=ylow[:, :],
                                       op0=ALU.add, op1=ALU.max).then_inc(s["y_rd"], 1)

            def x_out(i):
                dve.wait_ge(s["out_pe"], i + 1)
                after(dve, "out_st", 16 * i)
                v.tensor_tensor(xout[:, :], C2_[:, 0:TOK], x3[:, :], ALU.add).then_inc(s["out_rd"], 1)

            def step(n, p, threads):
                a, b, c = ("A" in threads), ("B" in threads), ("C" in threads)
                if b: rest_out(n - 1)
                if a: pool_out(n)
                if a: nmax0_out(n)
                if a: norm_p0(n)
                if a: x1_out(n)
                if a: group_variance(n, 0)
                if b: nmax_out(n - 1, 0)
                if a: xn_out(n, 0, x1T, xn1, "xn1_rd")
                if b: nmax_out(n - 1, 1)
                if a: v1_out(n)
                if b: nmax_out(n - 1, 2)
                if c: normalise_o(n - 2)
                if b: nmax_out(n - 1, 3)
                if a: nmax1_out(n)
                if b: nmax_out(n - 1, 4)
                if a: norm_p1(n)
                if c: x3_out(n - 2, p)
                if b: nmax_out(n - 1, 5)
                if c: wrap_z(n - 2)
                if b: nmax_out(n - 1, 6)
                if c: o1n_out(n - 2)
                if a: x2_out(n)
                if b: nmax_out(n - 1, 7)
                if c: y_out(n - 2)
                if b: split_maxima(n - 1)
                if a: group_variance(n, 1)
                if c: x_out(n - 2)
                if a: xn_out(n, 1, x2T, xn2, "xn2_rd")

            steps(dve, step)


def kernel(**inputs):
    import concourse.bacc as bacc
    from concourse.bass_utils import run_bass_kernel_spmd

    nc = bacc.Bacc("TRN2", target_bir_lowering=False, num_devices=1)
    arrays, tensors = {}, {}
    for name, a in {**inputs, "constants": constants()}.items():
        a = np.ascontiguousarray(a)
        arrays[f"in_{name}"] = a
        tensors[name] = nc.dram_tensor(f"in_{name}", a.shape, F32, kind="ExternalInput").ap()
    out = nc.dram_tensor("out", (IMAGES, H, W, C), F32, kind="ExternalOutput").ap()
    build(nc, tensors, out)
    got = run_bass_kernel_spmd(nc, [arrays], core_ids=[0])
    return got.results[0]["out"]
```

```python
from contextlib import ExitStack

import numpy as np

import concourse.bass as bass
from concourse import mybir

F32 = mybir.dt.float32
BF16 = mybir.dt.bfloat16
ALU = mybir.AluOpType
ACT = mybir.ActivationFunctionType
AX = mybir.AxisListType

IMAGES, H, W, C = 8, 16, 16, 128
P = 128
TOK = H * W
TILES = TOK // P
POOLED = TOK // 4
C8, C2 = C // 8, C // 2
HEADS, HD = 8, 16
HE, WE = H + 1, W + 1
EXT = HE * WE
PARTS = 3
PAIRS = ((0, 0), (1, 1), (0, 1), (1, 0), (0, 2), (2, 0))
ROWS = len(PAIRS) * HD
AUG = ROWS + PARTS
SPARSITY = 0.01
EPS1, EPS2 = 1e-6, 1e-5
GROUP1, GROUP2 = C // 32, C // 16

DEPTH = 5
START = 16

COLUMNS = ("b_phi_g", "b_theta", "sigma", "L0_conv_b_o", "L1_conv_gn_gamma", "L1_conv_gn_beta",
           "L1_conv_bq", "L1_conv_bk", "L1_conv_bv", "L1_conv_bo", "L2_conv_gn_scale",
           "L2_conv_gn_bias", "L2_conv_b_out", "b1_0", "b1_1", "b2_0", "b2_1")
LAYOUT = (
    (("columns", len(COLUMNS)), ("ident", P), ("w0", P), ("w0_o", C)),
    (("mean1", P), ("mean2", P), ("w1_q", C), ("w1_k", C), ("w1_vT", C), ("w1_o", C)),
    (("mlp", 6 * P), ("cas_c", C)),
    (("w2_q", C), ("w2_k", C), ("w2_v", C), ("w2_o", C), ("cas_w", P), ("cas_we", P // W * WE)),
)
AT = {}
for _group in LAYOUT:
    for _name, _width in _group:
        AT[_name] = (sum(w for _, w in AT.values()), _width)
TABLE_W = sum(w for _, w in AT.values())


def table(t):
    def cas(n):
        a = 2.0 * np.pi * (np.outer(np.arange(n), np.arange(n)) % n) / n
        return np.cos(a) + np.sin(a)

    def blocks(w):
        m = np.zeros((P, P), np.float32)
        for k in range(w.shape[0]):
            m[16 * k:16 * k + 16, 16 * k:16 * k + 16] = w[k]
        return m

    full = np.zeros((P, TABLE_W), np.float32)

    def at(name):
        first, width = AT[name]
        return full[:, first:first + width]

    rows = P // W
    at("ident")[:] = np.eye(P)
    at("mean1")[:] = np.kron(np.eye(C // GROUP1), np.full((GROUP1, GROUP1), 1.0 / GROUP1))
    at("mean2")[:] = np.kron(np.eye(C // GROUP2), np.full((GROUP2, GROUP2), 1.0 / GROUP2))
    at("cas_c")[:] = cas(C)
    at("cas_w")[:] = np.kron(np.eye(rows), cas(W))
    at("cas_we")[:] = np.kron(np.eye(rows), np.concatenate([cas(W), cas(W)[:, :1]], axis=1))
    at("w0")[:, 0:C8] = t["L0_conv_w_phi"]
    at("w0")[:, 32:32 + C8] = t["L0_conv_w_theta"]
    at("w0")[:, 64:128] = t["L0_conv_w_g"]
    at("w0_o")[64:128] = t["L0_conv_w_o"]
    at("w1_q")[:], at("w1_k")[:] = t["L1_conv_wq"], t["L1_conv_wk"]
    at("w1_vT")[:], at("w1_o")[:] = t["L1_conv_wv"].T, t["L1_conv_wo"]
    heads = t["L2_conv_w_qkv"].reshape(C, HEADS, 3, HD)
    at("w2_q")[:] = heads[:, :, 0].transpose(0, 2, 1).reshape(C, C)
    at("w2_k")[:] = heads[:, :, 1].transpose(0, 2, 1).reshape(C, C)
    at("w2_v")[:] = heads[:, :, 2].reshape(C, C)
    at("w2_o")[:] = t["L2_conv_w_out"]
    mlp = at("mlp").reshape(P, 2, 3, P)
    for k in range(2):
        w1, w2 = t["L3_conv_w1"][k], t["L3_conv_w2"][k]
        for n, m in enumerate((w1, w2, w2.transpose(0, 2, 1))):
            first = AT["mlp"][0] + (3 * k + n) * P
            full[:, first:first + P] = blocks(m)
    columns = dict(t)
    columns["b_phi_g"], columns["b_theta"] = np.zeros(P, np.float32), np.zeros(P, np.float32)
    columns["b_phi_g"][0:C8], columns["b_phi_g"][64:128] = t["L0_conv_b_phi"], t["L0_conv_b_g"]
    columns["b_theta"][0:C8] = t["L0_conv_b_theta"]
    columns["sigma"] = np.full(P, t["L0_conv_sigma"].reshape(-1)[0], np.float32)
    for k in range(2):
        columns[f"b1_{k}"], columns[f"b2_{k}"] = t["L3_conv_b1"][k].reshape(-1), t["L3_conv_b2"][k].reshape(-1)
    for n, name in enumerate(COLUMNS):
        at("columns")[:, n] = columns[name]
    return full


def build(nc, x, weights, out):
    x_tok = x.rearrange("b (u h) w c -> (b u) (h w) c", u=TILES)
    out_tok = out.rearrange("b (u h) w c -> (b u) (h w) c", u=TILES)

    with ExitStack() as ctx:
        def sb(name, shape, dt=F32):
            return ctx.enter_context(nc.sbuf_tensor(name, shape, dt))

        tab = sb("tab", [P, TABLE_W])

        def w(name):
            first, width = AT[name]
            return tab[:, first:first + width]

        def col(name):
            n = AT["columns"][0] + COLUMNS.index(name)
            return tab[:, n:n + 1]

        ident = w("ident")
        ident16 = sb("ident16", [P, P], BF16)
        w0s = sb("w0s", [P, C])
        wvo = sb("wvo", [P, C])
        w2qs = sb("w2qs", [P, C])
        mlp_half = sb("mlp_half", [P, 2, 3 * P])
        mlp_a = sb("mlp_a", [P, 3, P])
        mlp_b = sb("mlp_b", [P, 3, P])
        fold1 = sb("fold1", [P, 2, P])
        fold2 = sb("fold2", [P, 2, P])
        fold2t = sb("fold2t", [P, P])
        cas_out = sb("cas_out", [P, P])
        bq_s, bo0_s, bo1_f, c_t0, c_t1, c_low, c_high = (
            sb(n, [P, 1]) for n in ("bq_s", "bo0_s", "bo1_f", "c_t0", "c_t1", "c_low", "c_high"))
        half = sb("half", [P, 1])

        xin = sb("xin", [P, 2, TILES, C])
        x0T = sb("x0T", [P, TOK])
        pooled = sb("pooled", [P, POOLED])
        pg = sb("pg", [P, POOLED])
        thetaT = sb("thetaT", [P, TOK])
        nmax0, sum0, inv0 = (sb(n, [P, TILES]) for n in ("nmax0", "sum0", "inv0"))
        p0 = sb("p0", [P, TILES, POOLED])
        p0n = sb("p0n", [P, TILES, POOLED])
        p0T = sb("p0T", [P, TOK])
        gw = sb("gw", [P, C])
        x1T = [sb(f"x1T{p}", [P, TOK]) for p in range(2)]

        bn = [sb(f"bn{k}", [P, 6]) for k in (1, 2)]
        mv = [sb(f"mv{k}", [P, 2]) for k in (1, 2)]
        gst = [sb(f"gst{k}", [P, 2]) for k in (1, 2)]
        var, vare, rstd, gsc, gsh = ([sb(f"{n}{k}", [P, 1]) for k in (1, 2)]
                                     for n in ("var", "vare", "rstd", "gsc", "gsh"))

        xn1 = sb("xn1", [P, TOK])
        q1T, k1T = sb("q1T", [P, TOK]), sb("k1T", [P, TOK])
        v1 = sb("v1", [P, TILES, C])
        nmax1, sum1, inv1 = (sb(n, [P, TILES]) for n in ("nmax1", "sum1", "inv1"))
        p1 = sb("p1", [P, TILES, TOK])
        p1n = sb("p1n", [P, TILES, TOK])
        p1T = sb("p1T", [P, TILES, TOK])
        x2T = sb("x2T", [P, TOK])

        x2b = sb("x2b", [P, TOK])
        xn2 = sb("xn2", [P, TOK])
        x2tok = [sb(f"x2tok{p}", [P, TOK]) for p in range(2)]
        parts = sb("parts", [P, 2, PARTS, TOK], BF16)
        rest = sb("rest", [P, 2, TOK])
        stack = [sb(f"stack{p}", [P, HEADS, 2, TOK], BF16) for p in range(2)]
        vaug = [sb(f"vaug{p}", [P, TILES, HEADS, 32]) for p in range(2)]
        nmax = sb("nmax", [P, TILES, HEADS])
        nrest = sb("nrest", [P, TILES, HEADS])
        npart = sb("npart", [P, TILES, PARTS, HEADS], BF16)
        nmaxT = sb("nmaxT", [P, TOK], BF16)
        pT = sb("pT", [P, HEADS, TILES, TOK])
        oT = sb("oT", [P, 2, TOK])
        oinv = sb("oinv", [P, TILES, HEADS])
        on = sb("on", [P, TILES, HEADS, HD])
        onT = sb("onT", [P, TOK])
        x3 = sb("x3", [P, TOK])

        zE = sb("zE", [P, HE, WE])
        o1k = sb("o1k", [P, TOK])
        o1nE = sb("o1nE", [P, HE, WE])
        yhigh = sb("yhigh", [P, TOK])
        yneg = sb("yneg", [P, TOK])
        s3 = sb("s3", [P, TILES, C])
        xout = sb("xout", [P, TOK])

        banks = [ctx.enter_context(nc.psum_tensor(f"bank{n}", [P, 512], F32)) for n in range(8)]
        proj_ps = s1_ps = banks[0]
        s0_ps = p0T_ps = pv_ps = v3_ps = out_ps = banks[1]
        v1_ps = o2_ps = banks[2]
        p1T_ps = o1_ps = qk2_ps = xv2_ps = oTT_ps = banks[3]
        a_ps = y_ps = banks[4]
        gm2_ps = qk1_ps = banks[5]
        x0T_ps = gm1_ps = nmT_ps = onT_ps = z_ps = banks[6]
        o0_ps = gw_ps = banks[7]
        smax_ps = [banks[n] for n in (4, 3, 7, 4, 7, 5, 7, 4)]
        sT_ps = [banks[n] for n in (2, 1, 5, 0, 5, 6, 0, 2)]
        fold_ps0, fold_ps1, fold_ps2 = banks[4][:, 0:P + 1], banks[4][:, P + 1:3 * P + 1], banks[3]

        produced = dict(
            sync="""tab0_in tab1_in tab2_in tab3_in x_in0 x_in1 stack_in0 stack_in1 neg_in out_st""",
            pool="""pool_setup sums_rd rstd1_rd rstd2_rd x2b_rd part2_rd""",
            pe="""fold_pe x0T_pe proj_pe s0_pe p0T_pe o0_pe gn1_pe gn2_pe qk1_pe v1_pe s1_pe p1T_pe o1_pe
                xv2_pe qk2_pe smax_pe nmT_pe sT_pe pv_pe oTT_pe onT_pe o2_pe z_pe a_pe y_pe v3_pe out_pe""",
            act="""act_setup x0T_rd theta_rd gw_rd exp0_rd p0T_rd qk1_rd v1_rd exp1_rd p1T_rd part0_rd xv_rd nmT_rd
                exp_rd oT_rd onT_rd z_rd o1_rd yhigh_rd v3_rd""",
            dve="""dve_setup pool_rd pg_rd nmax0_rd inv0_rd p0n_rd x1_rd bn1_rd bn2_rd mv1_rd mv2_rd
                st1_rd st2_rd gst1_rd gst2_rd var1_rd var2_rd vare1_rd vare2_rd gsc1_rd gsc2_rd
                gsh1_rd gsh2_rd xn1_rd xn2_rd nmax1_rd inv1_rd p1n_rd x2_rd rest_rd part1_rd nmax_rd
                nb0_rd nr0_rd nb1_rd npart_rd oinv_rd on_rd x3_rd zE_rd y_rd out_rd""",
        )
        s = {n: ctx.enter_context(nc.semaphore(n)) for names in produced.values() for n in names.split()}
        block = ctx.enter_context(nc.Block())

        def start(engine, who):
            for name in produced[who].split():
                engine.sem_inc(s[name], START)

        def count(i, per=1, k=None):
            if isinstance(i, int):
                if i < 0:
                    return START
                i = min(i, IMAGES - 1)
            return i * per + (START + (per if k is None else k))

        def count_half(i, p, per=16):
            return START if isinstance(i, int) and i < 0 else (i - p) * (per // 2) + (START + per)

        def stand_apart(engine, *values):
            for value in values:
                if not isinstance(value, int):
                    engine.lower_val(value)
            engine.wait_ge(s["tab0_in"], START + 16)

        def first_is(n, k):
            return isinstance(n, int) and n == k

        def steps(engine, step):
            first, turns = DEPTH - 1, (IMAGES - (DEPTH - 1)) // 2

            def live(n):
                return {k for k in range(DEPTH) if 0 <= n - k < IMAGES}

            for n in range(first):
                step(n, n % 2, live(n))
            with engine.Fori(0, turns) as turn:
                for k in range(2):
                    step(turn * 2 + (first + k), (first + k) % 2, set(range(DEPTH)))
            for n in range(first + 2 * turns, IMAGES + DEPTH - 1):
                step(n, n % 2, live(n))

        STACKS = 16 * len(PAIRS)

        fills = ((thetaT[32:64, :], 0.0), (half[:, :], -0.5),
                 (vaug[0][:, :, :, HD:32], 0.0), (vaug[1][:, :, :, HD:32], 0.0),
                 (vaug[0][:, :, :, HD:HD + 1], 1.0), (vaug[1][:, :, :, HD:HD + 1], 1.0),
                 (stack[0][ROWS:AUG, :, 1, :], 1.0), (stack[1][ROWS:AUG, :, 1, :], 1.0))

        @block.sync
        def _(sp):
            start(sp, "sync")

            def load_x(i, p):
                sp.dma_start(xin[:, p, :, :], x_tok[bass.ds(i * TILES, TILES)].rearrange("u p c -> p u c")
                             ).then_inc(s[f"x_in{p}"], 16)

            def load_later_x(i, p):
                value = count(i - 2)
                stand_apart(sp, value)
                sp.wait_ge(s["x0T_pe"], value)
                load_x(i, p)

            def load_table(group):
                first = AT[LAYOUT[group][0][0]][0]
                width = sum(n for _, n in LAYOUT[group])
                sp.dma_start(tab[:, first:first + width], weights[:, first:first + width]
                             ).then_inc(s[f"tab{group}_in"], 16)

            def spread(i, p, pairs):
                whole, parts_rd = max(PAIRS[pairs[0]]), ("part0_rd", "part1_rd", "part2_rd")
                values = count(i), count(i - 2, HEADS)
                stand_apart(sp, *values)
                sp.wait_ge(s[parts_rd[whole]], values[0])
                if pairs[0] == 0:
                    sp.wait_ge(s["sT_pe"], values[1])
                for g in pairs:
                    a, b = PAIRS[g]
                    slots = parts[:, :, :, :].rearrange("p w a t -> p (w a) t")
                    sp.dma_start(stack[p][g * HD:(g + 1) * HD, :, :, :], slots[:, a:PARTS + b + 1:PARTS + b - a, :]
                                 ).then_inc(s[f"stack_in{p}"], 16)

            def spread_maxima(i, p):
                value = count(i)
                stand_apart(sp, value)
                sp.wait_ge(s["nmT_rd"], value)
                sp.dma_start(stack[p][ROWS:AUG, :, 0, :], nmaxT[0:PARTS * HEADS, :]).then_inc(s["neg_in"], 16)

            def store(i):
                value = count(i)
                stand_apart(sp, value)
                sp.wait_ge(s["out_rd"], value)
                sp.dma_start(out_tok[bass.ds(i * TILES, TILES)].rearrange("u p c -> p u c"),
                             xout[:, :].rearrange("p (u c) -> p u c", u=TILES)).then_inc(s["out_st"], 16)

            def step(n, p, live):
                q = 1 - p
                if 0 in live and not (isinstance(n, int) and n < 2): load_later_x(n, p)
                if 3 in live: spread_maxima(n - 3, q)
                if 2 in live: spread(n - 2, p, (0,))
                if 2 in live: spread(n - 2, p, (1, 2, 3))
                if 2 in live: spread(n - 2, p, (4, 5))
                if 4 in live: store(n - 4)

            load_x(0, 0)
            load_table(0)
            load_table(1)
            load_x(1, 1)
            load_table(2)
            load_table(3)
            steps(sp, step)
            sp.wait_ge(s["out_st"], count(IMAGES - 1, 16))

        @block.gpsimd
        def _(pool):
            start(pool, "pool")
            for n, (tile, value) in enumerate(fills):
                nc.gpsimd.memset(tile, value).then_inc(s["pool_setup"], 1)
                pool.wait_ge(s["pool_setup"], START + n + 1)

            def mlp_sums():
                pool.wait_ge(s["dve_setup"], START + 2)
                nc.gpsimd.tensor_tensor(mlp_a[:, :, :].rearrange("p m n -> p (m n)"), mlp_half[:, 0, :],
                                        mlp_half[:, 1, :], ALU.add).then_inc(s["sums_rd"], 1)
                nc.gpsimd.tensor_tensor(mlp_b[:, :, :].rearrange("p m n -> p (m n)"), mlp_half[:, 0, :],
                                        mlp_half[:, 1, :], ALU.subtract).then_inc(s["sums_rd"], 1)

            def deviation_inverse(i, layer):
                pool.wait_ge(s[f"vare{layer}_rd"], count(i))
                pool.wait_ge(s[f"gsc{layer}_rd"], count(i - 1))
                nc.gpsimd.tensor_tensor(rstd[layer - 1][:, :], vare[layer - 1][:, :], half[:, :], ALU.pow
                                        ).then_inc(s[f"rstd{layer}_rd"], 1)

            def add_out_bias(i):
                pool.wait_ge(s["x2_rd"], count(i))
                pool.wait_ge(s["xv2_pe"], count(i - 1))
                nc.gpsimd.tensor_tensor(x2b[:, :], x2T[:, :], col("L2_conv_b_out").to_broadcast((P, TOK)), ALU.add
                                        ).then_inc(s["x2b_rd"], 1)

            def part2(i):
                pool.wait_ge(s["part1_rd"], count(i))
                nc.gpsimd.tensor_tensor(parts[:, :, 2, :], rest[:, :, :], parts[:, :, 1, :], ALU.subtract
                                        ).then_inc(s["part2_rd"], 1)

            def step(n, p, live):
                q = 1 - p
                if 2 in live: deviation_inverse(n - 2, 2)
                if 2 in live: add_out_bias(n - 2)
                if 2 in live: part2(n - 2)
                if 0 in live: deviation_inverse(n, 1)

            mlp_sums()
            steps(pool, step)

        @block.tensor
        def _(pe):
            start(pe, "pe")
            mm, tr = nc.tensor.matmul, nc.tensor.transpose
            pe.wait_ge(s["tab0_in"], START + 16)

            def fold_weights1():
                pe.wait_ge(s["tab1_in"], START + 16)
                mm(fold_ps0[:, 0:C], w("w1_vT"), w("w1_o"), start=True, stop=True)
                mm(fold_ps0[:, C:C + 1], w("w1_o"), col("L1_conv_bv"), start=True, stop=True).then_inc(s["fold_pe"], 1)

            def fold_weights2():
                pe.wait_ge(s["sums_rd"], START + 2)
                pe.wait_ge(s["dve_setup"], START + 3)
                for m, blk in enumerate((mlp_a, mlp_b)):
                    mm(fold_ps1[:, m * P:(m + 1) * P], w("cas_c"), blk[:, 0, :], start=True, stop=True)
                for m, blkT in enumerate((mlp_a, mlp_b)):
                    mm(fold_ps2[:, m * P:(m + 1) * P], blkT[:, 2, :], mlp_b[:, 1, :], start=True, stop=True)
                mm(fold_ps2[:, 2 * P:2 * P + 1], mlp_b[:, 1, :], col("b2_0"), start=True, stop=True
                   ).then_inc(s["fold_pe"], 1)

            def x_transposed(i, p):
                pe.wait_ge(s[f"x_in{p}"], count_half(i, p))
                pe.wait_ge(s["exp_rd"], count(i - 4, 8, 6))
                if isinstance(i, int):
                    pe.wait_ge(s["gst1_rd"], count(i - 1))
                tr(x0T_ps[:, 0:P], xin[:, p, 0, :], ident)
                tr(x0T_ps[:, P:2 * P], xin[:, p, 1, :], ident).then_inc(s["x0T_pe"], 1)

            def project0(i):
                pe.wait_ge(s["x0T_rd"], count(i))
                pe.wait_ge(s["exp_rd"], count(i - 4, 8, 7))
                if isinstance(i, int):
                    pe.wait_ge(s["exp_rd"], count(i - 4, 8, 4))
                    pe.wait_ge(s["exp1_rd"], count(i - 2))
                    pe.wait_ge(s["theta_rd"], count(i - 1))
                mm(proj_ps[:, 0:TOK], w("w0"), x0T[:, :], start=True, stop=True).then_inc(s["proj_pe"], 1)

            def scores0(i):
                if first_is(i, 0):
                    pe.wait_ge(s["dve_setup"], START + 1)
                    pe.wait_ge(s["pool_setup"], START + 1)
                pe.wait_ge(s["theta_rd"], count(i))
                pe.wait_ge(s["pg_rd"], count(i))
                pe.wait_ge(s["oT_rd"], count(i - 4))
                if isinstance(i, int):
                    pe.wait_ge(s["out_rd"], count(i - 5))
                    pe.wait_ge(s["v3_rd"], count(i - 5))
                    pe.wait_ge(s["exp_rd"], count(i - 4, 8, 2))
                    pe.wait_ge(s["p0T_rd"], count(i - 1))
                pe.wait_ge(s["nmax_rd"], count(i - 3, 8, 7))
                if isinstance(i, int):
                    pe.wait_ge(s["nmax_rd"], count(i - 3, 8, 5))
                    pe.wait_ge(s["nmax_rd"], count(i - 3, 8, 3))
                    pe.wait_ge(s["x1_rd"], count(i - 1))
                for u in range(TILES):
                    mm(s0_ps[:, u * POOLED:(u + 1) * POOLED], thetaT[0:64, u * P:(u + 1) * P], pg[0:64, :],
                       start=True, stop=True)
                mm(gw_ps[0:POOLED, 0:C], pg[64:128, :], w0s[64:128, :], start=True, stop=True).then_inc(s["s0_pe"], 1)

            def p0_transposed(i):
                values = count(i), count(i)
                stand_apart(pe, *values)
                pe.wait_ge(s["p0n_rd"], values[0])
                pe.wait_ge(s["exp0_rd"], values[1])
                for u in range(TILES):
                    last = tr(p0T_ps[0:POOLED, u * P:(u + 1) * P], p0n[:, u, :], ident)
                last.then_inc(s["p0T_pe"], 1)

            def attend0(i):
                pe.wait_ge(s["p0T_rd"], count(i))
                pe.wait_ge(s["gw_rd"], count(i))
                pe.wait_ge(s["gw_rd"], count(i))
                mm(o0_ps[:, 0:TOK], gw[0:POOLED, :], p0T[0:POOLED, :], start=True, stop=True).then_inc(s["o0_pe"], 1)

            def group_means1(i):
                pe.wait_ge(s["st1_rd"], count(i))
                pe.wait_ge(s["z_rd"], count(i - 4))
                if isinstance(i, int):
                    pe.wait_ge(s["nmT_rd"], count(i - 3))
                    pe.wait_ge(s["onT_rd"], count(i - 4))
                    pe.wait_ge(s["x0T_rd"], count(i))
                mm(gm1_ps[:, 0:2], w("mean1"), mv[0][:, :], start=True, stop=True).then_inc(s["gn1_pe"], 1)

            def group_means2(i):
                pe.wait_ge(s["st2_rd"], count(i))
                pe.wait_ge(s["exp_rd"], count(i - 2, 8, 5))
                if isinstance(i, int):
                    pe.wait_ge(s["exp_rd"], count(i - 2, 8, 3))
                    pe.wait_ge(s["qk1_rd"], count(i))
                mm(gm2_ps[:, 0:2], w("mean2"), mv[1][:, :], start=True, stop=True).then_inc(s["gn2_pe"], 1)

            def project1(i):
                pe.wait_ge(s["xn1_rd"], count(i))
                pe.wait_ge(s["nmax_rd"], count(i - 2, 8, 6))
                if isinstance(i, int):
                    pe.wait_ge(s["gst2_rd"], count(i - 1))
                mm(qk1_ps[:, 0:TOK], w("w1_q"), xn1[:, :], start=True, stop=True)
                mm(qk1_ps[:, TOK:2 * TOK], w("w1_k"), xn1[:, :], start=True, stop=True).then_inc(s["qk1_pe"], 1)

            def values1(i):
                if first_is(i, 0):
                    pe.wait_ge(s["dve_setup"], START + 3)
                pe.wait_ge(s["xn1_rd"], count(i))
                pe.wait_ge(s["x3_rd"], count(i - 3))
                if isinstance(i, int):
                    pe.wait_ge(s["exp_rd"], count(i - 3, 8, 8))
                    pe.wait_ge(s["exp_rd"], count(i - 3, 8, 1))
                    pe.wait_ge(s["v1_rd"], count(i - 1))
                for u in range(TILES):
                    last = mm(v1_ps[:, u * C:(u + 1) * C], xn1[:, u * P:(u + 1) * P], wvo[:, :], start=True, stop=True)
                last.then_inc(s["v1_pe"], 1)

            def scores1(i):
                pe.wait_ge(s["qk1_rd"], count(i))
                pe.wait_ge(s["theta_rd"], count(i + 1))
                if isinstance(i, int):
                    pe.wait_ge(s["exp_rd"], count(i - 3, 8, 7))
                for u in range(TILES):
                    last = mm(s1_ps[:, u * TOK:(u + 1) * TOK], q1T[:, u * P:(u + 1) * P], k1T[:, :], start=True, stop=True)
                last.then_inc(s["s1_pe"], 1)

            def p1_transposed(i):
                pe.wait_ge(s["p1n_rd"], count(i))
                pe.wait_ge(s["xv_rd"], count(i - 1))
                for u in range(TILES):
                    for m in range(TILES):
                        last = tr(p1T_ps[:, m * TOK + u * P:m * TOK + (u + 1) * P], p1n[:, u, m * P:(m + 1) * P], ident)
                last.then_inc(s["p1T_pe"], 1)

            def attend1(i):
                pe.wait_ge(s["v1_rd"], count(i))
                pe.wait_ge(s["p1T_rd"], count(i))
                pe.wait_ge(s["p1T_rd"], count(i))
                for m in range(TILES):
                    last = mm(o1_ps[:, 0:TOK], v1[:, m, :], p1T[:, m, :], start=(m == 0), stop=(m == TILES - 1))
                last.then_inc(s["o1_pe"], 1)

            def project2(i):
                if first_is(i, 0):
                    pe.wait_ge(s["dve_setup"], START + 4)
                pe.wait_ge(s["xn2_rd"], count(i))
                pe.wait_ge(s["on_rd"], count(i - 2))
                if isinstance(i, int):
                    pe.wait_ge(s["nmax_rd"], count(i - 1, 8, 2))
                    pe.wait_ge(s["x2_rd"], count(i))
                mm(qk2_ps[:, 0:TOK], w2qs[:, :], xn2[:, :], start=True, stop=True)
                mm(qk2_ps[:, TOK:2 * TOK], w("w2_k"), xn2[:, :], start=True, stop=True).then_inc(s["qk2_pe"], 1)

            def values2(i):
                pe.wait_ge(s["x2b_rd"], count(i))
                pe.wait_ge(s["xn2_rd"], count(i))
                pe.wait_ge(s["rest_rd"], count(i))
                for u in range(TILES):
                    tr(xv2_ps[:, u * P:(u + 1) * P], x2b[:, u * P:(u + 1) * P], ident)
                for u in range(TILES):
                    last = mm(xv2_ps[:, TOK + u * C:TOK + (u + 1) * C], xn2[:, u * P:(u + 1) * P], w("w2_v"),
                              start=True, stop=True)
                last.then_inc(s["xv2_pe"], 1)

            def scores_by_query(i, p, h):
                if h == 0:
                    pe.wait_ge(s[f"stack_in{p}"], count_half(i, p, STACKS))
                if h == 0:
                    pe.wait_ge(s["y_rd"], count(i - 2))
                    if isinstance(i, int):
                        pe.wait_ge(s["o1_rd"], count(i - 2))
                        pe.wait_ge(s["nmax_rd"], count(i - 1, 8, 8))
                if h == 1:
                    pe.wait_ge(s["x2_rd"], count(i + 1))
                    if isinstance(i, int):
                        pe.wait_ge(s["p1T_rd"], count(i + 1))
                        pe.wait_ge(s["xv_rd"], count(i))
                if h == 2:
                    pe.wait_ge(s["x1_rd"], count(i + 2))
                    if isinstance(i, int):
                        pe.wait_ge(s["gw_rd"], count(i + 2))
                        pe.wait_ge(s["nmax_rd"], count(i - 1, 8, 7))
                if h == 3:
                    pe.wait_ge(s["nmax_rd"], count(i, 8, 1))
                if h == 4:
                    pe.wait_ge(s["nmax_rd"], count(i, 8, 3))
                if h == 5:
                    pe.wait_ge(s["gst2_rd"], count(i + 1))
                    if isinstance(i, int):
                        pe.wait_ge(s["exp_rd"], count(i - 1, 8, 5))
                if h == 6:
                    pe.wait_ge(s["nmax_rd"], count(i, 8, 5))
                if h == 7:
                    pe.wait_ge(s["nmax_rd"], count(i, 8, 4))
                for u in range(TILES):
                    last = mm(smax_ps[h][:, u * TOK:(u + 1) * TOK], stack[p][0:ROWS, h, 0, u * P:(u + 1) * P],
                              stack[p][0:ROWS, h, 1, :], start=True, stop=True)
                last.then_inc(s["smax_pe"], 1)

            def maxima_transposed(i):
                pe.wait_ge(s["onT_rd"], count(i - 1))
                if isinstance(i, int):
                    pe.wait_ge(s["x0T_rd"], count(i + 3))
                if first_is(i, 0):
                    pe.wait_ge(s["act_setup"], START + 1)
                pe.wait_ge(s["npart_rd"], count(i))
                turned = nmT_ps[:, :].bitcast(BF16)
                for u in range(TILES):
                    last = tr(turned[0:PARTS * HEADS, u * P:(u + 1) * P],
                              npart[:, u, :, :].rearrange("p a h -> p (a h)"), ident16[:, :])
                last.then_inc(s["nmT_pe"], 1)

            def scores_by_key(i, p, h):
                if h == 0:
                    if first_is(i, 0):
                        pe.wait_ge(s["pool_setup"], START + len(fills))
                    pe.wait_ge(s["neg_in"], count(i, 16))
                if h == 0:
                    pe.wait_ge(s["v1_rd"], count(i + 2))
                    if isinstance(i, int):
                        pe.wait_ge(s["x3_rd"], count(i - 1))
                if h == 1:
                    pe.wait_ge(s["p0T_rd"], count(i + 3))
                    if isinstance(i, int):
                        pe.wait_ge(s["exp0_rd"], count(i + 3))
                        pe.wait_ge(s["oT_rd"], count(i - 1))
                if h == 2:
                    pe.wait_ge(s["qk1_rd"], count(i + 2))
                    if isinstance(i, int):
                        pe.wait_ge(s["nmax_rd"], count(i, 8, 6))
                if h == 3:
                    pe.wait_ge(s["exp1_rd"], count(i + 2))
                    if isinstance(i, int):
                        pe.wait_ge(s["theta_rd"], count(i + 3))
                        pe.wait_ge(s["exp_rd"], count(i - 1, 8, 7))
                if h == 4:
                    pe.wait_ge(s["exp_rd"], count(i, 8, 3))
                if h == 5:
                    pe.wait_ge(s["gst1_rd"], count(i + 3))
                    if isinstance(i, int):
                        pe.wait_ge(s["z_rd"], count(i - 1))
                if h == 6:
                    pe.wait_ge(s["exp_rd"], count(i, 8, 4))
                if h == 7:
                    pe.wait_ge(s["exp_rd"], count(i, 8, 1))
                for m in range(TILES):
                    last = mm(sT_ps[h][:, m * TOK:(m + 1) * TOK], stack[p][0:AUG, h, 1, m * P:(m + 1) * P],
                              stack[p][0:AUG, h, 0, :], start=True, stop=True)
                last.then_inc(s["sT_pe"], 1)

            def attend2(i, p, g):
                pe.wait_ge(s["exp_rd"], count(i, HEADS, 4 * g + 4))
                if g == 0:
                    pe.wait_ge(s["xv_rd"], count(i))
                pe.wait_ge(s["out_rd"], count(i - 1))
                if isinstance(i, int):
                    pe.wait_ge(s["v3_rd"], count(i - 1))
                    pe.wait_ge(s["exp_rd"], count(i, 8, 2))
                for m in range(TILES):
                    for j in range(4):
                        last = mm(pv_ps[32 * j:32 * j + 32, g * TOK:(g + 1) * TOK], vaug[p][:, m, 4 * g + j, :],
                                  pT[:, 4 * g + j, m, :], start=(m == 0), stop=(m == TILES - 1))
                last.then_inc(s["pv_pe"], 1)

            def o_back(i):
                pe.wait_ge(s["oT_rd"], count(i))
                pe.wait_ge(s["nmax_rd"], count(i + 1, 8, 2))
                if isinstance(i, int):
                    pe.wait_ge(s["x2_rd"], count(i + 2))
                    pe.wait_ge(s["p1T_rd"], count(i + 2))
                    pe.wait_ge(s["xv_rd"], count(i + 1))
                    pe.wait_ge(s["rest_rd"], count(i + 1))
                    pe.wait_ge(s["on_rd"], count(i - 1))
                for u in range(TILES):
                    for g in range(2):
                        last = tr(oTT_ps[:, (2 * u + g) * P:(2 * u + g + 1) * P], oT[:, g, u * P:(u + 1) * P], ident)
                last.then_inc(s["oTT_pe"], 1)

            def on_transposed(i):
                pe.wait_ge(s["on_rd"], count(i))
                pe.wait_ge(s["x0T_rd"], count(i + 4))
                if isinstance(i, int):
                    pe.wait_ge(s["exp_rd"], count(i, 8, 6))
                for u in range(TILES):
                    last = tr(onT_ps[:, u * P:(u + 1) * P], on[:, u, :, :].rearrange("p h d -> p (h d)"), ident)
                last.then_inc(s["onT_pe"], 1)

            def project_out(i):
                pe.wait_ge(s["onT_rd"], count(i))
                pe.wait_ge(s["exp_rd"], count(i, 8, 8))
                for u in range(TILES):
                    last = mm(o2_ps[:, u * C:(u + 1) * C], onT[:, u * P:(u + 1) * P], w("w2_o"), start=True, stop=True)
                last.then_inc(s["o2_pe"], 1)

            def transform_w(i):
                pe.wait_ge(s["x3_rd"], count(i))
                pe.wait_ge(s["nmT_rd"], count(i + 1))
                if isinstance(i, int):
                    pe.wait_ge(s["onT_rd"], count(i))
                n = P // W * WE
                for u in range(TILES):
                    last = mm(z_ps[:, u * n:(u + 1) * n], x3[:, u * C:(u + 1) * C], w("cas_we"), start=True, stop=True)
                last.then_inc(s["z_pe"], 1)

            def hidden(i):
                if first_is(i, 0):
                    pe.wait_ge(s["dve_setup"], START + 7)
                pe.wait_ge(s["zE_rd"], count(i))
                pe.wait_ge(s["nmax_rd"], count(i + 1, 8, 8))
                if isinstance(i, int):
                    pe.wait_ge(s["nmax_rd"], count(i + 1, 8, 4))
                    pe.wait_ge(s["nmax_rd"], count(i + 1, 8, 1))
                    pe.wait_ge(s["y_rd"], count(i - 1))
                both = a_ps[:, 0:EXT].rearrange("p (h w) -> p h w", h=HE)
                mm(both, fold1[:, 0, :], zE[:, :, :], start=True, stop=False)
                mm(both, fold1[:, 1, :], zE[:, ::-1, ::-1], start=False, stop=True).then_inc(s["a_pe"], 1)

            def mlp_out(i):
                pe.wait_ge(s["o1_rd"], count(i))
                pe.wait_ge(s["o1_rd"], count(i))
                y = y_ps[:, 0:TOK].rearrange("p (h w) -> p h w", h=H)
                mm(y, fold2[:, 0, :], o1k[:, :].rearrange("p (h w) -> p h w", h=H), start=True, stop=False)
                mm(y, fold2[:, 1, :], o1nE[:, H:0:-1, W:0:-1], start=False, stop=True).then_inc(s["y_pe"], 1)

            def transform_c_back(i):
                pe.wait_ge(s["y_rd"], count(i))
                pe.wait_ge(s["exp_rd"], count(i + 1, 8, 2))
                if isinstance(i, int):
                    pe.wait_ge(s["p0T_rd"], count(i + 4))
                    pe.wait_ge(s["exp0_rd"], count(i + 4))
                    pe.wait_ge(s["oT_rd"], count(i))
                for u in range(TILES):
                    last = mm(v3_ps[:, u * C:(u + 1) * C], yneg[:, u * P:(u + 1) * P], cas_out[:, :], start=True, stop=True)
                last.then_inc(s["v3_pe"], 1)

            def transform_w_back(i):
                pe.wait_ge(s["v3_rd"], count(i))
                pe.wait_ge(s["v3_rd"], count(i))
                mm(out_ps[:, 0:TOK], w("cas_w"), s3[:, :, :].rearrange("p u c -> p (u c)"), start=True, stop=True
                   ).then_inc(s["out_pe"], 1)

            def step(n, p, live):
                q = 1 - p
                if 3 in live: scores_by_query(n - 3, q, 4)
                if 3 in live: scores_by_query(n - 3, q, 5)
                if 4 in live: attend2(n - 4, p, 1)
                if 3 in live: scores_by_query(n - 3, q, 6)
                if 0 in live: x_transposed(n, p)
                if 3 in live: scores_by_query(n - 3, q, 7)
                if 4 in live: o_back(n - 4)
                if 0 in live: project0(n)
                if 1 in live: project1(n - 1)
                if 4 in live: on_transposed(n - 4)
                if 2 in live: project2(n - 2)
                if 4 in live: project_out(n - 4)
                if 0 in live: scores0(n)
                if first_is(n, 0): fold_weights1()
                if 3 in live: maxima_transposed(n - 3)
                if 1 in live: scores1(n - 1)
                if 4 in live: transform_w(n - 4)
                if 1 in live: values1(n - 1)
                if 2 in live: values2(n - 2)
                if 0 in live: p0_transposed(n)
                if 4 in live: hidden(n - 4)
                if first_is(n, 1): pe.wait_ge(s["dve_setup"], START + 5)
                if 1 in live: p1_transposed(n - 1)
                if 0 in live: attend0(n)
                if 3 in live: scores_by_key(n - 3, q, 0)
                if 3 in live: scores_by_key(n - 3, q, 1)
                if 4 in live: mlp_out(n - 4)
                if 1 in live: attend1(n - 1)
                if 3 in live: scores_by_key(n - 3, q, 2)
                if 3 in live: scores_by_key(n - 3, q, 3)
                if 4 in live: transform_c_back(n - 4)
                if 0 in live: group_means1(n)
                if 2 in live: scores_by_query(n - 2, p, 0)
                if 3 in live: scores_by_key(n - 3, q, 4)
                if 4 in live: transform_w_back(n - 4)
                if 3 in live: scores_by_key(n - 3, q, 5)
                if 3 in live: scores_by_key(n - 3, q, 6)
                if 2 in live: scores_by_query(n - 2, p, 1)
                if 3 in live: scores_by_key(n - 3, q, 7)
                if 2 in live: scores_by_query(n - 2, p, 2)
                if 1 in live: group_means2(n - 1)
                if 2 in live: scores_by_query(n - 2, p, 3)
                if 3 in live: attend2(n - 3, q, 0)
                if first_is(n, 0): fold_weights2()

            steps(pe, step)

        @block.scalar
        def _(act):
            start(act, "act")
            go, copy = nc.scalar.activation, nc.scalar.copy
            act.wait_ge(s["tab0_in"], START + 16)
            copy(ident16[:, :], ident)
            go(bq_s[:, :], col("L1_conv_bq"), ACT.Copy, scale=float(C) ** -0.5).then_inc(s["act_setup"], 1)

            def x0T_out(i):
                act.wait_ge(s["x0T_pe"], count(i))
                act.wait_ge(s["proj_pe"], count(i - 1))
                act.wait_ge(s["x1_rd"], count(i - 1))
                copy(x0T[:, :], x0T_ps[:, 0:TOK]).then_inc(s["x0T_rd"], 1)

            def theta_out(i):
                act.wait_ge(s["pool_rd"], count(i))
                act.wait_ge(s["s0_pe"], count(i - 1))
                go(thetaT[0:32, :], proj_ps[32:64, 0:TOK], ACT.Identity, bias=col("b_theta")[0:32, :]
                   ).then_inc(s["theta_rd"], 1)

            def gw_out(i):
                act.wait_ge(s["s0_pe"], count(i))
                act.wait_ge(s["o0_pe"], count(i - 1))
                copy(gw[0:POOLED, :], gw_ps[0:POOLED, 0:C]).then_inc(s["gw_rd"], 1)

            def exp0(i):
                act.wait_ge(s["nmax0_rd"], count(i))
                act.wait_ge(s["p0n_rd"], count(i - 1))
                for u in range(TILES):
                    last = go(p0[:, u, :], s0_ps[:, u * POOLED:(u + 1) * POOLED], ACT.Exp, bias=nmax0[:, u:u + 1],
                              accum_out=sum0[:, u:u + 1])
                last.then_inc(s["exp0_rd"], 1)

            def p0T_out(i):
                act.wait_ge(s["p0T_pe"], count(i))
                act.wait_ge(s["o0_pe"], count(i - 1))
                copy(p0T[0:POOLED, :], p0T_ps[0:POOLED, 0:TOK]).then_inc(s["p0T_rd"], 1)

            def qk1_out(i):
                if first_is(i, 0):
                    act.wait_ge(s["act_setup"], START + 1)
                act.wait_ge(s["qk1_pe"], count(i))
                act.wait_ge(s["s1_pe"], count(i - 1))
                go(q1T[:, :], qk1_ps[:, 0:TOK], ACT.Identity, bias=bq_s[:, :], scale=float(C) ** -0.5)
                go(k1T[:, :], qk1_ps[:, TOK:2 * TOK], ACT.Identity, bias=col("L1_conv_bk")).then_inc(s["qk1_rd"], 1)

            def v1_out(i):
                act.wait_ge(s["v1_pe"], count(i))
                act.wait_ge(s["o1_pe"], count(i - 1))
                copy(v1[:, :, :].rearrange("p u c -> p (u c)"), v1_ps[:, 0:TOK]).then_inc(s["v1_rd"], 1)

            def exp1(i):
                act.wait_ge(s["nmax1_rd"], count(i))
                act.wait_ge(s["p1n_rd"], count(i - 1))
                for u in range(TILES):
                    last = go(p1[:, u, :], s1_ps[:, u * TOK:(u + 1) * TOK], ACT.Exp, bias=nmax1[:, u:u + 1],
                              accum_out=sum1[:, u:u + 1])
                last.then_inc(s["exp1_rd"], 1)

            def p1T_out(i):
                act.wait_ge(s["p1T_pe"], count(i))
                act.wait_ge(s["o1_pe"], count(i - 1))
                copy(p1T[:, :, :].rearrange("p m t -> p (m t)"), p1T_ps[:, :]).then_inc(s["p1T_rd"], 1)

            def part0(i, p):
                act.wait_ge(s["qk2_pe"], count(i))
                act.wait_ge(s["rest_rd"], count(i - 1))
                act.wait_ge(s[f"stack_in{1 - p}"], count_half(i - 1, 1 - p, STACKS))
                copy(parts[:, :, 0, :], qk2_ps[:, :].rearrange("p (w t) -> p w t", w=2)).then_inc(s["part0_rd"], 1)

            def xv_out(i, p):
                act.wait_ge(s["xv2_pe"], count(i))
                act.wait_ge(s["x3_rd"], count(i - 2))
                act.wait_ge(s["pv_pe"], count(i - 2, 2))
                copy(x2tok[p][:, :], xv2_ps[:, 0:TOK])
                copy(vaug[p][:, :, :, 0:HD], xv2_ps[:, TOK:2 * TOK].rearrange("p (u h d) -> p u h d", u=TILES, h=HEADS)
                     ).then_inc(s["xv_rd"], 1)

            def maxima_out(i):
                act.wait_ge(s["nmT_pe"], count(i))
                act.wait_ge(s["neg_in"], count(i - 1, 16))
                copy(nmaxT[0:PARTS * HEADS, :], nmT_ps[:, :].bitcast(BF16)[0:PARTS * HEADS, 0:TOK]
                     ).then_inc(s["nmT_rd"], 1)

            def exp2(i, h):
                act.wait_ge(s["sT_pe"], count(i, HEADS, h + 1))
                if h == 0:
                    act.wait_ge(s["pv_pe"], count(i - 1, 2, 1))
                if h == 4:
                    act.wait_ge(s["pv_pe"], count(i - 1, 2, 2))
                go(pT[:, h, :, :].rearrange("p m t -> p (m t)"), sT_ps[h][:, :], ACT.Exp).then_inc(s["exp_rd"], 1)

            def oT_out(i):
                act.wait_ge(s["pv_pe"], count(i, 2))
                act.wait_ge(s["oTT_pe"], count(i - 1))
                copy(oT[:, :, :].rearrange("p g t -> p (g t)"), pv_ps[:, :]).then_inc(s["oT_rd"], 1)

            def onT_out(i):
                act.wait_ge(s["onT_pe"], count(i))
                act.wait_ge(s["o2_pe"], count(i - 1))
                copy(onT[:, :], onT_ps[:, 0:TOK]).then_inc(s["onT_rd"], 1)

            def z_out(i):
                act.wait_ge(s["z_pe"], count(i))
                act.wait_ge(s["a_pe"], count(i - 1))
                copy(zE[:, 0:H, :].rearrange("p h w -> p (h w)"), z_ps[:, 0:H * WE]).then_inc(s["z_rd"], 1)

            def o1_out(i):
                act.wait_ge(s["a_pe"], count(i))
                act.wait_ge(s["y_pe"], count(i - 1))
                go(o1k[:, :].rearrange("p (h w) -> p h w", h=H),
                   a_ps[:, 0:EXT].rearrange("p (h w) -> p h w", h=HE)[:, 0:H, 0:W], ACT.Relu, bias=col("b1_0"))
                go(o1nE[:, :, :].rearrange("p h w -> p (h w)"), a_ps[:, 0:EXT], ACT.Relu, bias=col("b1_1")
                   ).then_inc(s["o1_rd"], 1)

            def yhigh_out(i):
                act.wait_ge(s["y_pe"], count(i))
                act.wait_ge(s["y_rd"], count(i - 1))
                if first_is(i, 0):
                    act.wait_ge(s["dve_setup"], START + 7)
                go(yhigh[:, :], y_ps[:, 0:TOK], ACT.Relu, bias=c_low[:, :]).then_inc(s["yhigh_rd"], 1)

            def v3_out(i):
                act.wait_ge(s["v3_pe"], count(i))
                act.wait_ge(s["out_pe"], count(i - 1))
                copy(s3[:, :, :].rearrange("p u c -> p (u c)"), v3_ps[:, 0:TOK]).then_inc(s["v3_rd"], 1)

            def step(n, p, live):
                q = 1 - p
                if 4 in live: exp2(n - 4, 7)
                if 4 in live: oT_out(n - 4)
                if 0 in live: x0T_out(n)
                if 4 in live: onT_out(n - 4)
                if 0 in live: theta_out(n)
                if 1 in live: qk1_out(n - 1)
                if 2 in live: part0(n - 2, p)
                if 3 in live: maxima_out(n - 3)
                if 0 in live: exp0(n)
                if 4 in live: z_out(n - 4)
                if 1 in live: exp1(n - 1)
                if 0 in live: gw_out(n)
                if 2 in live: xv_out(n - 2, p)
                if 1 in live: v1_out(n - 1)
                if 0 in live: p0T_out(n)
                if 4 in live: o1_out(n - 4)
                if 1 in live: p1T_out(n - 1)
                if 3 in live: exp2(n - 3, 0)
                if 4 in live: yhigh_out(n - 4)
                if 3 in live: exp2(n - 3, 1)
                if 3 in live: exp2(n - 3, 2)
                if 4 in live: v3_out(n - 4)
                if 3 in live: exp2(n - 3, 3)
                if 3 in live: exp2(n - 3, 4)
                if 3 in live: exp2(n - 3, 5)
                if 3 in live: exp2(n - 3, 6)

            steps(act, step)

        @block.vector
        def _(dve):
            start(dve, "dve")
            v = nc.vector
            dve.wait_ge(s["tab0_in"], START + 16)
            v.tensor_scalar(bo0_s[:, :], col("L0_conv_b_o"), col("sigma"), None, ALU.mult)
            v.tensor_scalar(w0s[64:128, :], w("w0_o")[64:128, :], col("sigma")[64:128, :], None, ALU.mult
                            ).then_inc(s["dve_setup"], 1)

            def setup_values1():
                dve.wait_ge(s["fold_pe"], START + 1)
                v.tensor_scalar(bo1_f[:, :], fold_ps0[:, C:C + 1], col("L1_conv_bo"), None, ALU.add)
                v.tensor_copy(wvo[:, :], fold_ps0[:, 0:C]).then_inc(s["dve_setup"], 1)

            def setup_halves():
                dve.wait_ge(s["tab2_in"], START + 16)
                v.tensor_scalar(mlp_half[:, :, :].rearrange("p k n -> p (k n)"), w("mlp"), 0.5, None, ALU.mult
                                ).then_inc(s["dve_setup"], 1)

            def setup_scales():
                dve.wait_ge(s["tab3_in"], START + 16)
                v.tensor_scalar(w2qs[:, :], w("w2_q"), float(HD) ** -0.5, None, ALU.mult)
                v.tensor_scalar(cas_out[:, :], w("cas_c"), -1.0 / (W * C), None, ALU.mult).then_inc(s["dve_setup"], 1)

            def setup_layer3():
                dve.wait_ge(s["fold_pe"], START + 2)
                v.tensor_copy(fold1[:, :, :].rearrange("p m n -> p (m n)"), fold_ps1[:, 0:2 * P])
                v.scalar_tensor_tensor(out=fold2[:, 0, :], in0=mlp_a[:, 1, :], scalar=-1.0, in1=fold_ps2[:, 0:P],
                                       op0=ALU.mult, op1=ALU.subtract)
                v.scalar_tensor_tensor(out=fold2t[:, :], in0=mlp_a[:, 1, :], scalar=-1.0, in1=fold_ps2[:, P:2 * P],
                                       op0=ALU.mult, op1=ALU.subtract)
                v.tensor_scalar(c_t0[:, :], fold_ps2[:, 2 * P:2 * P + 1], col("b2_0"), None, ALU.add
                                ).then_inc(s["dve_setup"], 1)
                dve.wait_ge(s["dve_setup"], START + 5)
                v.tensor_tensor(fold2[:, 1, :], fold2t[:, :], mlp_b[:, 1, :], ALU.subtract)
                v.tensor_scalar(c_t1[:, :], c_t0[:, :], col("b2_1"), None, ALU.add).then_inc(s["dve_setup"], 1)
                dve.wait_ge(s["dve_setup"], START + 6)
                v.tensor_scalar(c_low[:, :], c_t1[:, :], -1.0, -SPARSITY, ALU.mult, ALU.add)
                v.tensor_scalar(c_high[:, :], c_t1[:, :], -1.0, SPARSITY, ALU.mult, ALU.add).then_inc(s["dve_setup"], 1)

            def pool_out(i):
                dve.wait_ge(s["proj_pe"], count(i))
                v.tensor_reduce(pooled[:, :], proj_ps[:, 0:TOK].rearrange("p (h a w b) -> p h w a b", h=H // 2, a=2, b=2),
                                AX.XY, ALU.max).then_inc(s["pool_rd"], 1)

            def pg_out(i):
                dve.wait_ge(s["pool_rd"], count(i))
                dve.wait_ge(s["s0_pe"], count(i - 1))
                v.tensor_scalar(pg[:, :], pooled[:, :], col("b_phi_g"), None, ALU.add).then_inc(s["pg_rd"], 1)

            def nmax0_out(i):
                dve.wait_ge(s["s0_pe"], count(i))
                dve.wait_ge(s["exp0_rd"], count(i - 1))
                v.tensor_reduce(nmax0[:, :], s0_ps[:, 0:TILES * POOLED].rearrange("p (u m) -> p u m", u=TILES),
                                AX.X, ALU.max, negate=True).then_inc(s["nmax0_rd"], 1)

            def inv0_out(i):
                dve.wait_ge(s["exp0_rd"], count(i))
                dve.wait_ge(s["p0n_rd"], count(i - 1))
                v.reciprocal(inv0[:, :], sum0[:, :]).then_inc(s["inv0_rd"], 1)

            def normalise_p0(i):
                dve.wait_ge(s["inv0_rd"], count(i))
                dve.wait_ge(s["p0T_pe"], count(i - 1))
                v.tensor_tensor(p0n[:, :, :], p0[:, :, :], inv0[:, :].unsqueeze(2).to_broadcast((P, TILES, POOLED)),
                                ALU.mult).then_inc(s["p0n_rd"], 1)

            def x1_out(i, p):
                dve.wait_ge(s["o0_pe"], count(i))
                dve.wait_ge(s["x0T_rd"], count(i))
                dve.wait_ge(s["x2_rd"], count(i - 2))
                v.scalar_tensor_tensor(out=x1T[p][:, :], in0=o0_ps[:, 0:TOK], scalar=bo0_s[:, :], in1=x0T[:, :],
                                       op0=ALU.add, op1=ALU.add).then_inc(s["x1_rd"], 1)

            def channel_statistics(i, layer, x):
                dve.wait_ge(s[f"x{layer}_rd"], count(i))
                dve.wait_ge(s[f"mv{layer}_rd"], count(i - 1))
                v.bn_stats(bn[layer - 1][:, :], x[:, :]).then_inc(s[f"bn{layer}_rd"], 1)

            def channel_mean(i, layer):
                values = count(i), count(i - 1)
                stand_apart(dve, *values)
                dve.wait_ge(s[f"bn{layer}_rd"], values[0])
                dve.wait_ge(s[f"gn{layer}_pe"], values[1])
                v.bn_aggr(mv[layer - 1][:, :], bn[layer - 1][:, :]).then_inc(s[f"mv{layer}_rd"], 1)

            def mean_square(i, layer):
                dve.wait_ge(s[f"mv{layer}_rd"], count(i))
                m = mv[layer - 1]
                v.scalar_tensor_tensor(out=m[:, 1:2], in0=m[:, 0:1], scalar=m[:, 0:1], in1=m[:, 1:2],
                                       op0=ALU.mult, op1=ALU.add).then_inc(s[f"st{layer}_rd"], 1)

            def group_statistics(i, layer):
                dve.wait_ge(s[f"gn{layer}_pe"], count(i))
                dve.wait_ge(s[f"gsh{layer}_rd"], count(i - 1))
                v.tensor_copy(gst[layer - 1][:, :], (gm1_ps, gm2_ps)[layer - 1][:, 0:2]).then_inc(s[f"gst{layer}_rd"], 1)

            def group_variance(i, layer):
                g = gst[layer - 1]
                dve.wait_ge(s[f"gst{layer}_rd"], count(i))
                dve.wait_ge(s[f"vare{layer}_rd"], count(i - 1))
                v.scalar_tensor_tensor(out=var[layer - 1][:, :], in0=g[:, 0:1], scalar=g[:, 0:1], in1=g[:, 1:2],
                                       op0=ALU.mult, op1=ALU.subtract, reverse1=True).then_inc(s[f"var{layer}_rd"], 1)

            def variance_guarded(i, layer):
                dve.wait_ge(s[f"var{layer}_rd"], count(i))
                dve.wait_ge(s[f"rstd{layer}_rd"], count(i - 1))
                v.tensor_scalar(vare[layer - 1][:, :], var[layer - 1][:, :], 0.0, (EPS1, EPS2)[layer - 1],
                                ALU.max, ALU.add).then_inc(s[f"vare{layer}_rd"], 1)

            def group_scale(i, layer):
                dve.wait_ge(s[f"rstd{layer}_rd"], count(i))
                dve.wait_ge(s[f"xn{layer}_rd"], count(i - 1))
                v.tensor_scalar(gsc[layer - 1][:, :], rstd[layer - 1][:, :],
                                col(("L1_conv_gn_gamma", "L2_conv_gn_scale")[layer - 1]), None, ALU.mult
                                ).then_inc(s[f"gsc{layer}_rd"], 1)

            def group_shift(i, layer):
                dve.wait_ge(s[f"gsc{layer}_rd"], count(i))
                dve.wait_ge(s[f"xn{layer}_rd"], count(i - 1))
                v.scalar_tensor_tensor(out=gsh[layer - 1][:, :], in0=gst[layer - 1][:, 0:1], scalar=gsc[layer - 1][:, :],
                                       in1=col(("L1_conv_gn_beta", "L2_conv_gn_bias")[layer - 1]),
                                       op0=ALU.mult, op1=ALU.subtract, reverse1=True).then_inc(s[f"gsh{layer}_rd"], 1)

            def normalised(i, layer, x, xn):
                dve.wait_ge(s[f"gsh{layer}_rd"], count(i))
                if layer == 1:
                    dve.wait_ge(s["qk1_pe"], count(i - 1))
                    dve.wait_ge(s["v1_pe"], count(i - 1))
                else:
                    dve.wait_ge(s["qk2_pe"], count(i - 1))
                    dve.wait_ge(s["xv2_pe"], count(i - 1))
                v.tensor_scalar(xn[:, :], x[:, :], gsc[layer - 1][:, :], gsh[layer - 1][:, :], ALU.mult, ALU.add
                                ).then_inc(s[f"xn{layer}_rd"], 1)

            def nmax1_out(i):
                dve.wait_ge(s["s1_pe"], count(i))
                dve.wait_ge(s["exp1_rd"], count(i - 1))
                v.tensor_reduce(nmax1[:, :], s1_ps[:, :].rearrange("p (u m) -> p u m", u=TILES), AX.X, ALU.max,
                                negate=True).then_inc(s["nmax1_rd"], 1)

            def inv1_out(i):
                dve.wait_ge(s["exp1_rd"], count(i))
                dve.wait_ge(s["p1n_rd"], count(i - 1))
                v.reciprocal(inv1[:, :], sum1[:, :]).then_inc(s["inv1_rd"], 1)

            def normalise_p1(i):
                dve.wait_ge(s["inv1_rd"], count(i))
                dve.wait_ge(s["p1T_pe"], count(i - 1))
                for u in range(TILES):
                    last = v.tensor_scalar(p1n[:, u, :], p1[:, u, :], inv1[:, u:u + 1], None, ALU.mult)
                last.then_inc(s["p1n_rd"], 1)

            def x2_out(i, p):
                dve.wait_ge(s["o1_pe"], count(i))
                dve.wait_ge(s["x2b_rd"], count(i - 1))
                dve.wait_ge(s["xn2_rd"], count(i - 1))
                v.scalar_tensor_tensor(out=x2T[:, :], in0=o1_ps[:, 0:TOK], scalar=bo1_f[:, :], in1=x1T[p][:, :],
                                       op0=ALU.add, op1=ALU.add).then_inc(s["x2_rd"], 1)

            def rest_out(i):
                dve.wait_ge(s["part0_rd"], count(i))
                dve.wait_ge(s["part2_rd"], count(i - 1))
                v.tensor_tensor(rest[:, :, :], qk2_ps[:, :].rearrange("p (w t) -> p w t", w=2), parts[:, :, 0, :],
                                ALU.subtract).then_inc(s["rest_rd"], 1)

            def part1(i):
                dve.wait_ge(s["rest_rd"], count(i))
                v.tensor_copy(parts[:, :, 1, :], rest[:, :, :]).then_inc(s["part1_rd"], 1)

            def nmax_out(i, h):
                dve.wait_ge(s["smax_pe"], count(i, HEADS, h + 1))
                if h == 0:
                    dve.wait_ge(s["npart_rd"], count(i - 1))
                v.tensor_reduce(nmax[:, :, h], smax_ps[h][:, :].rearrange("p (u m) -> p u m", u=TILES),
                                AX.X, ALU.max, negate=True).then_inc(s["nmax_rd"], 1)

            def split_maxima(i):
                dve.wait_ge(s["nmax_rd"], count(i, HEADS))
                dve.wait_ge(s["nmT_pe"], count(i - 1))
                v.tensor_copy(npart[:, :, 0, :], nmax[:, :, :]).then_inc(s["nb0_rd"], 1)
                dve.wait_ge(s["nb0_rd"], count(i))
                v.tensor_tensor(nrest[:, :, :], nmax[:, :, :], npart[:, :, 0, :], ALU.subtract).then_inc(s["nr0_rd"], 1)
                dve.wait_ge(s["nr0_rd"], count(i))
                v.tensor_copy(npart[:, :, 1, :], nrest[:, :, :]).then_inc(s["nb1_rd"], 1)
                dve.wait_ge(s["nb1_rd"], count(i))
                v.tensor_tensor(npart[:, :, 2, :], nrest[:, :, :], npart[:, :, 1, :], ALU.subtract
                                ).then_inc(s["npart_rd"], 1)

            def oinv_out(i):
                dve.wait_ge(s["oTT_pe"], count(i))
                dve.wait_ge(s["on_rd"], count(i - 1))
                v.reciprocal(oinv[:, :, :], oTT_ps[:, :].rearrange("p (u h d) -> p u h d", u=TILES, h=HEADS)[:, :, :, HD]
                             ).then_inc(s["oinv_rd"], 1)

            def normalise_o(i):
                dve.wait_ge(s["oinv_rd"], count(i))
                dve.wait_ge(s["onT_pe"], count(i - 1))
                v.tensor_tensor(on[:, :, :, :],
                                oTT_ps[:, :].rearrange("p (u h d) -> p u h d", u=TILES, h=HEADS)[:, :, :, 0:HD],
                                oinv[:, :, :].unsqueeze(3).to_broadcast((P, TILES, HEADS, HD)), ALU.mult
                                ).then_inc(s["on_rd"], 1)

            def x3_out(i, p):
                dve.wait_ge(s["o2_pe"], count(i))
                dve.wait_ge(s["xv_rd"], count(i))
                dve.wait_ge(s["z_pe"], count(i - 1))
                dve.wait_ge(s["out_rd"], count(i - 1))
                v.tensor_tensor(x3[:, :], o2_ps[:, 0:TOK], x2tok[p][:, :], ALU.add).then_inc(s["x3_rd"], 1)

            def wrap_z(i):
                dve.wait_ge(s["z_rd"], count(i))
                v.tensor_copy(zE[:, H, :], zE[:, 0, :]).then_inc(s["zE_rd"], 1)

            def y_out(i):
                dve.wait_ge(s["yhigh_rd"], count(i))
                dve.wait_ge(s["v3_pe"], count(i - 1))
                v.scalar_tensor_tensor(out=yneg[:, :], in0=y_ps[:, 0:TOK], scalar=c_high[:, :], in1=yhigh[:, :],
                                       op0=ALU.add, op1=ALU.min).then_inc(s["y_rd"], 1)

            def x_out(i):
                dve.wait_ge(s["out_pe"], count(i))
                dve.wait_ge(s["out_st"], count(i - 1, 16))
                v.tensor_tensor(xout[:, :], out_ps[:, 0:TOK], x3[:, :], ALU.add).then_inc(s["out_rd"], 1)

            def step(n, p, live):
                q = 1 - p
                if 3 in live: nmax_out(n - 3, 3)
                if 2 in live: group_variance(n - 2, 2)
                if 1 in live: group_shift(n - 1, 1)
                if 2 in live: variance_guarded(n - 2, 2)
                if 3 in live: nmax_out(n - 3, 4)
                if 1 in live: normalised(n - 1, 1, x1T[q], xn1)
                if 3 in live: nmax_out(n - 3, 5)
                if 2 in live: group_scale(n - 2, 2)
                if 3 in live: nmax_out(n - 3, 6)
                if 2 in live: group_shift(n - 2, 2)
                if 4 in live: oinv_out(n - 4)
                if 2 in live: normalised(n - 2, 2, x2T, xn2)
                if 4 in live: normalise_o(n - 4)
                if 0 in live: pool_out(n)
                if 3 in live: nmax_out(n - 3, 7)
                if 0 in live: pg_out(n)
                if first_is(n, 1): setup_layer3()
                if 3 in live: split_maxima(n - 3)
                if 4 in live: x3_out(n - 4, p)
                if 0 in live: nmax0_out(n)
                if first_is(n, 0): setup_halves()
                if 2 in live: rest_out(n - 2)
                if 1 in live: nmax1_out(n - 1)
                if 2 in live: part1(n - 2)
                if 0 in live: inv0_out(n)
                if 4 in live: wrap_z(n - 4)
                if 0 in live: normalise_p0(n)
                if first_is(n, 0): setup_values1()
                if 1 in live: inv1_out(n - 1)
                if 1 in live: normalise_p1(n - 1)
                if 0 in live: x1_out(n, p)
                if 0 in live: channel_statistics(n, 1, x1T[p])
                if 0 in live: channel_mean(n, 1)
                if 0 in live: mean_square(n, 1)
                if 4 in live: y_out(n - 4)
                if 1 in live: x2_out(n - 1, q)
                if 1 in live: channel_statistics(n - 1, 2, x2T)
                if 0 in live: group_statistics(n, 1)
                if 1 in live: channel_mean(n - 1, 2)
                if 0 in live: group_variance(n, 1)
                if 2 in live: nmax_out(n - 2, 0)
                if 4 in live: x_out(n - 4)
                if 0 in live: variance_guarded(n, 1)
                if first_is(n, 0): setup_scales()
                if 1 in live: mean_square(n - 1, 2)
                if 2 in live: nmax_out(n - 2, 1)
                if 1 in live: group_statistics(n - 1, 2)
                if 2 in live: nmax_out(n - 2, 2)
                if 0 in live: group_scale(n, 1)

            steps(dve, step)


def kernel(**inputs):
    import concourse.bacc as bacc
    from concourse.bass_utils import run_bass_kernel_spmd

    nc = bacc.Bacc("TRN2", target_bir_lowering=False, num_devices=1)
    inputs = {name: np.ascontiguousarray(a) for name, a in inputs.items()}
    arrays = {"in_x": inputs["x"], "in_weights": table(inputs)}
    x, weights = (nc.dram_tensor(name, a.shape, F32, kind="ExternalInput").ap() for name, a in arrays.items())
    out = nc.dram_tensor("out", (IMAGES, H, W, C), F32, kind="ExternalOutput").ap()
    build(nc, x, weights, out)
    got = run_bass_kernel_spmd(nc, [arrays], core_ids=[0])
    return got.results[0]["out"]
```

```python
from contextlib import ExitStack

import numpy as np

import concourse.bass as bass
from concourse import mybir

F32 = mybir.dt.float32
BF16 = mybir.dt.bfloat16
ALU = mybir.AluOpType
ACT = mybir.ActivationFunctionType
AX = mybir.AxisListType

IMAGES, H, W, C = 8, 16, 16, 128
P = 128
TOK = H * W
TILES = TOK // P
POOLED = TOK // 4
C8, C2 = C // 8, C // 2
HEADS, HD = 8, 16
HE, WE = H + 1, W + 1
EXT = HE * WE
PARTS = 3
PAIRS = ((0, 0), (1, 1), (0, 1), (1, 0), (0, 2), (2, 0))
ROWS = len(PAIRS) * HD
AUG = ROWS + PARTS
SPARSITY = 0.01
EPS1, EPS2 = 1e-6, 1e-5
GROUP1, GROUP2 = C // 32, C // 16

DEPTH = 5
BEHIND = """a_pe o2_pe oTT_pe onT_pe on_rd out_pe out_rd out_st v3_pe y_pe y_rd z_pe""".split()
START = 16

COLUMNS = ("b_phi_g", "b_theta", "sigma", "L0_conv_b_o", "L1_conv_gn_gamma", "L1_conv_gn_beta",
           "L1_conv_bq", "L1_conv_bk", "L1_conv_bv", "L1_conv_bo", "L2_conv_gn_scale",
           "L2_conv_gn_bias", "L2_conv_b_out", "b1_0", "b1_1", "b2_0", "b2_1")
LAYOUT = (
    (("columns", len(COLUMNS)), ("ident", P), ("w0", P), ("w0_o", C)),
    (("mean1", P), ("mean2", P), ("w1_q", C), ("w1_k", C), ("w1_vT", C), ("w1_o", C)),
    (("mlp", 6 * P), ("cas_c", C)),
    (("w2_q", C), ("w2_k", C), ("w2_v", C), ("w2_o", C), ("cas_w", P), ("cas_we", P // W * WE)),
)
AT = {}
for _group in LAYOUT:
    for _name, _width in _group:
        AT[_name] = (sum(w for _, w in AT.values()), _width)
TABLE_W = sum(w for _, w in AT.values())


def table(t):
    def cas(n):
        a = 2.0 * np.pi * (np.outer(np.arange(n), np.arange(n)) % n) / n
        return np.cos(a) + np.sin(a)

    def blocks(w):
        m = np.zeros((P, P), np.float32)
        for k in range(w.shape[0]):
            m[16 * k:16 * k + 16, 16 * k:16 * k + 16] = w[k]
        return m

    full = np.zeros((P, TABLE_W), np.float32)

    def at(name):
        first, width = AT[name]
        return full[:, first:first + width]

    rows = P // W
    at("ident")[:] = np.eye(P)
    at("mean1")[:] = np.kron(np.eye(C // GROUP1), np.full((GROUP1, GROUP1), 1.0 / GROUP1))
    at("mean2")[:] = np.kron(np.eye(C // GROUP2), np.full((GROUP2, GROUP2), 1.0 / GROUP2))
    at("cas_c")[:] = cas(C)
    at("cas_w")[:] = np.kron(np.eye(rows), cas(W))
    at("cas_we")[:] = np.kron(np.eye(rows), np.concatenate([cas(W), cas(W)[:, :1]], axis=1))
    at("w0")[:, 0:C8] = t["L0_conv_w_phi"]
    at("w0")[:, 32:32 + C8] = t["L0_conv_w_theta"]
    at("w0")[:, 64:128] = t["L0_conv_w_g"]
    at("w0_o")[64:128] = t["L0_conv_w_o"]
    at("w1_q")[:], at("w1_k")[:] = t["L1_conv_wq"], t["L1_conv_wk"]
    at("w1_vT")[:], at("w1_o")[:] = t["L1_conv_wv"].T, t["L1_conv_wo"]
    heads = t["L2_conv_w_qkv"].reshape(C, HEADS, 3, HD)
    at("w2_q")[:] = heads[:, :, 0].transpose(0, 2, 1).reshape(C, C)
    at("w2_k")[:] = heads[:, :, 1].transpose(0, 2, 1).reshape(C, C)
    at("w2_v")[:] = heads[:, :, 2].reshape(C, C)
    at("w2_o")[:] = t["L2_conv_w_out"]
    for k in range(2):
        w1, w2 = t["L3_conv_w1"][k], t["L3_conv_w2"][k]
        for n, m in enumerate((w1, w2, w2.transpose(0, 2, 1))):
            first = AT["mlp"][0] + (3 * k + n) * P
            full[:, first:first + P] = blocks(m)
    columns = dict(t)
    columns["b_phi_g"], columns["b_theta"] = np.zeros(P, np.float32), np.zeros(P, np.float32)
    columns["b_phi_g"][0:C8], columns["b_phi_g"][64:128] = t["L0_conv_b_phi"], t["L0_conv_b_g"]
    columns["b_theta"][0:C8] = t["L0_conv_b_theta"]
    columns["sigma"] = np.full(P, t["L0_conv_sigma"].reshape(-1)[0], np.float32)
    for k in range(2):
        columns[f"b1_{k}"], columns[f"b2_{k}"] = t["L3_conv_b1"][k].reshape(-1), t["L3_conv_b2"][k].reshape(-1)
    for n, name in enumerate(COLUMNS):
        at("columns")[:, n] = columns[name]
    return full


def build(nc, x, weights, out):
    x_tok = x.rearrange("b (u h) w c -> (b u) (h w) c", u=TILES)
    out_tok = out.rearrange("b (u h) w c -> (b u) (h w) c", u=TILES)

    with ExitStack() as ctx:
        def sb(name, shape, dt=F32):
            return ctx.enter_context(nc.sbuf_tensor(name, shape, dt))

        tab = sb("tab", [P, TABLE_W])

        def w(name):
            first, width = AT[name]
            return tab[:, first:first + width]

        def col(name):
            n = AT["columns"][0] + COLUMNS.index(name)
            return tab[:, n:n + 1]

        ident = w("ident")
        ident16 = sb("ident16", [P, P], BF16)
        w0s = sb("w0s", [P, C])
        wvo = sb("wvo", [P, C])
        w2qs = sb("w2qs", [P, C])
        mlp_half = sb("mlp_half", [P, 2, 3 * P])
        mlp_a = sb("mlp_a", [P, 3, P])
        mlp_b = sb("mlp_b", [P, 3, P])
        fold1 = sb("fold1", [P, 2, P])
        fold2 = sb("fold2", [P, 2, P])
        fold2t = sb("fold2t", [P, P])
        cas_out = sb("cas_out", [P, P])
        bq_s, bo0_s, bo1_f, c_t0, c_t1, c_low, c_high = (
            sb(n, [P, 1]) for n in ("bq_s", "bo0_s", "bo1_f", "c_t0", "c_t1", "c_low", "c_high"))
        busy = sb("busy", [P, 256], BF16)
        half = sb("half", [P, 1])

        xin = sb("xin", [P, 2, TILES, C])
        x0T = sb("x0T", [P, TOK])
        pooled = sb("pooled", [P, POOLED])
        pg = sb("pg", [P, POOLED])
        thetaT = sb("thetaT", [P, TOK])
        nmax0, sum0, inv0 = (sb(n, [P, TILES]) for n in ("nmax0", "sum0", "inv0"))
        p0 = sb("p0", [P, TILES, POOLED])
        p0n = sb("p0n", [P, TILES, POOLED])
        p0T = sb("p0T", [P, TOK])
        gw = sb("gw", [P, C])
        x1T = [sb(f"x1T{p}", [P, TOK]) for p in range(2)]

        bn = [sb(f"bn{k}", [P, 6]) for k in (1, 2)]
        mv = [sb(f"mv{k}", [P, 2]) for k in (1, 2)]
        gst = [sb(f"gst{k}", [P, 2]) for k in (1, 2)]
        var, vare, rstd, gsc, gsh = ([sb(f"{n}{k}", [P, 1]) for k in (1, 2)]
                                     for n in ("var", "vare", "rstd", "gsc", "gsh"))

        xn1 = sb("xn1", [P, TOK])
        q1T, k1T = sb("q1T", [P, TOK]), sb("k1T", [P, TOK])
        v1 = sb("v1", [P, TILES, C])
        nmax1, sum1, inv1 = (sb(n, [P, TILES]) for n in ("nmax1", "sum1", "inv1"))
        p1 = sb("p1", [P, TILES, TOK])
        p1n = sb("p1n", [P, TILES, TOK])
        p1T = sb("p1T", [P, TILES, TOK])
        x2T = sb("x2T", [P, TOK])

        x2b = sb("x2b", [P, TOK])
        xn2 = sb("xn2", [P, TOK])
        x2tok = [sb(f"x2tok{p}", [P, TOK]) for p in range(2)]
        parts = sb("parts", [P, 2, PARTS, TOK], BF16)
        rest = sb("rest", [P, 2, TOK])
        stack = [sb(f"stack{p}", [P, HEADS, 2, TOK], BF16) for p in range(2)]
        vaug = [sb(f"vaug{p}", [P, TILES, HEADS, 32]) for p in range(2)]
        nmax = sb("nmax", [P, TILES, HEADS])
        nrest = sb("nrest", [P, TILES, HEADS])
        npart = sb("npart", [P, TILES, PARTS, HEADS], BF16)
        nmaxT = sb("nmaxT", [P, TOK], BF16)
        pT = sb("pT", [P, HEADS, TILES, TOK])
        oT = sb("oT", [P, 2, TOK])
        oinv = sb("oinv", [P, TILES, HEADS])
        on = sb("on", [P, TILES, HEADS, HD])
        onT = sb("onT", [P, TOK])
        x3 = sb("x3", [P, TOK])

        zE = sb("zE", [P, HE, WE])
        o1k = sb("o1k", [P, TOK])
        o1nE = sb("o1nE", [P, HE, WE])
        yhigh = sb("yhigh", [P, TOK])
        yneg = sb("yneg", [P, TOK])
        s3 = sb("s3", [P, TILES, C])
        xout = sb("xout", [P, TOK])

        banks = [ctx.enter_context(nc.psum_tensor(f"bank{n}", [P, 512], F32)) for n in range(8)]
        gm1_ps = p1T_ps = nmT_ps = banks[0]
        s0_ps = v1_ps = banks[1]
        p0T_ps = o1_ps = pv_ps = onT_ps = z_ps = out_ps = banks[2]
        o2_ps = banks[3]
        gm2_ps = oTT_ps = a_ps = v3_ps = gw_ps = banks[4]
        proj_ps = o0_ps = s1_ps = y_ps = banks[5]
        x0T_ps = qk2_ps = banks[6]
        qk1_ps = xv2_ps = banks[7]
        smax_ps = [banks[n] for n in (6, 7, 1, 6, 4, 1, 3, 0)]
        sT_ps = [banks[n] for n in (1, 3, 6, 7, 1, 3, 0, 5)]
        fold_ps0, fold_ps1, fold_ps2 = banks[3][:, 0:P + 1], banks[3][:, P + 1:3 * P + 1], banks[7]

        produced = dict(
            sync="""tab0_in tab1_in tab2_in tab3_in x_in0 x_in1 stack_in0 stack_in1 neg_in out_st""",
            pool="""pool_setup sums_rd rstd1_rd rstd2_rd x2b_rd part2_rd""",
            pe="""fold_pe x0T_pe proj_pe s0_pe p0T_pe o0_pe gn1_pe gn2_pe qk1_pe v1_pe s1_pe p1T_pe o1_pe
                xv2_pe qk2_pe smax_pe nmT_pe sT_pe pv_pe oTT_pe onT_pe o2_pe z_pe a_pe y_pe v3_pe out_pe""",
            act="""act_setup x0T_rd theta_rd gw_rd exp0_rd p0T_rd qk1_rd v1_rd exp1_rd p1T_rd part0_rd xv_rd nmT_rd
                exp_rd oT_rd onT_rd z_rd o1_rd yhigh_rd v3_rd""",
            dve="""dve_setup pool_rd pg_rd nmax0_rd inv0_rd p0n_rd x1_rd bn1_rd bn2_rd mv1_rd mv2_rd
                st1_rd st2_rd gst1_rd gst2_rd var1_rd var2_rd vare1_rd vare2_rd gsc1_rd gsc2_rd
                gsh1_rd gsh2_rd xn1_rd xn2_rd nmax1_rd inv1_rd p1n_rd x2_rd rest_rd part1_rd nmax_rd
                nb0_rd nr0_rd nb1_rd npart_rd oinv_rd on_rd x3_rd zE_rd y_rd out_rd""",
        )
        s = {n: ctx.enter_context(nc.semaphore(n)) for names in produced.values() for n in names.split()}
        block = ctx.enter_context(nc.Block())

        def start(engine, who):
            for name in produced[who].split():
                if name in BEHIND:
                    engine.sem_inc(s[name], START)

        def count(name, i, per=1, k=None):
            start = START if name in BEHIND else 0
            if isinstance(i, int):
                if i < 0:
                    return start
                i = min(i, IMAGES - 1)
            return i * per + (start + (per if k is None else k))

        def count_half(name, i, p, per=16):
            start = START if name in BEHIND else 0
            return start if isinstance(i, int) and i < 0 else (i - p) * (per // 2) + (start + per)

        def stand_apart(engine, *values):
            for value in values:
                if not isinstance(value, int):
                    engine.lower_val(value)
            engine.wait_ge(s["tab0_in"], 16)

        def first_is(n, k):
            return isinstance(n, int) and n == k

        def steps(engine, step):
            first, turns = DEPTH - 1, (IMAGES - (DEPTH - 1)) // 2

            def live(n):
                return {k for k in range(DEPTH) if 0 <= n - k < IMAGES}

            for n in range(first):
                step(n, n % 2, live(n))
            with engine.Fori(0, turns) as turn:
                for k in range(2):
                    step(turn * 2 + (first + k), (first + k) % 2, set(range(DEPTH)))
            for n in range(first + 2 * turns, IMAGES + DEPTH - 1):
                step(n, n % 2, live(n))

        STACKS = 16 * len(PAIRS)

        fills = ((busy[:, :], 0.0), (thetaT[32:64, :], 0.0), (half[:, :], -0.5),
                 (vaug[0][:, :, :, HD:32], 0.0), (vaug[1][:, :, :, HD:32], 0.0),
                 (vaug[0][:, :, :, HD:HD + 1], 1.0), (vaug[1][:, :, :, HD:HD + 1], 1.0),
                 (stack[0][ROWS:AUG, :, 1, :], 1.0), (stack[1][ROWS:AUG, :, 1, :], 1.0))

        @block.sync
        def _(sp):
            start(sp, "sync")

            def load_x(i, p):
                sp.dma_start(xin[:, p, :, :], x_tok[bass.ds(i * TILES, TILES)].rearrange("u p c -> p u c")
                             ).then_inc(s[f"x_in{p}"], 16)

            def load_later_x(i, p):
                value = count("x0T_pe", i - 2)
                stand_apart(sp, value)
                sp.wait_ge(s["x0T_pe"], value)
                load_x(i, p)

            def load_table(group):
                first = AT[LAYOUT[group][0][0]][0]
                width = sum(n for _, n in LAYOUT[group])
                sp.dma_start(tab[:, first:first + width], weights[:, first:first + width]
                             ).then_inc(s[f"tab{group}_in"], 16)

            def spread(i, p, pairs):
                part_rd = ("part0_rd", "part1_rd", "part2_rd")[max(PAIRS[pairs[0]])]
                values = count(part_rd, i), count("sT_pe", i - 2, HEADS)
                stand_apart(sp, *values)
                sp.wait_ge(s[part_rd], values[0])
                if pairs[0] == 0:
                    sp.wait_ge(s["sT_pe"], values[1])
                for g in pairs:
                    a, b = PAIRS[g]
                    slots = parts[:, :, :, :].rearrange("p w a t -> p (w a) t")
                    sp.dma_start(stack[p][g * HD:(g + 1) * HD, :, :, :], slots[:, a:PARTS + b + 1:PARTS + b - a, :]
                                 ).then_inc(s[f"stack_in{p}"], 16)

            def spread_maxima(i, p):
                value = count("nmT_rd", i)
                stand_apart(sp, value)
                sp.wait_ge(s["nmT_rd"], value)
                sp.dma_start(stack[p][ROWS:AUG, :, 0, :], nmaxT[0:PARTS * HEADS, :]).then_inc(s["neg_in"], 16)

            def store(i):
                value = count("out_rd", i)
                stand_apart(sp, value)
                sp.wait_ge(s["out_rd"], value)
                sp.dma_start(out_tok[bass.ds(i * TILES, TILES)].rearrange("u p c -> p u c"),
                             xout[:, :].rearrange("p (u c) -> p u c", u=TILES)).then_inc(s["out_st"], 16)

            def step(n, p, live):
                q = 1 - p
                if 0 in live and not (isinstance(n, int) and n < 2): load_later_x(n, p)
                if 2 in live: spread(n - 2, p, (0,))
                if 3 in live: spread_maxima(n - 3, q)
                if 2 in live: spread(n - 2, p, (1, 2, 3))
                if 2 in live: spread(n - 2, p, (4, 5))
                if 4 in live: store(n - 4)

            load_x(0, 0)
            load_table(0)
            load_table(1)
            load_x(1, 1)
            load_table(2)
            load_table(3)
            steps(sp, step)
            sp.wait_ge(s["out_st"], count("out_st", IMAGES - 1, 16))

        @block.gpsimd
        def _(pool):
            start(pool, "pool")
            for n, (tile, value) in enumerate(fills):
                nc.gpsimd.memset(tile, value).then_inc(s["pool_setup"], 1)
                pool.wait_ge(s["pool_setup"], n + 1)

            def mlp_sums():
                pool.wait_ge(s["dve_setup"], 2)
                nc.gpsimd.tensor_tensor(mlp_a[:, :, :].rearrange("p m n -> p (m n)"), mlp_half[:, 0, :],
                                        mlp_half[:, 1, :], ALU.add).then_inc(s["sums_rd"], 1)
                nc.gpsimd.tensor_tensor(mlp_b[:, :, :].rearrange("p m n -> p (m n)"), mlp_half[:, 0, :],
                                        mlp_half[:, 1, :], ALU.subtract).then_inc(s["sums_rd"], 1)

            def deviation_inverse(i, layer):
                pool.wait_ge(s[f"vare{layer}_rd"], count(f"vare{layer}_rd", i))
                pool.wait_ge(s[f"gsc{layer}_rd"], count(f"gsc{layer}_rd", i - 1))
                nc.gpsimd.tensor_tensor(rstd[layer - 1][:, :], vare[layer - 1][:, :], half[:, :], ALU.pow
                                        ).then_inc(s[f"rstd{layer}_rd"], 1)

            def add_out_bias(i):
                pool.wait_ge(s["x2_rd"], count("x2_rd", i))
                pool.wait_ge(s["xv2_pe"], count("xv2_pe", i - 1))
                nc.gpsimd.tensor_tensor(x2b[:, :], x2T[:, :], col("L2_conv_b_out").to_broadcast((P, TOK)), ALU.add
                                        ).then_inc(s["x2b_rd"], 1)

            def part2(i):
                pool.wait_ge(s["part1_rd"], count("part1_rd", i))
                nc.gpsimd.tensor_tensor(parts[:, :, 2, :], rest[:, :, :], parts[:, :, 1, :], ALU.subtract
                                        ).then_inc(s["part2_rd"], 1)

            def step(n, p, live):
                q = 1 - p
                if 2 in live: deviation_inverse(n - 2, 2)
                if 2 in live: part2(n - 2)
                if 1 in live: add_out_bias(n - 1)
                if 0 in live: deviation_inverse(n, 1)

            mlp_sums()
            steps(pool, step)

        @block.tensor
        def _(pe):
            start(pe, "pe")
            mm, tr = nc.tensor.matmul, nc.tensor.transpose

            def keep_clock(i, bank, products):
                for _ in range(products.get(i, 0) if isinstance(i, int) else 0):
                    mm(bank[:, 0:256], busy[:, 0:P], busy[:, :], start=True, stop=True)

            pe.wait_ge(s["pool_setup"], 1)

            def fold_weights1():
                pe.wait_ge(s["tab1_in"], 16)
                mm(fold_ps0[:, 0:C], w("w1_vT"), w("w1_o"), start=True, stop=True)
                mm(fold_ps0[:, C:C + 1], w("w1_o"), col("L1_conv_bv"), start=True, stop=True).then_inc(s["fold_pe"], 1)

            def fold_weights2():
                pe.wait_ge(s["sums_rd"], 2)
                pe.wait_ge(s["dve_setup"], 3)
                for m, blk in enumerate((mlp_a, mlp_b)):
                    mm(fold_ps1[:, m * P:(m + 1) * P], w("cas_c"), blk[:, 0, :], start=True, stop=True)
                for m, blkT in enumerate((mlp_a, mlp_b)):
                    mm(fold_ps2[:, m * P:(m + 1) * P], blkT[:, 2, :], mlp_b[:, 1, :], start=True, stop=True)
                mm(fold_ps2[:, 2 * P:2 * P + 1], mlp_b[:, 1, :], col("b2_0"), start=True, stop=True
                   ).then_inc(s["fold_pe"], 1)

            def x_transposed(i, p):
                pe.wait_ge(s["nmax_rd"], count("nmax_rd", i - 3, 8, 4))
                if isinstance(i, int):
                    pe.wait_ge(s["nmax_rd"], count("nmax_rd", i - 3, 8, 1))
                    pe.wait_ge(s["exp_rd"], count("exp_rd", i - 4, 8, 3))
                    pe.wait_ge(s["rest_rd"], count("rest_rd", i - 3))
                    pe.wait_ge(s["x0T_rd"], count("x0T_rd", i - 1))
                keep_clock(i, x0T_ps, {0: 9})
                if first_is(i, 0):
                    pe.wait_ge(s["tab0_in"], 16)
                pe.wait_ge(s[f"x_in{p}"], count_half(f"x_in{p}", i, p))
                tr(x0T_ps[:, 0:P], xin[:, p, 0, :], ident)
                tr(x0T_ps[:, P:2 * P], xin[:, p, 1, :], ident).then_inc(s["x0T_pe"], 1)

            def project0(i):
                pe.wait_ge(s["exp_rd"], count("exp_rd", i - 4, 8, 8))
                if isinstance(i, int):
                    pe.wait_ge(s["y_rd"], count("y_rd", i - 5))
                    pe.wait_ge(s["x1_rd"], count("x1_rd", i - 1))
                keep_clock(i, proj_ps, {0: 3, 1: 4, 2: 4, 3: 4})
                pe.wait_ge(s["x0T_rd"], count("x0T_rd", i))
                mm(proj_ps[:, 0:TOK], w("w0"), x0T[:, :], start=True, stop=True).then_inc(s["proj_pe"], 1)

            def scores0(i):
                pe.wait_ge(s["nmax_rd"], count("nmax_rd", i - 3, 8, 6))
                if isinstance(i, int):
                    pe.wait_ge(s["nmax_rd"], count("nmax_rd", i - 3, 8, 3))
                    pe.wait_ge(s["exp_rd"], count("exp_rd", i - 4, 8, 5))
                    pe.wait_ge(s["exp_rd"], count("exp_rd", i - 4, 8, 1))
                    pe.wait_ge(s["v1_rd"], count("v1_rd", i - 2))
                    pe.wait_ge(s["exp0_rd"], count("exp0_rd", i - 1))
                pe.wait_ge(s["on_rd"], count("on_rd", i - 4))
                if isinstance(i, int):
                    pe.wait_ge(s["nmax_rd"], count("nmax_rd", i - 3, 8, 5))
                    pe.wait_ge(s["gst2_rd"], count("gst2_rd", i - 2))
                    pe.wait_ge(s["v3_rd"], count("v3_rd", i - 5))
                    pe.wait_ge(s["o1_rd"], count("o1_rd", i - 5))
                    pe.wait_ge(s["gw_rd"], count("gw_rd", i - 1))
                keep_clock(i, s0_ps, {0: 5})
                if first_is(i, 0):
                    pe.wait_ge(s["dve_setup"], 1)
                    pe.wait_ge(s["pool_setup"], 2)
                pe.wait_ge(s["theta_rd"], count("theta_rd", i))
                pe.wait_ge(s["pg_rd"], count("pg_rd", i))
                for u in range(TILES):
                    mm(s0_ps[:, u * POOLED:(u + 1) * POOLED], thetaT[0:64, u * P:(u + 1) * P], pg[0:64, :],
                       start=True, stop=True)
                mm(gw_ps[0:POOLED, 0:C], pg[64:128, :], w0s[64:128, :], start=True, stop=True).then_inc(s["s0_pe"], 1)

            def p0_transposed(i):
                keep_clock(i, p0T_ps, {0: 9})
                values = count("p0n_rd", i), count("z_rd", i - 4)
                stand_apart(pe, *values)
                pe.wait_ge(s["p0n_rd"], values[0])
                pe.wait_ge(s["z_rd"], values[1])
                if isinstance(i, int):
                    pe.wait_ge(s["onT_rd"], count("onT_rd", i - 4))
                    pe.wait_ge(s["oT_rd"], count("oT_rd", i - 4))
                    pe.wait_ge(s["out_rd"], count("out_rd", i - 5))
                    pe.wait_ge(s["x2_rd"], count("x2_rd", i - 2))
                    pe.wait_ge(s["p0T_rd"], count("p0T_rd", i - 1))
                for u in range(TILES):
                    last = tr(p0T_ps[0:POOLED, u * P:(u + 1) * P], p0n[:, u, :], ident)
                last.then_inc(s["p0T_pe"], 1)

            def attend0(i):
                pe.wait_ge(s["exp1_rd"], count("exp1_rd", i - 1))
                if isinstance(i, int):
                    pe.wait_ge(s["theta_rd"], count("theta_rd", i))
                keep_clock(i, o0_ps, {0: 3, 1: 3, 2: 3})
                pe.wait_ge(s["p0T_rd"], count("p0T_rd", i))
                pe.wait_ge(s["gw_rd"], count("gw_rd", i))
                mm(o0_ps[:, 0:TOK], gw[0:POOLED, :], p0T[0:POOLED, :], start=True, stop=True).then_inc(s["o0_pe"], 1)

            def group_means1(i):
                pe.wait_ge(s["p1T_rd"], count("p1T_rd", i - 1))
                keep_clock(i, gm1_ps, {0: 6})
                pe.wait_ge(s["st1_rd"], count("st1_rd", i))
                mm(gm1_ps[:, 0:2], w("mean1"), mv[0][:, :], start=True, stop=True).then_inc(s["gn1_pe"], 1)

            def group_means2(i):
                pe.wait_ge(s["v3_rd"], count("v3_rd", i - 3))
                if isinstance(i, int):
                    pe.wait_ge(s["o1_rd"], count("o1_rd", i - 3))
                    pe.wait_ge(s["gw_rd"], count("gw_rd", i + 1))
                keep_clock(i, gm2_ps, {0: 5, 1: 3})
                pe.wait_ge(s["st2_rd"], count("st2_rd", i))
                mm(gm2_ps[:, 0:2], w("mean2"), mv[1][:, :], start=True, stop=True).then_inc(s["gn2_pe"], 1)

            def project1(i):
                pe.wait_ge(s["nmax_rd"], count("nmax_rd", i - 2, 8, 2))
                if isinstance(i, int):
                    pe.wait_ge(s["exp_rd"], count("exp_rd", i - 3, 8, 4))
                    pe.wait_ge(s["xv_rd"], count("xv_rd", i - 2))
                    pe.wait_ge(s["qk1_rd"], count("qk1_rd", i - 1))
                keep_clock(i, qk1_ps, {0: 5})
                pe.wait_ge(s["xn1_rd"], count("xn1_rd", i))
                mm(qk1_ps[:, 0:TOK], w("w1_q"), xn1[:, :], start=True, stop=True)
                mm(qk1_ps[:, TOK:2 * TOK], w("w1_k"), xn1[:, :], start=True, stop=True).then_inc(s["qk1_pe"], 1)

            def values1(i):
                pe.wait_ge(s["exp0_rd"], count("exp0_rd", i + 1))
                if isinstance(i, int):
                    pe.wait_ge(s["nmax_rd"], count("nmax_rd", i - 2, 8, 6))
                if first_is(i, 0):
                    pe.wait_ge(s["dve_setup"], 3)
                pe.wait_ge(s["xn1_rd"], count("xn1_rd", i))
                for u in range(TILES):
                    last = mm(v1_ps[:, u * C:(u + 1) * C], xn1[:, u * P:(u + 1) * P], wvo[:, :], start=True, stop=True)
                last.then_inc(s["v1_pe"], 1)

            def scores1(i):
                pe.wait_ge(s["theta_rd"], count("theta_rd", i + 1))
                if isinstance(i, int):
                    pe.wait_ge(s["exp_rd"], count("exp_rd", i - 3, 8, 8))
                keep_clock(i, s1_ps, {0: 4})
                pe.wait_ge(s["qk1_rd"], count("qk1_rd", i))
                for u in range(TILES):
                    last = mm(s1_ps[:, u * TOK:(u + 1) * TOK], q1T[:, u * P:(u + 1) * P], k1T[:, :],
                              start=True, stop=True)
                last.then_inc(s["s1_pe"], 1)

            def p1_transposed(i):
                pe.wait_ge(s["nmT_rd"], count("nmT_rd", i - 2))
                if isinstance(i, int):
                    pe.wait_ge(s["nmax_rd"], count("nmax_rd", i - 2, 8, 8))
                    pe.wait_ge(s["exp_rd"], count("exp_rd", i - 3, 8, 7))
                    pe.wait_ge(s["gst1_rd"], count("gst1_rd", i))
                keep_clock(i, p1T_ps, {0: 4, 1: 4})
                pe.wait_ge(s["p1n_rd"], count("p1n_rd", i))
                for u in range(TILES):
                    for m in range(TILES):
                        last = tr(p1T_ps[:, m * TOK + u * P:m * TOK + (u + 1) * P], p1n[:, u, m * P:(m + 1) * P], ident)
                last.then_inc(s["p1T_pe"], 1)

            def attend1(i):
                pe.wait_ge(s["p0T_rd"], count("p0T_rd", i + 1))
                if isinstance(i, int):
                    pe.wait_ge(s["z_rd"], count("z_rd", i - 3))
                keep_clock(i, o1_ps, {0: 4, 1: 4})
                pe.wait_ge(s["v1_rd"], count("v1_rd", i))
                pe.wait_ge(s["p1T_rd"], count("p1T_rd", i))
                for m in range(TILES):
                    last = mm(o1_ps[:, 0:TOK], v1[:, m, :], p1T[:, m, :], start=(m == 0), stop=(m == TILES - 1))
                last.then_inc(s["o1_pe"], 1)

            def project2(i):
                pe.wait_ge(s["x0T_rd"], count("x0T_rd", i + 2))
                if isinstance(i, int):
                    pe.wait_ge(s["nmax_rd"], count("nmax_rd", i - 1, 8, 4))
                if first_is(i, 0):
                    pe.wait_ge(s["dve_setup"], 4)
                pe.wait_ge(s["xn2_rd"], count("xn2_rd", i))
                mm(qk2_ps[:, 0:TOK], w2qs[:, :], xn2[:, :], start=True, stop=True)
                mm(qk2_ps[:, TOK:2 * TOK], w("w2_k"), xn2[:, :], start=True, stop=True).then_inc(s["qk2_pe"], 1)

            def values2(i):
                pe.wait_ge(s["qk1_rd"], count("qk1_rd", i + 1))
                if isinstance(i, int):
                    pe.wait_ge(s["nmax_rd"], count("nmax_rd", i - 1, 8, 2))
                pe.wait_ge(s["x2b_rd"], count("x2b_rd", i))
                pe.wait_ge(s["xn2_rd"], count("xn2_rd", i))
                for u in range(TILES):
                    tr(xv2_ps[:, u * P:(u + 1) * P], x2b[:, u * P:(u + 1) * P], ident)
                for u in range(TILES):
                    last = mm(xv2_ps[:, TOK + u * C:TOK + (u + 1) * C], xn2[:, u * P:(u + 1) * P], w("w2_v"),
                              start=True, stop=True)
                last.then_inc(s["xv2_pe"], 1)

            def scores_by_query(i, p, h):
                if h == 0:
                    pe.wait_ge(s["exp_rd"], count("exp_rd", i - 1, 8, 3))
                    if isinstance(i, int):
                        pe.wait_ge(s["rest_rd"], count("rest_rd", i))
                if h == 1:
                    pe.wait_ge(s["exp_rd"], count("exp_rd", i - 1, 8, 4))
                    if isinstance(i, int):
                        pe.wait_ge(s["xv_rd"], count("xv_rd", i))
                if h == 2:
                    pe.wait_ge(s["exp_rd"], count("exp_rd", i - 1, 8, 5))
                    if isinstance(i, int):
                        pe.wait_ge(s["exp_rd"], count("exp_rd", i - 1, 8, 1))
                        pe.wait_ge(s["v1_rd"], count("v1_rd", i + 1))
                if h == 3:
                    pe.wait_ge(s["nmax_rd"], count("nmax_rd", i, 8, 1))
                if h == 4:
                    pe.wait_ge(s["gst2_rd"], count("gst2_rd", i + 1))
                    if isinstance(i, int):
                        pe.wait_ge(s["v3_rd"], count("v3_rd", i - 2))
                if h == 5:
                    pe.wait_ge(s["nmax_rd"], count("nmax_rd", i, 8, 3))
                if h == 6:
                    pe.wait_ge(s["exp_rd"], count("exp_rd", i - 1, 8, 6))
                if h == 7:
                    pe.wait_ge(s["exp_rd"], count("exp_rd", i - 1, 8, 7))
                    if isinstance(i, int):
                        pe.wait_ge(s["gst1_rd"], count("gst1_rd", i + 2))
                if h == 0:
                    keep_clock(i, smax_ps[h], {0: 4, 1: 4})
                    pe.wait_ge(s[f"stack_in{p}"], count_half(f"stack_in{p}", i, p, STACKS))
                for u in range(TILES):
                    last = mm(smax_ps[h][:, u * TOK:(u + 1) * TOK], stack[p][0:ROWS, h, 0, u * P:(u + 1) * P],
                              stack[p][0:ROWS, h, 1, :], start=True, stop=True)
                last.then_inc(s["smax_pe"], 1)

            def maxima_transposed(i):
                pe.wait_ge(s["nmax_rd"], count("nmax_rd", i, 8, 8))
                if first_is(i, 0):
                    pe.wait_ge(s["act_setup"], 1)
                pe.wait_ge(s["npart_rd"], count("npart_rd", i))
                turned = nmT_ps[:, :].bitcast(BF16)
                for u in range(TILES):
                    last = tr(turned[0:PARTS * HEADS, u * P:(u + 1) * P],
                              npart[:, u, :, :].rearrange("p a h -> p (a h)"), ident16[:, :])
                last.then_inc(s["nmT_pe"], 1)

            def scores_by_key(i, p, h):
                if h == 0:
                    pe.wait_ge(s["v1_rd"], count("v1_rd", i + 2))
                    if isinstance(i, int):
                        pe.wait_ge(s["exp0_rd"], count("exp0_rd", i + 3))
                        pe.wait_ge(s["nmax_rd"], count("nmax_rd", i, 8, 6))
                if h == 1:
                    pe.wait_ge(s["x3_rd"], count("x3_rd", i - 1))
                    if isinstance(i, int):
                        pe.wait_ge(s["nmax_rd"], count("nmax_rd", i, 8, 7))
                if h == 2:
                    pe.wait_ge(s["rest_rd"], count("rest_rd", i + 1))
                    if isinstance(i, int):
                        pe.wait_ge(s["x0T_rd"], count("x0T_rd", i + 3))
                        pe.wait_ge(s["nmax_rd"], count("nmax_rd", i, 8, 4))
                if h == 3:
                    pe.wait_ge(s["xv_rd"], count("xv_rd", i + 1))
                    if isinstance(i, int):
                        pe.wait_ge(s["qk1_rd"], count("qk1_rd", i + 2))
                        pe.wait_ge(s["nmax_rd"], count("nmax_rd", i, 8, 2))
                if h == 4:
                    pe.wait_ge(s["exp_rd"], count("exp_rd", i, 8, 1))
                if h == 5:
                    pe.wait_ge(s["exp_rd"], count("exp_rd", i, 8, 2))
                if h == 6:
                    pe.wait_ge(s["gst1_rd"], count("gst1_rd", i + 3))
                    if isinstance(i, int):
                        pe.wait_ge(s["p1T_rd"], count("p1T_rd", i + 2))
                        pe.wait_ge(s["nmT_rd"], count("nmT_rd", i))
                if h == 7:
                    pe.wait_ge(s["y_rd"], count("y_rd", i - 1))
                    if isinstance(i, int):
                        pe.wait_ge(s["x1_rd"], count("x1_rd", i + 3))
                if h == 0:
                    if first_is(i, 0):
                        pe.wait_ge(s["pool_setup"], len(fills))
                    pe.wait_ge(s["neg_in"], count("neg_in", i, 16))
                for m in range(TILES):
                    last = mm(sT_ps[h][:, m * TOK:(m + 1) * TOK], stack[p][0:AUG, h, 1, m * P:(m + 1) * P],
                              stack[p][0:AUG, h, 0, :], start=True, stop=True)
                last.then_inc(s["sT_pe"], 1)

            def attend2(i, p, g):
                pe.wait_ge(s["out_rd"], count("out_rd", i - 1))
                pe.wait_ge(s["x2_rd"], count("x2_rd", i + 2))
                pe.wait_ge(s["exp_rd"], count("exp_rd", i, HEADS, 4 * g + 4))
                if g == 0:
                    pe.wait_ge(s["xv_rd"], count("xv_rd", i))
                for m in range(TILES):
                    for j in range(4):
                        last = mm(pv_ps[32 * j:32 * j + 32, g * TOK:(g + 1) * TOK], vaug[p][:, m, 4 * g + j, :],
                                  pT[:, 4 * g + j, m, :], start=(m == 0), stop=(m == TILES - 1))
                last.then_inc(s["pv_pe"], 1)

            def o_back(i):
                pe.wait_ge(s["nmax_rd"], count("nmax_rd", i + 1, 8, 5))
                if isinstance(i, int):
                    pe.wait_ge(s["gst2_rd"], count("gst2_rd", i + 2))
                    pe.wait_ge(s["v3_rd"], count("v3_rd", i - 1))
                keep_clock(i, oTT_ps, {7: 4})
                pe.wait_ge(s["oT_rd"], count("oT_rd", i))
                for u in range(TILES):
                    for g in range(2):
                        last = tr(oTT_ps[:, (2 * u + g) * P:(2 * u + g + 1) * P], oT[:, g, u * P:(u + 1) * P], ident)
                last.then_inc(s["oTT_pe"], 1)

            def on_transposed(i):
                pe.wait_ge(s["oT_rd"], count("oT_rd", i))
                keep_clock(i, onT_ps, {6: 5, 7: 5})
                pe.wait_ge(s["on_rd"], count("on_rd", i))
                for u in range(TILES):
                    last = tr(onT_ps[:, u * P:(u + 1) * P], on[:, u, :, :].rearrange("p h d -> p (h d)"), ident)
                last.then_inc(s["onT_pe"], 1)

            def project_out(i):
                pe.wait_ge(s["nmax_rd"], count("nmax_rd", i + 1, 8, 7))
                if isinstance(i, int):
                    pe.wait_ge(s["exp_rd"], count("exp_rd", i, 8, 6))
                keep_clock(i, o2_ps, {6: 3, 7: 4})
                pe.wait_ge(s["onT_rd"], count("onT_rd", i))
                for u in range(TILES):
                    last = mm(o2_ps[:, u * C:(u + 1) * C], onT[:, u * P:(u + 1) * P], w("w2_o"), start=True, stop=True)
                last.then_inc(s["o2_pe"], 1)

            def transform_w(i):
                pe.wait_ge(s["onT_rd"], count("onT_rd", i))
                keep_clock(i, z_ps, {7: 3})
                pe.wait_ge(s["x3_rd"], count("x3_rd", i))
                n = P // W * WE
                for u in range(TILES):
                    last = mm(z_ps[:, u * n:(u + 1) * n], x3[:, u * C:(u + 1) * C], w("cas_we"), start=True, stop=True)
                last.then_inc(s["z_pe"], 1)

            def hidden(i):
                pe.wait_ge(s["gw_rd"], count("gw_rd", i + 4))
                if isinstance(i, int):
                    pe.wait_ge(s["on_rd"], count("on_rd", i))
                keep_clock(i, a_ps, {6: 6, 7: 3})
                if first_is(i, 0):
                    pe.wait_ge(s["dve_setup"], 7)
                pe.wait_ge(s["zE_rd"], count("zE_rd", i))
                both = a_ps[:, 0:EXT].rearrange("p (h w) -> p h w", h=HE)
                mm(both, fold1[:, 0, :], zE[:, :, :], start=True, stop=False)
                mm(both, fold1[:, 1, :], zE[:, ::-1, ::-1], start=False, stop=True).then_inc(s["a_pe"], 1)

            def mlp_out(i):
                pe.wait_ge(s["x1_rd"], count("x1_rd", i + 4))
                if isinstance(i, int):
                    pe.wait_ge(s["exp1_rd"], count("exp1_rd", i + 3))
                    pe.wait_ge(s["theta_rd"], count("theta_rd", i + 4))
                    pe.wait_ge(s["exp_rd"], count("exp_rd", i, 8, 8))
                keep_clock(i, y_ps, {6: 3, 7: 4})
                pe.wait_ge(s["o1_rd"], count("o1_rd", i))
                y = y_ps[:, 0:TOK].rearrange("p (h w) -> p h w", h=H)
                mm(y, fold2[:, 0, :], o1k[:, :].rearrange("p (h w) -> p h w", h=H), start=True, stop=False)
                mm(y, fold2[:, 1, :], o1nE[:, H:0:-1, W:0:-1], start=False, stop=True).then_inc(s["y_pe"], 1)

            def transform_c_back(i):
                pe.wait_ge(s["o1_rd"], count("o1_rd", i))
                keep_clock(i, v3_ps, {6: 4, 7: 5})
                pe.wait_ge(s["y_rd"], count("y_rd", i))
                for u in range(TILES):
                    last = mm(v3_ps[:, u * C:(u + 1) * C], yneg[:, u * P:(u + 1) * P], cas_out[:, :],
                              start=True, stop=True)
                last.then_inc(s["v3_pe"], 1)

            def transform_w_back(i):
                pe.wait_ge(s["x2_rd"], count("x2_rd", i + 3))
                if isinstance(i, int):
                    pe.wait_ge(s["p0T_rd"], count("p0T_rd", i + 4))
                    pe.wait_ge(s["z_rd"], count("z_rd", i))
                keep_clock(i, out_ps, {7: 4})
                pe.wait_ge(s["v3_rd"], count("v3_rd", i))
                mm(out_ps[:, 0:TOK], w("cas_w"), s3[:, :, :].rearrange("p u c -> p (u c)"), start=True, stop=True
                   ).then_inc(s["out_pe"], 1)

            def step(n, p, live):
                q = 1 - p
                if 3 in live: scores_by_query(n - 3, q, 3)
                if 3 in live: scores_by_query(n - 3, q, 4)
                if 4 in live: attend2(n - 4, p, 0)
                if 4 in live: attend2(n - 4, p, 1)
                if 3 in live: scores_by_query(n - 3, q, 5)
                if 3 in live: scores_by_query(n - 3, q, 6)
                if 0 in live: x_transposed(n, p)
                if 3 in live: scores_by_query(n - 3, q, 7)
                if 4 in live: o_back(n - 4)
                if 0 in live: project0(n)
                if first_is(n, 1): pe.wait_ge(s["dve_setup"], 5)
                if first_is(n, 1): pe.wait_ge(s["act_setup"], 2)
                if 1 in live: project1(n - 1)
                if 4 in live: on_transposed(n - 4)
                if 2 in live: project2(n - 2)
                if 4 in live: project_out(n - 4)
                if 0 in live: scores0(n)
                if first_is(n, 0): fold_weights1()
                if 1 in live: scores1(n - 1)
                if 3 in live: maxima_transposed(n - 3)
                if 4 in live: transform_w(n - 4)
                if 2 in live: values2(n - 2)
                if 1 in live: values1(n - 1)
                if 0 in live: p0_transposed(n)
                if 4 in live: hidden(n - 4)
                if 0 in live: attend0(n)
                if 1 in live: p1_transposed(n - 1)
                if 3 in live: scores_by_key(n - 3, q, 0)
                if 3 in live: scores_by_key(n - 3, q, 1)
                if 4 in live: mlp_out(n - 4)
                if 3 in live: scores_by_key(n - 3, q, 2)
                if 1 in live: attend1(n - 1)
                if 3 in live: scores_by_key(n - 3, q, 3)
                if 0 in live: group_means1(n)
                if 3 in live: scores_by_key(n - 3, q, 4)
                if 4 in live: transform_c_back(n - 4)
                if 3 in live: scores_by_key(n - 3, q, 5)
                if 2 in live: scores_by_query(n - 2, p, 0)
                if 3 in live: scores_by_key(n - 3, q, 6)
                if 4 in live: transform_w_back(n - 4)
                if 2 in live: scores_by_query(n - 2, p, 1)
                if 1 in live: group_means2(n - 1)
                if 3 in live: scores_by_key(n - 3, q, 7)
                if 2 in live: scores_by_query(n - 2, p, 2)
                if first_is(n, 0): fold_weights2()

            steps(pe, step)

        @block.scalar
        def _(act):
            start(act, "act")
            go, copy = nc.scalar.activation, nc.scalar.copy
            act.wait_ge(s["tab0_in"], 16)
            copy(ident16[:, :], ident)
            go(bq_s[:, :], col("L1_conv_bq"), ACT.Copy, scale=float(C) ** -0.5).then_inc(s["act_setup"], 1)

            def setup_fold1():
                act.wait_ge(s["fold_pe"], 2)
                copy(fold1[:, :, :].rearrange("p m n -> p (m n)"), fold_ps1[:, 0:2 * P]).then_inc(s["act_setup"], 1)

            def x0T_out(i):
                act.wait_ge(s["x0T_pe"], count("x0T_pe", i))
                act.wait_ge(s["proj_pe"], count("proj_pe", i - 1))
                act.wait_ge(s["x1_rd"], count("x1_rd", i - 1))
                copy(x0T[:, :], x0T_ps[:, 0:TOK]).then_inc(s["x0T_rd"], 1)

            def theta_out(i):
                act.wait_ge(s["pool_rd"], count("pool_rd", i))
                act.wait_ge(s["s0_pe"], count("s0_pe", i - 1))
                go(thetaT[0:32, :], proj_ps[32:64, 0:TOK], ACT.Identity, bias=col("b_theta")[0:32, :]
                   ).then_inc(s["theta_rd"], 1)

            def gw_out(i):
                act.wait_ge(s["s0_pe"], count("s0_pe", i))
                act.wait_ge(s["o0_pe"], count("o0_pe", i - 1))
                copy(gw[0:POOLED, :], gw_ps[0:POOLED, 0:C]).then_inc(s["gw_rd"], 1)

            def exp0(i):
                act.wait_ge(s["nmax0_rd"], count("nmax0_rd", i))
                act.wait_ge(s["p0n_rd"], count("p0n_rd", i - 1))
                for u in range(TILES):
                    last = go(p0[:, u, :], s0_ps[:, u * POOLED:(u + 1) * POOLED], ACT.Exp, bias=nmax0[:, u:u + 1],
                              accum_out=sum0[:, u:u + 1])
                last.then_inc(s["exp0_rd"], 1)

            def p0T_out(i):
                act.wait_ge(s["p0T_pe"], count("p0T_pe", i))
                act.wait_ge(s["o0_pe"], count("o0_pe", i - 1))
                copy(p0T[0:POOLED, :], p0T_ps[0:POOLED, 0:TOK]).then_inc(s["p0T_rd"], 1)

            def qk1_out(i):
                if first_is(i, 0):
                    act.wait_ge(s["act_setup"], 1)
                act.wait_ge(s["qk1_pe"], count("qk1_pe", i))
                act.wait_ge(s["s1_pe"], count("s1_pe", i - 1))
                go(q1T[:, :], qk1_ps[:, 0:TOK], ACT.Identity, bias=bq_s[:, :], scale=float(C) ** -0.5)
                go(k1T[:, :], qk1_ps[:, TOK:2 * TOK], ACT.Identity, bias=col("L1_conv_bk")).then_inc(s["qk1_rd"], 1)

            def v1_out(i):
                act.wait_ge(s["v1_pe"], count("v1_pe", i))
                act.wait_ge(s["o1_pe"], count("o1_pe", i - 1))
                copy(v1[:, :, :].rearrange("p u c -> p (u c)"), v1_ps[:, 0:TOK]).then_inc(s["v1_rd"], 1)

            def exp1(i):
                act.wait_ge(s["nmax1_rd"], count("nmax1_rd", i))
                act.wait_ge(s["p1n_rd"], count("p1n_rd", i - 1))
                for u in range(TILES):
                    last = go(p1[:, u, :], s1_ps[:, u * TOK:(u + 1) * TOK], ACT.Exp, bias=nmax1[:, u:u + 1],
                              accum_out=sum1[:, u:u + 1])
                last.then_inc(s["exp1_rd"], 1)

            def p1T_out(i):
                act.wait_ge(s["p1T_pe"], count("p1T_pe", i))
                act.wait_ge(s["o1_pe"], count("o1_pe", i - 1))
                copy(p1T[:, :, :].rearrange("p m t -> p (m t)"), p1T_ps[:, :]).then_inc(s["p1T_rd"], 1)

            def part0(i, p):
                act.wait_ge(s["qk2_pe"], count("qk2_pe", i))
                act.wait_ge(s["rest_rd"], count("rest_rd", i - 1))
                act.wait_ge(s[f"stack_in{1 - p}"], count_half(f"stack_in{1 - p}", i - 1, 1 - p, STACKS))
                copy(parts[:, :, 0, :], qk2_ps[:, :].rearrange("p (w t) -> p w t", w=2)).then_inc(s["part0_rd"], 1)

            def xv_out(i, p):
                act.wait_ge(s["xv2_pe"], count("xv2_pe", i))
                act.wait_ge(s["x3_rd"], count("x3_rd", i - 2))
                act.wait_ge(s["pv_pe"], count("pv_pe", i - 2, 2))
                copy(x2tok[p][:, :], xv2_ps[:, 0:TOK])
                copy(vaug[p][:, :, :, 0:HD], xv2_ps[:, TOK:2 * TOK].rearrange("p (u h d) -> p u h d", u=TILES, h=HEADS)
                     ).then_inc(s["xv_rd"], 1)

            def maxima_out(i):
                act.wait_ge(s["nmT_pe"], count("nmT_pe", i))
                act.wait_ge(s["neg_in"], count("neg_in", i - 1, 16))
                copy(nmaxT[0:PARTS * HEADS, :], nmT_ps[:, :].bitcast(BF16)[0:PARTS * HEADS, 0:TOK]
                     ).then_inc(s["nmT_rd"], 1)

            def exp2(i, h):
                act.wait_ge(s["sT_pe"], count("sT_pe", i, HEADS, h + 1))
                if h == 0:
                    act.wait_ge(s["pv_pe"], count("pv_pe", i - 1, 2, 1))
                if h == 4:
                    act.wait_ge(s["pv_pe"], count("pv_pe", i - 1, 2, 2))
                go(pT[:, h, :, :].rearrange("p m t -> p (m t)"), sT_ps[h][:, :], ACT.Exp).then_inc(s["exp_rd"], 1)

            def oT_out(i):
                act.wait_ge(s["pv_pe"], count("pv_pe", i, 2))
                act.wait_ge(s["oTT_pe"], count("oTT_pe", i - 1))
                copy(oT[:, :, :].rearrange("p g t -> p (g t)"), pv_ps[:, :]).then_inc(s["oT_rd"], 1)

            def onT_out(i):
                act.wait_ge(s["onT_pe"], count("onT_pe", i))
                act.wait_ge(s["o2_pe"], count("o2_pe", i - 1))
                copy(onT[:, :], onT_ps[:, 0:TOK]).then_inc(s["onT_rd"], 1)

            def z_out(i):
                act.wait_ge(s["z_pe"], count("z_pe", i))
                act.wait_ge(s["a_pe"], count("a_pe", i - 1))
                copy(zE[:, 0:H, :].rearrange("p h w -> p (h w)"), z_ps[:, 0:H * WE]).then_inc(s["z_rd"], 1)

            def o1_out(i):
                act.wait_ge(s["a_pe"], count("a_pe", i))
                act.wait_ge(s["y_pe"], count("y_pe", i - 1))
                go(o1k[:, :].rearrange("p (h w) -> p h w", h=H),
                   a_ps[:, 0:EXT].rearrange("p (h w) -> p h w", h=HE)[:, 0:H, 0:W], ACT.Relu, bias=col("b1_0"))
                go(o1nE[:, :, :].rearrange("p h w -> p (h w)"), a_ps[:, 0:EXT], ACT.Relu, bias=col("b1_1")
                   ).then_inc(s["o1_rd"], 1)

            def yhigh_out(i):
                act.wait_ge(s["y_pe"], count("y_pe", i))
                act.wait_ge(s["y_rd"], count("y_rd", i - 1))
                if first_is(i, 0):
                    act.wait_ge(s["dve_setup"], 7)
                go(yhigh[:, :], y_ps[:, 0:TOK], ACT.Relu, bias=c_low[:, :]).then_inc(s["yhigh_rd"], 1)

            def v3_out(i):
                act.wait_ge(s["v3_pe"], count("v3_pe", i))
                act.wait_ge(s["out_pe"], count("out_pe", i - 1))
                copy(s3[:, :, :].rearrange("p u c -> p (u c)"), v3_ps[:, 0:TOK]).then_inc(s["v3_rd"], 1)

            def step(n, p, live):
                q = 1 - p
                if 4 in live: exp2(n - 4, 7)
                if 4 in live: oT_out(n - 4)
                if 0 in live: x0T_out(n)
                if 4 in live: onT_out(n - 4)
                if 0 in live: theta_out(n)
                if 1 in live: qk1_out(n - 1)
                if 2 in live: part0(n - 2, p)
                if 0 in live: gw_out(n)
                if 0 in live: exp0(n)
                if 3 in live: maxima_out(n - 3)
                if 4 in live: z_out(n - 4)
                if 1 in live: exp1(n - 1)
                if 0 in live: p0T_out(n)
                if 2 in live: xv_out(n - 2, p)
                if 1 in live: v1_out(n - 1)
                if 4 in live: o1_out(n - 4)
                if 1 in live: p1T_out(n - 1)
                if 3 in live: exp2(n - 3, 0)
                if 3 in live: exp2(n - 3, 1)
                if 4 in live: yhigh_out(n - 4)
                if 3 in live: exp2(n - 3, 2)
                if 3 in live: exp2(n - 3, 3)
                if 4 in live: v3_out(n - 4)
                if 3 in live: exp2(n - 3, 4)
                if 3 in live: exp2(n - 3, 5)
                if 3 in live: exp2(n - 3, 6)
                if first_is(n, 0): setup_fold1()

            steps(act, step)

        @block.vector
        def _(dve):
            start(dve, "dve")
            v = nc.vector
            dve.wait_ge(s["tab0_in"], 16)
            v.tensor_scalar(bo0_s[:, :], col("L0_conv_b_o"), col("sigma"), None, ALU.mult)
            v.tensor_scalar(w0s[64:128, :], w("w0_o")[64:128, :], col("sigma")[64:128, :], None, ALU.mult
                            ).then_inc(s["dve_setup"], 1)

            def setup_values1():
                dve.wait_ge(s["fold_pe"], 1)
                v.tensor_scalar(bo1_f[:, :], fold_ps0[:, C:C + 1], col("L1_conv_bo"), None, ALU.add)
                v.tensor_copy(wvo[:, :], fold_ps0[:, 0:C]).then_inc(s["dve_setup"], 1)

            def setup_halves():
                dve.wait_ge(s["tab2_in"], 16)
                v.tensor_scalar(mlp_half[:, :, :].rearrange("p k n -> p (k n)"), w("mlp"), 0.5, None, ALU.mult
                                ).then_inc(s["dve_setup"], 1)

            def setup_scales():
                dve.wait_ge(s["tab3_in"], 16)
                v.tensor_scalar(w2qs[:, :], w("w2_q"), float(HD) ** -0.5, None, ALU.mult)
                v.tensor_scalar(cas_out[:, :], w("cas_c"), -1.0 / (W * C), None, ALU.mult).then_inc(s["dve_setup"], 1)

            def setup_layer3():
                dve.wait_ge(s["fold_pe"], 2)
                v.scalar_tensor_tensor(out=fold2[:, 0, :], in0=mlp_a[:, 1, :], scalar=-1.0, in1=fold_ps2[:, 0:P],
                                       op0=ALU.mult, op1=ALU.subtract)
                v.scalar_tensor_tensor(out=fold2t[:, :], in0=mlp_a[:, 1, :], scalar=-1.0, in1=fold_ps2[:, P:2 * P],
                                       op0=ALU.mult, op1=ALU.subtract)
                v.tensor_scalar(c_t0[:, :], fold_ps2[:, 2 * P:2 * P + 1], col("b2_0"), None, ALU.add
                                ).then_inc(s["dve_setup"], 1)

            def setup_layer3_sums():
                dve.wait_ge(s["dve_setup"], 5)
                v.tensor_tensor(fold2[:, 1, :], fold2t[:, :], mlp_b[:, 1, :], ALU.subtract)
                v.tensor_scalar(c_t1[:, :], c_t0[:, :], col("b2_1"), None, ALU.add).then_inc(s["dve_setup"], 1)
                dve.wait_ge(s["dve_setup"], 6)
                v.tensor_scalar(c_low[:, :], c_t1[:, :], -1.0, -SPARSITY, ALU.mult, ALU.add)
                v.tensor_scalar(c_high[:, :], c_t1[:, :], -1.0, SPARSITY, ALU.mult, ALU.add).then_inc(s["dve_setup"], 1)

            def pool_out(i):
                dve.wait_ge(s["proj_pe"], count("proj_pe", i))
                v.tensor_reduce(pooled[:, :], proj_ps[:, 0:TOK].rearrange("p (h a w b) -> p h w a b", h=H // 2, a=2, b=2),
                                AX.XY, ALU.max).then_inc(s["pool_rd"], 1)

            def pg_out(i):
                dve.wait_ge(s["pool_rd"], count("pool_rd", i))
                dve.wait_ge(s["s0_pe"], count("s0_pe", i - 1))
                v.tensor_scalar(pg[:, :], pooled[:, :], col("b_phi_g"), None, ALU.add).then_inc(s["pg_rd"], 1)

            def nmax0_out(i):
                dve.wait_ge(s["s0_pe"], count("s0_pe", i))
                dve.wait_ge(s["exp0_rd"], count("exp0_rd", i - 1))
                v.tensor_reduce(nmax0[:, :], s0_ps[:, 0:TILES * POOLED].rearrange("p (u m) -> p u m", u=TILES),
                                AX.X, ALU.max, negate=True).then_inc(s["nmax0_rd"], 1)

            def inv0_out(i):
                dve.wait_ge(s["exp0_rd"], count("exp0_rd", i))
                dve.wait_ge(s["p0n_rd"], count("p0n_rd", i - 1))
                v.reciprocal(inv0[:, :], sum0[:, :]).then_inc(s["inv0_rd"], 1)

            def normalise_p0(i):
                dve.wait_ge(s["inv0_rd"], count("inv0_rd", i))
                dve.wait_ge(s["p0T_pe"], count("p0T_pe", i - 1))
                v.tensor_tensor(p0n[:, :, :], p0[:, :, :], inv0[:, :].unsqueeze(2).to_broadcast((P, TILES, POOLED)),
                                ALU.mult).then_inc(s["p0n_rd"], 1)

            def x1_out(i, p):
                dve.wait_ge(s["o0_pe"], count("o0_pe", i))
                dve.wait_ge(s["x0T_rd"], count("x0T_rd", i))
                dve.wait_ge(s["x2_rd"], count("x2_rd", i - 2))
                v.scalar_tensor_tensor(out=x1T[p][:, :], in0=o0_ps[:, 0:TOK], scalar=bo0_s[:, :], in1=x0T[:, :],
                                       op0=ALU.add, op1=ALU.add).then_inc(s["x1_rd"], 1)

            def channel_statistics(i, layer, x):
                dve.wait_ge(s[f"x{layer}_rd"], count(f"x{layer}_rd", i))
                dve.wait_ge(s[f"mv{layer}_rd"], count(f"mv{layer}_rd", i - 1))
                v.bn_stats(bn[layer - 1][:, :], x[:, :]).then_inc(s[f"bn{layer}_rd"], 1)

            def channel_mean(i, layer):
                values = count(f"bn{layer}_rd", i), count(f"gn{layer}_pe", i - 1)
                stand_apart(dve, *values)
                dve.wait_ge(s[f"bn{layer}_rd"], values[0])
                dve.wait_ge(s[f"gn{layer}_pe"], values[1])
                v.bn_aggr(mv[layer - 1][:, :], bn[layer - 1][:, :]).then_inc(s[f"mv{layer}_rd"], 1)

            def mean_square(i, layer):
                dve.wait_ge(s[f"mv{layer}_rd"], count(f"mv{layer}_rd", i))
                m = mv[layer - 1]
                v.scalar_tensor_tensor(out=m[:, 1:2], in0=m[:, 0:1], scalar=m[:, 0:1], in1=m[:, 1:2],
                                       op0=ALU.mult, op1=ALU.add).then_inc(s[f"st{layer}_rd"], 1)

            def group_statistics(i, layer):
                dve.wait_ge(s[f"gn{layer}_pe"], count(f"gn{layer}_pe", i))
                dve.wait_ge(s[f"gsh{layer}_rd"], count(f"gsh{layer}_rd", i - 1))
                v.tensor_copy(gst[layer - 1][:, :], (gm1_ps, gm2_ps)[layer - 1][:, 0:2]).then_inc(s[f"gst{layer}_rd"], 1)

            def group_variance(i, layer):
                g = gst[layer - 1]
                dve.wait_ge(s[f"gst{layer}_rd"], count(f"gst{layer}_rd", i))
                dve.wait_ge(s[f"vare{layer}_rd"], count(f"vare{layer}_rd", i - 1))
                v.scalar_tensor_tensor(out=var[layer - 1][:, :], in0=g[:, 0:1], scalar=g[:, 0:1], in1=g[:, 1:2],
                                       op0=ALU.mult, op1=ALU.subtract, reverse1=True).then_inc(s[f"var{layer}_rd"], 1)

            def variance_guarded(i, layer):
                dve.wait_ge(s[f"var{layer}_rd"], count(f"var{layer}_rd", i))
                dve.wait_ge(s[f"rstd{layer}_rd"], count(f"rstd{layer}_rd", i - 1))
                v.tensor_scalar(vare[layer - 1][:, :], var[layer - 1][:, :], 0.0, (EPS1, EPS2)[layer - 1],
                                ALU.max, ALU.add).then_inc(s[f"vare{layer}_rd"], 1)

            def group_scale(i, layer):
                dve.wait_ge(s[f"rstd{layer}_rd"], count(f"rstd{layer}_rd", i))
                dve.wait_ge(s[f"xn{layer}_rd"], count(f"xn{layer}_rd", i - 1))
                v.tensor_scalar(gsc[layer - 1][:, :], rstd[layer - 1][:, :],
                                col(("L1_conv_gn_gamma", "L2_conv_gn_scale")[layer - 1]), None, ALU.mult
                                ).then_inc(s[f"gsc{layer}_rd"], 1)

            def group_shift(i, layer):
                dve.wait_ge(s[f"gsc{layer}_rd"], count(f"gsc{layer}_rd", i))
                dve.wait_ge(s[f"xn{layer}_rd"], count(f"xn{layer}_rd", i - 1))
                v.scalar_tensor_tensor(out=gsh[layer - 1][:, :], in0=gst[layer - 1][:, 0:1], scalar=gsc[layer - 1][:, :],
                                       in1=col(("L1_conv_gn_beta", "L2_conv_gn_bias")[layer - 1]),
                                       op0=ALU.mult, op1=ALU.subtract, reverse1=True).then_inc(s[f"gsh{layer}_rd"], 1)

            def normalised(i, layer, x, xn):
                dve.wait_ge(s[f"gsh{layer}_rd"], count(f"gsh{layer}_rd", i))
                if layer == 1:
                    dve.wait_ge(s["qk1_pe"], count("qk1_pe", i - 1))
                    dve.wait_ge(s["v1_pe"], count("v1_pe", i - 1))
                else:
                    dve.wait_ge(s["qk2_pe"], count("qk2_pe", i - 1))
                    dve.wait_ge(s["xv2_pe"], count("xv2_pe", i - 1))
                v.tensor_scalar(xn[:, :], x[:, :], gsc[layer - 1][:, :], gsh[layer - 1][:, :], ALU.mult, ALU.add
                                ).then_inc(s[f"xn{layer}_rd"], 1)

            def nmax1_out(i):
                dve.wait_ge(s["s1_pe"], count("s1_pe", i))
                dve.wait_ge(s["exp1_rd"], count("exp1_rd", i - 1))
                v.tensor_reduce(nmax1[:, :], s1_ps[:, :].rearrange("p (u m) -> p u m", u=TILES), AX.X, ALU.max,
                                negate=True).then_inc(s["nmax1_rd"], 1)

            def inv1_out(i):
                dve.wait_ge(s["exp1_rd"], count("exp1_rd", i))
                dve.wait_ge(s["p1n_rd"], count("p1n_rd", i - 1))
                v.reciprocal(inv1[:, :], sum1[:, :]).then_inc(s["inv1_rd"], 1)

            def normalise_p1(i):
                dve.wait_ge(s["inv1_rd"], count("inv1_rd", i))
                dve.wait_ge(s["p1T_pe"], count("p1T_pe", i - 1))
                for u in range(TILES):
                    last = v.tensor_scalar(p1n[:, u, :], p1[:, u, :], inv1[:, u:u + 1], None, ALU.mult)
                last.then_inc(s["p1n_rd"], 1)

            def x2_out(i, p):
                dve.wait_ge(s["o1_pe"], count("o1_pe", i))
                dve.wait_ge(s["x2b_rd"], count("x2b_rd", i - 1))
                dve.wait_ge(s["xn2_rd"], count("xn2_rd", i - 1))
                v.scalar_tensor_tensor(out=x2T[:, :], in0=o1_ps[:, 0:TOK], scalar=bo1_f[:, :], in1=x1T[p][:, :],
                                       op0=ALU.add, op1=ALU.add).then_inc(s["x2_rd"], 1)

            def rest_out(i):
                dve.wait_ge(s["part0_rd"], count("part0_rd", i))
                dve.wait_ge(s["part2_rd"], count("part2_rd", i - 1))
                v.tensor_tensor(rest[:, :, :], qk2_ps[:, :].rearrange("p (w t) -> p w t", w=2), parts[:, :, 0, :],
                                ALU.subtract).then_inc(s["rest_rd"], 1)

            def part1(i):
                dve.wait_ge(s["rest_rd"], count("rest_rd", i))
                v.tensor_copy(parts[:, :, 1, :], rest[:, :, :]).then_inc(s["part1_rd"], 1)

            def nmax_out(i, h):
                dve.wait_ge(s["smax_pe"], count("smax_pe", i, HEADS, h + 1))
                if h == 0:
                    dve.wait_ge(s["npart_rd"], count("npart_rd", i - 1))
                v.tensor_reduce(nmax[:, :, h], smax_ps[h][:, :].rearrange("p (u m) -> p u m", u=TILES),
                                AX.X, ALU.max, negate=True).then_inc(s["nmax_rd"], 1)

            def split_maxima(i):
                dve.wait_ge(s["nmax_rd"], count("nmax_rd", i, HEADS))
                dve.wait_ge(s["nmT_pe"], count("nmT_pe", i - 1))
                v.tensor_copy(npart[:, :, 0, :], nmax[:, :, :]).then_inc(s["nb0_rd"], 1)
                dve.wait_ge(s["nb0_rd"], count("nb0_rd", i))
                v.tensor_tensor(nrest[:, :, :], nmax[:, :, :], npart[:, :, 0, :], ALU.subtract).then_inc(s["nr0_rd"], 1)
                dve.wait_ge(s["nr0_rd"], count("nr0_rd", i))
                v.tensor_copy(npart[:, :, 1, :], nrest[:, :, :]).then_inc(s["nb1_rd"], 1)
                dve.wait_ge(s["nb1_rd"], count("nb1_rd", i))
                v.tensor_tensor(npart[:, :, 2, :], nrest[:, :, :], npart[:, :, 1, :], ALU.subtract
                                ).then_inc(s["npart_rd"], 1)

            def oinv_out(i):
                dve.wait_ge(s["oTT_pe"], count("oTT_pe", i))
                dve.wait_ge(s["on_rd"], count("on_rd", i - 1))
                v.reciprocal(oinv[:, :, :], oTT_ps[:, :].rearrange("p (u h d) -> p u h d", u=TILES, h=HEADS)[:, :, :, HD]
                             ).then_inc(s["oinv_rd"], 1)

            def normalise_o(i):
                dve.wait_ge(s["oinv_rd"], count("oinv_rd", i))
                dve.wait_ge(s["onT_pe"], count("onT_pe", i - 1))
                v.tensor_tensor(on[:, :, :, :],
                                oTT_ps[:, :].rearrange("p (u h d) -> p u h d", u=TILES, h=HEADS)[:, :, :, 0:HD],
                                oinv[:, :, :].unsqueeze(3).to_broadcast((P, TILES, HEADS, HD)), ALU.mult
                                ).then_inc(s["on_rd"], 1)

            def x3_out(i, p):
                dve.wait_ge(s["o2_pe"], count("o2_pe", i))
                dve.wait_ge(s["xv_rd"], count("xv_rd", i))
                dve.wait_ge(s["z_pe"], count("z_pe", i - 1))
                dve.wait_ge(s["out_rd"], count("out_rd", i - 1))
                v.tensor_tensor(x3[:, :], o2_ps[:, 0:TOK], x2tok[p][:, :], ALU.add).then_inc(s["x3_rd"], 1)

            def wrap_z(i):
                dve.wait_ge(s["z_rd"], count("z_rd", i))
                v.tensor_copy(zE[:, H, :], zE[:, 0, :]).then_inc(s["zE_rd"], 1)

            def y_out(i):
                dve.wait_ge(s["yhigh_rd"], count("yhigh_rd", i))
                dve.wait_ge(s["v3_pe"], count("v3_pe", i - 1))
                v.scalar_tensor_tensor(out=yneg[:, :], in0=y_ps[:, 0:TOK], scalar=c_high[:, :], in1=yhigh[:, :],
                                       op0=ALU.add, op1=ALU.min).then_inc(s["y_rd"], 1)

            def x_out(i):
                dve.wait_ge(s["out_pe"], count("out_pe", i))
                dve.wait_ge(s["out_st"], count("out_st", i - 1, 16))
                v.tensor_tensor(xout[:, :], out_ps[:, 0:TOK], x3[:, :], ALU.add).then_inc(s["out_rd"], 1)

            def step(n, p, live):
                q = 1 - p
                if 3 in live: nmax_out(n - 3, 2)
                if 1 in live: group_shift(n - 1, 1)
                if 2 in live: variance_guarded(n - 2, 2)
                if 3 in live: nmax_out(n - 3, 3)
                if 1 in live: normalised(n - 1, 1, x1T[q], xn1)
                if first_is(n, 1): setup_layer3_sums()
                if 2 in live: group_scale(n - 2, 2)
                if 3 in live: nmax_out(n - 3, 4)
                if 2 in live: group_shift(n - 2, 2)
                if 3 in live: nmax_out(n - 3, 5)
                if 2 in live: normalised(n - 2, 2, x2T, xn2)
                if 4 in live: oinv_out(n - 4)
                if 4 in live: normalise_o(n - 4)
                if 0 in live: pool_out(n)
                if 3 in live: nmax_out(n - 3, 6)
                if 0 in live: pg_out(n)
                if 3 in live: nmax_out(n - 3, 7)
                if 3 in live: split_maxima(n - 3)
                if 0 in live: nmax0_out(n)
                if first_is(n, 0): setup_halves()
                if 4 in live: x3_out(n - 4, p)
                if 2 in live: rest_out(n - 2)
                if 1 in live: nmax1_out(n - 1)
                if 0 in live: inv0_out(n)
                if 4 in live: wrap_z(n - 4)
                if 0 in live: normalise_p0(n)
                if first_is(n, 0): setup_values1()
                if 2 in live: part1(n - 2)
                if 1 in live: inv1_out(n - 1)
                if 1 in live: normalise_p1(n - 1)
                if 0 in live: x1_out(n, p)
                if 0 in live: channel_statistics(n, 1, x1T[p])
                if 0 in live: channel_mean(n, 1)
                if 0 in live: mean_square(n, 1)
                if 4 in live: y_out(n - 4)
                if 1 in live: x2_out(n - 1, q)
                if 0 in live: group_statistics(n, 1)
                if 1 in live: channel_statistics(n - 1, 2, x2T)
                if 0 in live: group_variance(n, 1)
                if 1 in live: channel_mean(n - 1, 2)
                if 0 in live: variance_guarded(n, 1)
                if first_is(n, 0): setup_scales()
                if 1 in live: mean_square(n - 1, 2)
                if 2 in live: nmax_out(n - 2, 0)
                if 4 in live: x_out(n - 4)
                if 0 in live: group_scale(n, 1)
                if 1 in live: group_statistics(n - 1, 2)
                if 2 in live: nmax_out(n - 2, 1)
                if 1 in live: group_variance(n - 1, 2)
                if first_is(n, 0): setup_layer3()

            steps(dve, step)


def kernel(**inputs):
    import concourse.bacc as bacc
    from concourse.bass_utils import run_bass_kernel_spmd

    nc = bacc.Bacc("TRN2", target_bir_lowering=False, num_devices=1)
    inputs = {name: np.ascontiguousarray(a) for name, a in inputs.items()}
    arrays = {"in_x": inputs["x"], "in_weights": table(inputs)}
    x, weights = (nc.dram_tensor(name, a.shape, F32, kind="ExternalInput").ap() for name, a in arrays.items())
    out = nc.dram_tensor("out", (IMAGES, H, W, C), F32, kind="ExternalOutput").ap()
    build(nc, x, weights, out)
    got = run_bass_kernel_spmd(nc, [arrays], core_ids=[0])
    return got.results[0]["out"]
```
